# Optimizing a Trainium2 kernel written in Bass

```python
import numpy as np
import jax
import jax.numpy as jnp

def _softmax(x, axis=-1):
    return jax.nn.softmax(x, axis=axis)

def _gelu(x):
    return jax.nn.gelu(x, approximate=True)

def _silu(x):
    return jax.nn.silu(x)

def _sigmoid(x):
    return jax.nn.sigmoid(x)

def _layernorm(x, axis=-1, eps=1e-05):
    m = jnp.mean(x, axis=axis, keepdims=True)
    v = jnp.var(x, axis=axis, keepdims=True)
    return (x - m) / jnp.sqrt(v + eps)

def _scatter_add(tgt, idx, src, axis=0):
    return tgt.at[idx].add(src)

def _segment_sum(src, seg, n):
    return jax.ops.segment_sum(src, seg, n)
kernel_name = 'mk_gnn_ffn_d2_gnn_r8_707b2c'

def setup_inputs(seed: int=0):
    np.random.seed(seed)
    _w = jnp.asarray

    def _rec_inputs():
        import jax
        import jax.numpy as jnp
        _gk = jax.random.key(seed)
        x = -0.0003713 + 1 * jax.random.normal(jax.random.fold_in(_gk, 1), (6250, 256), jnp.float32)
        _s = jax.random.randint(jax.random.fold_in(_gk, 2), (100000,), 0, 6250, jnp.int32)
        _d = jax.random.randint(jax.random.fold_in(_gk, 3), (100000,), 0, 6250, jnp.int32)
        _loop = jnp.arange(6250, dtype=jnp.int32)
        src = jnp.concatenate([_s, _d, _loop])
        dst = jnp.concatenate([_d, _s, _loop])
        _o = jnp.argsort(dst, stable=True)
        src = src[_o]
        dst = dst[_o]
        edge_weight = jax.random.uniform(jax.random.fold_in(_gk, 13), (206250,), jnp.float32, 0.0, 0.03125)
        return (x, src, dst, edge_weight)
    x, src, dst, edge_weight = _rec_inputs()

    def _L0_gnn_setup():
        import jax, jax.numpy as jnp
        import numpy as np
        N_NODES = 6250
        N_EDGES = 100000
        IN_DIM = 256
        OUT_DIM = 64
        HEADS = 4
        NEG_SLOPE = 0.2
        key = jax.random.key(seed)
        k1, k2, k3, k4, k5, k6 = jax.random.split(key, 6)
        x = jax.random.normal(k1, (N_NODES, IN_DIM), dtype=jnp.float32)
        edge_index = jax.random.randint(k2, (2, N_EDGES), 0, N_NODES, dtype=jnp.int64)
        scale = 1.0 / np.sqrt(IN_DIM)
        W = jax.random.normal(k3, (IN_DIM, HEADS * OUT_DIM), dtype=jnp.float32) * scale
        att_src = jax.random.normal(k4, (HEADS, OUT_DIM), dtype=jnp.float32) * scale
        att_dst = jax.random.normal(k5, (HEADS, OUT_DIM), dtype=jnp.float32) * scale
        bias = jnp.zeros((HEADS * OUT_DIM,), dtype=jnp.float32)
        return {'x': x, 'edge_index': edge_index, 'W': W, 'att_src': att_src, 'att_dst': att_dst, 'bias': bias}
    _L0_gnn_all = _L0_gnn_setup()
    _L0_gnn_in = {k: v for k, v in _L0_gnn_all.items() if k in ('W', 'att_src', 'att_dst', 'bias')}
    del _L0_gnn_all

    def _L0_ffn_setup():
        import jax, jax.numpy as jnp
        import numpy as np
        TOP_K = 2
        LN_EPS = 1e-05
        key = jax.random.key(seed)
        ks = jax.random.split(key, 8)
        B, S, D, E, H = (16, 1024, 256, 8, 1024)
        x = jax.random.normal(ks[0], (B, S, D), dtype=jnp.float32)
        Wr = jax.random.normal(ks[1], (D, E), dtype=jnp.float32) * 0.1
        br = jnp.zeros((E,), dtype=jnp.float32)
        ln_g = jnp.ones((E, D), dtype=jnp.float32)
        ln_b = jnp.zeros((E, D), dtype=jnp.float32)
        W1 = jax.random.normal(ks[2], (E, D, H), dtype=jnp.float32) * (1.0 / np.sqrt(D))
        b1 = jnp.zeros((E, H), dtype=jnp.float32)
        W2 = jax.random.normal(ks[3], (E, H, D), dtype=jnp.float32) * (1.0 / np.sqrt(H))
        b2 = jnp.zeros((E, D), dtype=jnp.float32)
        return {'x': x, 'Wr': Wr, 'br': br, 'ln_g': ln_g, 'ln_b': ln_b, 'W1': W1, 'b1': b1, 'W2': W2, 'b2': b2}
    _L0_ffn_all = _L0_ffn_setup()
    _L0_ffn_in = {k: v for k, v in _L0_ffn_all.items() if k in ('Wr', 'br', 'ln_g', 'ln_b', 'W1', 'b1', 'W2', 'b2')}
    del _L0_ffn_all

    def _L1_gnn_setup():
        import jax, jax.numpy as jnp
        import numpy as np
        N_NODES = 12500
        N_EDGES = 400000
        DIM = 256
        LEAKY_SLOPE = 0.2
        EPS = 1e-12
        key = jax.random.key(seed)
        ks = jax.random.split(key, 8)
        embeddings = jax.random.normal(ks[0], (N_NODES, DIM), dtype=jnp.float32)
        edge_src = jax.random.randint(ks[1], (N_EDGES,), 0, N_NODES, dtype=jnp.int32)
        edge_dst = jax.random.randint(ks[2], (N_EDGES,), 0, N_NODES, dtype=jnp.int32)
        edge_val = jax.random.uniform(ks[3], (N_EDGES,), dtype=jnp.float32) / 32.0
        scale = 1.0 / np.sqrt(DIM)
        W1 = jax.random.normal(ks[4], (DIM, DIM), dtype=jnp.float32) * scale
        b1 = jax.random.normal(ks[5], (DIM,), dtype=jnp.float32) * 0.01
        W2 = jax.random.normal(ks[6], (DIM, DIM), dtype=jnp.float32) * scale
        b2 = jax.random.normal(ks[7], (DIM,), dtype=jnp.float32) * 0.01
        return {'embeddings': embeddings, 'edge_src': edge_src, 'edge_dst': edge_dst, 'edge_val': edge_val, 'W1': W1, 'b1': b1, 'W2': W2, 'b2': b2}
    _L1_gnn_all = _L1_gnn_setup()
    _L1_gnn_in = {k: v for k, v in _L1_gnn_all.items() if k in ('W1', 'b1', 'W2', 'b2')}
    del _L1_gnn_all

    def _L1_ffn_setup():
        import jax, jax.numpy as jnp
        import numpy as np
        B, N, D = (16, 512, 256)
        NUM_EXPERTS, TOP_K, HEADS = (4, 2, 4)
        N_EDGES = 131072
        LN_EPS = 1e-05

        def _layernorm(x, g, b):
            mu = x.mean(-1, keepdims=True)
            var = ((x - mu) ** 2).mean(-1, keepdims=True)
            return (x - mu) * jax.lax.rsqrt(var + LN_EPS) * g + b

        def _forward(x, edge_index, W_gat, att_src, att_dst, b_gat, ln_gamma, ln_beta, W1, b1, W2, b2):
            Bc, Nc, Dc = x.shape
            M = Bc * Nc
            x_flat = x.reshape(M, Dc)
            h = (x_flat @ W_gat).reshape(M, HEADS, NUM_EXPERTS)
            loops = jnp.arange(M, dtype=edge_index.dtype)
            src = jnp.concatenate([edge_index[0], loops])
            dst = jnp.concatenate([edge_index[1], loops])
            a_src = (h * att_src).sum(-1)
            a_dst = (h * att_dst).sum(-1)
            e = jax.nn.leaky_relu(a_src[src] + a_dst[dst], negative_slope=0.2)
            e_max = jax.ops.segment_max(e, dst, num_segments=M)
            ee = jnp.exp(e - e_max[dst])
            denom = jax.ops.segment_sum(ee, dst, num_segments=M)
            alpha = ee / (denom[dst] + 1e-16)
            msg = h[src] * alpha[:, :, None]
            agg = jax.ops.segment_sum(msg, dst, num_segments=M).reshape(M, HEADS * NUM_EXPERTS) + b_gat
            scores = _layernorm(agg, ln_gamma, ln_beta).reshape(M, HEADS, NUM_EXPERTS).mean(1)
            scores = scores.reshape(Bc, Nc, NUM_EXPERTS)
            topk_s, topk_i = jax.lax.top_k(scores, TOP_K)
            w = jax.nn.softmax(topk_s, axis=-1)
            out = jnp.zeros_like(x)
            for ei in range(NUM_EXPERTS):
                g = jnp.where(topk_i == ei, w, 0.0).sum(-1)
                hh = jax.nn.gelu(x @ W1[ei] + b1[ei], approximate=False)
                out = out + g[..., None] * (hh @ W2[ei] + b2[ei])
            return out
        key = jax.random.key(seed)
        ks = jax.random.split(key, 8)
        s = 0.05
        return {'x': jax.random.normal(ks[0], (B, N, D), jnp.float32), 'W_gat': jax.random.normal(ks[1], (D, HEADS * NUM_EXPERTS), jnp.float32) * s, 'att_src': jax.random.normal(ks[2], (HEADS, NUM_EXPERTS), jnp.float32) * s, 'att_dst': jax.random.normal(ks[3], (HEADS, NUM_EXPERTS), jnp.float32) * s, 'b_gat': jnp.zeros((HEADS * NUM_EXPERTS,), jnp.float32), 'ln_gamma': jnp.ones((HEADS * NUM_EXPERTS,), jnp.float32), 'ln_beta': jnp.zeros((HEADS * NUM_EXPERTS,), jnp.float32), 'W1': jax.random.normal(ks[4], (NUM_EXPERTS, D, 2 * D), jnp.float32) * s, 'b1': jnp.zeros((NUM_EXPERTS, 2 * D), jnp.float32), 'W2': jax.random.normal(ks[5], (NUM_EXPERTS, 2 * D, D), jnp.float32) * s, 'b2': jnp.zeros((NUM_EXPERTS, D), jnp.float32), 'edge_index': jax.random.randint(ks[6], (2, N_EDGES), 0, B * N, jnp.int32)}
    _L1_ffn_all = _L1_ffn_setup()
    _L1_ffn_in = {k: v for k, v in _L1_ffn_all.items() if k in ('W_gat', 'att_src', 'att_dst', 'b_gat', 'ln_gamma', 'ln_beta', 'W1', 'b1', 'W2', 'b2', 'edge_index')}
    del _L1_ffn_all
    return {'x': x, 'src': src, 'dst': dst, 'edge_weight': edge_weight, 'L0_gnn_W': _L0_gnn_in['W'], 'L0_gnn_att_src': _L0_gnn_in['att_src'], 'L0_gnn_att_dst': _L0_gnn_in['att_dst'], 'L0_gnn_bias': _L0_gnn_in['bias'], 'L0_ffn_Wr': _L0_ffn_in['Wr'], 'L0_ffn_br': _L0_ffn_in['br'], 'L0_ffn_ln_g': _L0_ffn_in['ln_g'], 'L0_ffn_ln_b': _L0_ffn_in['ln_b'], 'L0_ffn_W1': _L0_ffn_in['W1'], 'L0_ffn_b1': _L0_ffn_in['b1'], 'L0_ffn_W2': _L0_ffn_in['W2'], 'L0_ffn_b2': _L0_ffn_in['b2'], 'L1_gnn_W1': _L1_gnn_in['W1'], 'L1_gnn_b1': _L1_gnn_in['b1'], 'L1_gnn_W2': _L1_gnn_in['W2'], 'L1_gnn_b2': _L1_gnn_in['b2'], 'L1_ffn_W_gat': _L1_ffn_in['W_gat'], 'L1_ffn_att_src': _L1_ffn_in['att_src'], 'L1_ffn_att_dst': _L1_ffn_in['att_dst'], 'L1_ffn_b_gat': _L1_ffn_in['b_gat'], 'L1_ffn_ln_gamma': _L1_ffn_in['ln_gamma'], 'L1_ffn_ln_beta': _L1_ffn_in['ln_beta'], 'L1_ffn_W1': _L1_ffn_in['W1'], 'L1_ffn_b1': _L1_ffn_in['b1'], 'L1_ffn_W2': _L1_ffn_in['W2'], 'L1_ffn_b2': _L1_ffn_in['b2'], 'L1_ffn_edge_index': _L1_ffn_in['edge_index']}

def reference(x, src, dst, edge_weight, L0_gnn_W, L0_gnn_att_src, L0_gnn_att_dst, L0_gnn_bias, L0_ffn_Wr, L0_ffn_br, L0_ffn_ln_g, L0_ffn_ln_b, L0_ffn_W1, L0_ffn_b1, L0_ffn_W2, L0_ffn_b2, L1_gnn_W1, L1_gnn_b1, L1_gnn_W2, L1_gnn_b2, L1_ffn_W_gat, L1_ffn_att_src, L1_ffn_att_dst, L1_ffn_b_gat, L1_ffn_ln_gamma, L1_ffn_ln_beta, L1_ffn_W1, L1_ffn_b1, L1_ffn_W2, L1_ffn_b2, L1_ffn_edge_index):
    import jax
    import jax.numpy as jnp

    def _L0_gnn_ref(x, edge_index, W, att_src, att_dst, bias):
        import jax, jax.numpy as jnp
        import numpy as np
        N_NODES = 6250
        N_EDGES = 100000
        IN_DIM = 256
        OUT_DIM = 64
        HEADS = 4
        NEG_SLOPE = 0.2
        N = x.shape[0]
        H, C = att_src.shape
        loop = jnp.arange(N, dtype=edge_index.dtype)
        src = jnp.concatenate([edge_index[0], loop])
        dst = jnp.concatenate([edge_index[1], loop])
        h = (x @ W).reshape(N, H, C)
        a_src = jnp.einsum('nhc,hc->nh', h, att_src)
        a_dst = jnp.einsum('nhc,hc->nh', h, att_dst)
        e = jax.nn.leaky_relu(a_src[src] + a_dst[dst], negative_slope=NEG_SLOPE)
        m = jax.ops.segment_max(e, dst, num_segments=N)
        p = jnp.exp(e - m[dst])
        denom = jax.ops.segment_sum(p, dst, num_segments=N)
        alpha = p / (denom[dst] + 1e-16)
        out = jax.ops.segment_sum(alpha[:, :, None] * h[src], dst, num_segments=N)
        out = out.reshape(N, H * C) + bias
        return jax.nn.relu(out)

    def _L0_ffn_ref(x, Wr, br, ln_g, ln_b, W1, b1, W2, b2):
        import jax, jax.numpy as jnp
        import numpy as np
        TOP_K = 2
        LN_EPS = 1e-05
        B, S, D = x.shape
        N = B * S
        xt = x.reshape(N, D)
        logits = xt @ Wr + br
        probs = jax.nn.softmax(logits, axis=-1)
        top_p, top_idx = jax.lax.top_k(probs, TOP_K)
        weights = top_p / top_p.sum(axis=-1, keepdims=True)
        mu = xt.mean(axis=-1, keepdims=True)
        var = ((xt - mu) ** 2).mean(axis=-1, keepdims=True)
        xn = (xt - mu) * jax.lax.rsqrt(var + LN_EPS)
        xe = xn[None, :, :] * ln_g[:, None, :] + ln_b[:, None, :]
        h = jax.nn.gelu(jnp.einsum('end,edh->enh', xe, W1) + b1[:, None, :], approximate=False)
        y = jnp.einsum('enh,ehd->end', h, W2) + b2[:, None, :]
        y_tok = jnp.transpose(y, (1, 0, 2))
        sel = jnp.take_along_axis(y_tok, top_idx[:, :, None], axis=1)
        out = (weights[:, :, None] * sel).sum(axis=1)
        return out.reshape(B, S, D)

    def _L1_gnn_ref(embeddings, edge_src, edge_dst, edge_val, W1, b1, W2, b2):
        import jax, jax.numpy as jnp
        import numpy as np
        N_NODES = 12500
        N_EDGES = 400000
        DIM = 256
        LEAKY_SLOPE = 0.2
        EPS = 1e-12
        ego_emb = embeddings @ W1.T + b1
        messages = edge_val[:, None] * embeddings[edge_src]
        neighbor_emb = jax.ops.segment_sum(messages, edge_dst, num_segments=embeddings.shape[0])
        interaction_emb = neighbor_emb * embeddings
        side_emb = (neighbor_emb + interaction_emb) @ W2.T + b2
        out = ego_emb + side_emb
        out = jnp.where(out >= 0, out, LEAKY_SLOPE * out)
        norm = jnp.sqrt(jnp.sum(out * out, axis=1, keepdims=True))
        return out / jnp.maximum(norm, EPS)

    def _L1_ffn_ref(x, W_gat, att_src, att_dst, b_gat, ln_gamma, ln_beta, W1, b1, W2, b2, edge_index):
        import jax, jax.numpy as jnp
        import numpy as np
        B, N, D = (16, 512, 256)
        NUM_EXPERTS, TOP_K, HEADS = (4, 2, 4)
        N_EDGES = 131072
        LN_EPS = 1e-05

        def _layernorm(x, g, b):
            mu = x.mean(-1, keepdims=True)
            var = ((x - mu) ** 2).mean(-1, keepdims=True)
            return (x - mu) * jax.lax.rsqrt(var + LN_EPS) * g + b

        def _forward(x, edge_index, W_gat, att_src, att_dst, b_gat, ln_gamma, ln_beta, W1, b1, W2, b2):
            Bc, Nc, Dc = x.shape
            M = Bc * Nc
            x_flat = x.reshape(M, Dc)
            h = (x_flat @ W_gat).reshape(M, HEADS, NUM_EXPERTS)
            loops = jnp.arange(M, dtype=edge_index.dtype)
            src = jnp.concatenate([edge_index[0], loops])
            dst = jnp.concatenate([edge_index[1], loops])
            a_src = (h * att_src).sum(-1)
            a_dst = (h * att_dst).sum(-1)
            e = jax.nn.leaky_relu(a_src[src] + a_dst[dst], negative_slope=0.2)
            e_max = jax.ops.segment_max(e, dst, num_segments=M)
            ee = jnp.exp(e - e_max[dst])
            denom = jax.ops.segment_sum(ee, dst, num_segments=M)
            alpha = ee / (denom[dst] + 1e-16)
            msg = h[src] * alpha[:, :, None]
            agg = jax.ops.segment_sum(msg, dst, num_segments=M).reshape(M, HEADS * NUM_EXPERTS) + b_gat
            scores = _layernorm(agg, ln_gamma, ln_beta).reshape(M, HEADS, NUM_EXPERTS).mean(1)
            scores = scores.reshape(Bc, Nc, NUM_EXPERTS)
            topk_s, topk_i = jax.lax.top_k(scores, TOP_K)
            w = jax.nn.softmax(topk_s, axis=-1)
            out = jnp.zeros_like(x)
            for ei in range(NUM_EXPERTS):
                g = jnp.where(topk_i == ei, w, 0.0).sum(-1)
                hh = jax.nn.gelu(x @ W1[ei] + b1[ei], approximate=False)
                out = out + g[..., None] * (hh @ W2[ei] + b2[ei])
            return out
        return _forward(x, edge_index, W_gat, att_src, att_dst, b_gat, ln_gamma, ln_beta, W1, b1, W2, b2)
    edge_index = jnp.stack([src, dst])
    x = x + _L0_gnn_ref(_layernorm(x, axis=-1), edge_index, L0_gnn_W, L0_gnn_att_src, L0_gnn_att_dst, L0_gnn_bias)
    x = x + _L0_ffn_ref(_layernorm(x, axis=-1)[None], L0_ffn_Wr, L0_ffn_br, L0_ffn_ln_g, L0_ffn_ln_b, L0_ffn_W1, L0_ffn_b1, L0_ffn_W2, L0_ffn_b2)[0]
    x = x + _L1_gnn_ref(_layernorm(x, axis=-1), src, dst, edge_weight, L1_gnn_W1, L1_gnn_b1, L1_gnn_W2, L1_gnn_b2)
    x = x + _L1_ffn_ref(_layernorm(x, axis=-1)[None], L1_ffn_W_gat, L1_ffn_att_src, L1_ffn_att_dst, L1_ffn_b_gat, L1_ffn_ln_gamma, L1_ffn_ln_beta, L1_ffn_W1, L1_ffn_b1, L1_ffn_W2, L1_ffn_b2, L1_ffn_edge_index)[0]
    return x

_drawn_inputs = setup_inputs


def setup_inputs(seed=0):
    import zlib

    import numpy as np

    out = dict(_drawn_inputs(seed))
    spreads = {'L0_gnn_bias': (0.0, 0.1),
     'L0_ffn_br': (0.0, 0.1),
     'L0_ffn_ln_g': (1.0, 0.2),
     'L0_ffn_ln_b': (0.0, 0.1),
     'L0_ffn_b1': (0.0, 0.1),
     'L0_ffn_b2': (0.0, 0.1),
     'L1_ffn_b_gat': (0.0, 0.1),
     'L1_ffn_ln_gamma': (1.0, 0.2),
     'L1_ffn_ln_beta': (0.0, 0.1),
     'L1_ffn_b1': (0.0, 0.1),
     'L1_ffn_b2': (0.0, 0.1)}
    factors = {'edge_weight': 5.277, 'L1_gnn_b1': 39.875, 'L1_gnn_W2': 2.856, 'L1_gnn_b2': 35.029}
    for name, (base, spread) in spreads.items():
        noise = np.random.default_rng([zlib.crc32(name.encode()), seed]).standard_normal(out[name].shape)
        drawn = base * np.exp(spread * noise) if base else spread * noise
        out[name] = jnp.asarray(drawn.astype(out[name].dtype))
    for name, factor in factors.items():
        out[name] = (out[name] * factor).astype(out[name].dtype)
    return out
```

```python
from contextlib import ExitStack

import concourse.bass as bass
from concourse import mybir

F32 = mybir.dt.float32
I32 = mybir.dt.int32
U32 = mybir.dt.uint32
ALU = mybir.AluOpType
ACT = mybir.ActivationFunctionType
AX = mybir.AxisListType
RMAX = bass.bass_isa.ReduceOp.max

P = 128
N = 6250
D = 256
NB = -(-N // P)
NP = NB * P
LAST = N - (NB - 1) * P
KC = D // P
U7 = 7
HEADS = 4
EPS = 1e-5
SLOPE = 0.2
BIG = 3e38

E_SORTED = 206250
GRP = 8
NTE = -(-E_SORTED // (P * 2 * GRP)) * 2 * GRP
NGRP = NTE // GRP
WIN = P
NACC = NP + WIN
E_FREE = 131072
NTF = E_FREE // P
NGRF = NTF // GRP

TOP = 2


def tiles_of(experts):
    most = (TOP * N + experts * (P - 1)) // P
    return most + 1 - most % 2


NT_MAX = tiles_of(8)
ROWS = NT_MAX * P


class Shared:

    def __init__(self, nc, ctx):
        self.nc, self.ctx = nc, ctx
        self.layer, self.sems = ExitStack(), []

    def lasting_sem(self, name):
        return self.ctx.enter_context(self.nc.semaphore(name))

    def sem(self, name):
        self.sems.append(self.layer.enter_context(self.nc.semaphore(name)))
        return self.sems[-1]

    def end_layer(self):
        with self.nc.Block() as block:
            @block.gpsimd
            def _(pool):
                for sem in self.sems:
                    pool.sem_clear(sem)
        self.layer.close()
        self.layer, self.sems = ExitStack(), []

    def sb(self, name, shape, dt=F32):
        return self.ctx.enter_context(self.nc.sbuf_tensor(name, shape, dt))


class Scope:

    def __init__(self, nc):
        self.nc, self.ctx = nc, ExitStack()

    def __enter__(self):
        self.ctx.__enter__()
        return self

    def __exit__(self, *a):
        return self.ctx.__exit__(*a)

    def sb(self, name, shape, dt=F32):
        return self.ctx.enter_context(self.nc.sbuf_tensor(name, shape, dt))

    def ps(self, name, shape, dt=F32):
        return self.ctx.enter_context(self.nc.psum_tensor(name, shape, dt))

    def block(self):
        return self.ctx.enter_context(self.nc.Block())


def at_least(eng, sem, value):
    if not isinstance(value, int) or value > 0:
        eng.wait_ge(sem, value)


class Chain:

    def __init__(self, eng, sem):
        self.eng, self.sem, self.n = eng, sem, 0

    def __call__(self, ins, sem=None):
        if sem is None:
            self.n += 1
            ins.then_inc(self.sem, 1)
            self.eng.wait_ge(self.sem, self.n)
        else:
            ins.then_inc(sem, 1)
            self.eng.wait_ge(sem, 1)


def bcast_rows(vec, n=P):
    return vec.partition_broadcast(n)


def setup(sh, x, xs_rows):
    nc = sh.nc
    sh.X = sh.sb("X", [P, NB, D])
    sh.ident = sh.sb("ident", [P, P])
    sh.iota = sh.sb("iota", [P, P])
    sh.ones = sh.sb("ones", [P, P])
    sh.tri = sh.sb("tri", [P, P])
    sh.valid = sh.sb("valid", [P, NB])
    s_x, s_cst, sh.rows_zeroed, s_pre = sh.sem("x_loaded"), sh.sem("constants"), sh.lasting_sem("rows_zeroed"), sh.sem("memsets")
    with Scope(nc) as sc:
        zero = sc.sb("zero", [P, 3, D])
        block = sc.block()

        @block.gpsimd
        def _(pool):
            pool.memset(sh.X[:, NB - 1, :], 0.0).then_inc(s_pre, 1)
            pool.memset(zero[:, :, :], 0.0).then_inc(s_pre, 1)
            pool.memset(sh.ident[:, :], 0.0).then_inc(s_pre, 1)
            pool.memset(sh.ones[:, :], 1.0).then_inc(s_pre, 1)
            pool.memset(sh.valid[:, :], 1.0).then_inc(s_pre, 1)
            pool.iota(sh.iota[:, :], [[1, P]], base=0, channel_multiplier=0,
                      allow_small_or_imprecise_dtypes=True).then_inc(s_cst, 1)
            pool.wait_ge(s_pre, 5)
            pool.affine_select(out=sh.ident[:, :], in_=sh.ident[:, :], compare_op=ALU.not_equal, fill=1.0,
                               base=0, pattern=[[-1, P]], channel_multiplier=1).then_inc(s_cst, 1)
            pool.affine_select(out=sh.tri[:, :], in_=sh.ones[:, :], compare_op=ALU.is_gt, fill=0.0,
                               base=0, pattern=[[1, P]], channel_multiplier=-1).then_inc(s_cst, 1)
            pool.affine_select(out=sh.valid[:, :], in_=sh.valid[:, :], compare_op=ALU.is_ge, fill=0.0,
                               base=N - 1, pattern=[[-P, NB]], channel_multiplier=-1).then_inc(s_cst, 1)

        @block.sync
        def _(sp):
            full = x[0:(NB - 1) * P, :].rearrange("(i p) d -> p i d", p=P)
            for c in range(6):
                sp.dma_start(sh.X[:, 8 * c:8 * c + 8, :], full[:, 8 * c:8 * c + 8, :]).then_inc(s_x, 16)
            sp.wait_ge(s_pre, 1)
            sp.dma_start(sh.X[0:LAST, NB - 1, :], x[(NB - 1) * P:N, :]).then_inc(s_x, 16)
            sp.wait_ge(s_pre, 2)
            rows = xs_rows[0:ROWS, :].rearrange("(a p) d -> p a d", p=P)
            for a in range(NT_MAX // 3):
                sp.dma_start(rows[:, 3 * a:3 * a + 3, :], zero[:, :, :]).then_inc(sh.rows_zeroed, 16)
            sp.wait_ge(s_x, 7 * 16)
            sp.wait_ge(sh.rows_zeroed, NT_MAX // 3 * 16)


def layer_norm_stats(sh, tag, mean_rstd):
    nc = sh.nc
    s_st, s_ag, s_sq, s_ve, s_r = (sh.sem(f"{tag}_{n}") for n in ("bn_stats", "bn_aggr", "sqrt", "eps", "rstd"))
    with Scope(nc) as sc:
        st = sc.sb(f"{tag}_st", [P, 8, 6])
        block = sc.block()

        @block.vector
        def _(v):
            for i in range(NB):
                if i >= 8:
                    v.wait_ge(s_ag, i - 7)
                v.bn_stats(st[:, i % 8, :], sh.X[:, i, :]).then_inc(s_st, 1)
                if i >= 4:
                    v.wait_ge(s_st, i - 3)
                    v.bn_aggr(mean_rstd[:, i - 4, :], st[:, (i - 4) % 8, :]).then_inc(s_ag, 1)
            for i in range(NB - 4, NB):
                v.wait_ge(s_st, i + 1)
                v.bn_aggr(mean_rstd[:, i, :], st[:, i % 8, :]).then_inc(s_ag, 1)
            v.wait_ge(s_ag, NB)
            v.tensor_scalar(mean_rstd[:, :, 1], mean_rstd[:, :, 1], EPS, None, ALU.add).then_inc(s_ve, 1)
            v.wait_ge(s_sq, 1)
            v.reciprocal(mean_rstd[:, :, 1], mean_rstd[:, :, 1]).then_inc(s_r, 1)
            v.wait_ge(s_r, 1)

        @block.scalar
        def _(a):
            a.wait_ge(s_ve, 1)
            a.activation(mean_rstd[:, :, 1], mean_rstd[:, :, 1], ACT.Sqrt).then_inc(s_sq, 1)


def project_nodes(sh, tag, stats, weight, ncols, att=None, table=None, table_cols=0, keep=None, keep_from=0,
                  stats2=None):
    nc = sh.nc
    wc = weight.shape[1]
    per = wc // HEADS
    s = {n: sh.sem(f"{tag}_{n}") for n in ("w", "att", "fold", "xn", "xrfree", "tr", "xt", "mm", "ev", "kept", "st", "st_seen", "ag", "agc")}
    s_tab = [sh.sem(f"{tag}_tab{u}") for u in range(U7)] if table is not None else None
    with Scope(nc) as sc:
        W = sc.sb(f"{tag}_W", [P, KC, ncols])
        XR = sc.sb(f"{tag}_XR", [P, U7, D])
        XT = sc.sb(f"{tag}_XT", [P, 2, KC, P])
        OUT = sc.sb(f"{tag}_OUT", [P, U7, table_cols]) if table is not None else None
        ATT = sc.sb(f"{tag}_ATT", [P, 2, wc]) if att else None
        FT = sc.sb(f"{tag}_FT", [P, KC, 2, wc]) if att else None
        ST = sc.sb(f"{tag}_ST", [P, U7, 6]) if stats2 is not None else None
        AG = sc.sb(f"{tag}_AG", [P, U7, 2]) if stats2 is not None else None
        pT = [sc.ps(f"{tag}_pT{j}", [P, KC, P]) for j in range(2)]
        pO = [sc.ps(f"{tag}_pO{j}", [P, ncols]) for j in range(4)]
        block = sc.block()

        @block.sync
        def _(sp):
            sp.dma_start(W[:, :, 0:wc], weight.rearrange("(c k) n -> k c n", k=P)).then_inc(s["w"], 16)
            if att:
                for a in range(2):
                    sp.dma_start(ATT[:, a, :], bcast_rows(att[a].rearrange("h c -> (h c)"))).then_inc(s["att"], 16)
            if table is not None:
                with sp.Fori(0, NB // U7) as it:
                    for u in range(U7):
                        sp.wait_ge(s["ev"], it * U7 + u + 1)
                        sp.dma_start(table[bass.ds((it * U7 + u) * P, P), :], OUT[:, u, :]).then_inc(s_tab[u], 16)
                for u in range(U7):
                    sp.wait_ge(s_tab[u], 16 * (NB // U7))

        @block.vector
        def _(v):
            v.wait_ge(s["w"], 16)
            if att:
                v.wait_ge(s["att"], 32)
                for c in range(KC):
                    for a in range(2):
                        v.tensor_tensor(FT[:, c, a, :], W[:, c, 0:wc], ATT[:, a, :], ALU.mult).then_inc(s["fold"], 1)
                v.wait_ge(s["fold"], 2 * KC)
                for c in range(KC):
                    for a in range(2):
                        v.tensor_reduce(W[:, c, wc + a * HEADS:wc + (a + 1) * HEADS],
                                        FT[:, c, a, :].rearrange("p (h q) -> p h q", q=per),
                                        AX.X, ALU.add).then_inc(s["fold"], 1)
            with v.Fori(0, NB // U7) as it:
                for u in range(U7):
                    i = it * U7 + u
                    v.wait_ge(s["tr"], 0 + it * U7)
                    v.tensor_scalar(XR[:, u, :], sh.X[:, bass.ds(i, 1), :].rearrange("p a d -> p (a d)"),
                                    stats[:, bass.ds(i, 1), 0:1].rearrange("p a b -> p (a b)"),
                                    stats[:, bass.ds(i, 1), 1:2].rearrange("p a b -> p (a b)"),
                                    ALU.subtract, ALU.mult).then_inc(s["xn"], 1)
                if stats2 is not None:
                    v.wait_ge(s["agc"], it)
                    for u in range(U7):
                        v.wait_ge(s["xn"], it * U7 + u + 1)
                        v.bn_stats(ST[:, u, :], XR[:, u, :]).then_inc(s["st"], 1)
                    v.wait_ge(s["st"], (it + 1) * U7)
                    v.sem_inc(s["st_seen"], 1)
                    for u in range(U7):
                        v.bn_aggr(AG[:, u, :], ST[:, u, :]).then_inc(s["ag"], 1)
                    v.wait_ge(s["ag"], (it + 1) * U7)
                    v.tensor_copy(stats2[:, bass.ds(it * U7, U7), :], AG[:, :, :]).then_inc(s["agc"], 1)
                for u in range(U7):
                    i = it * U7 + u
                    v.wait_ge(s["mm"], i + 1)
                    if table is not None:
                        v.wait_ge(s_tab[u], it * 16)
                        v.tensor_copy(OUT[:, u, :], pO[u % 4][:, 0:table_cols]).then_inc(s["ev"], 1)
                    if keep is not None:
                        v.tensor_copy(keep[:, bass.ds(i, 1), :].rearrange("p a b -> p (a b)"),
                                      pO[u % 4][:, keep_from:ncols]).then_inc(s["kept"], 1)

        @block.scalar
        def _(a):
            with a.Fori(0, NB // U7) as it:
                for u in range(U7):
                    i = it * U7 + u
                    a.wait_ge(s["tr"], i + 1)
                    if u >= 2:
                        a.wait_ge(s["mm"], i - 1)
                    else:
                        a.wait_ge(s["mm"], it * U7)
                    a.activation(XT[:, u % 2, :, :], pT[u % 2][:, :, :], ACT.Copy).then_inc(s["xt"], 1)

        @block.tensor
        def _(pe):
            def turn(it, u):
                pe.wait_ge(s["xn"], it * U7 + u + 1)
                if u >= 2:
                    pe.wait_ge(s["xt"], it * U7 + u - 1)
                else:
                    pe.wait_ge(s["xt"], it * U7)
                for c in range(KC):
                    m = pe.transpose(pT[u % 2][:, c, :], XR[:, u, c * P:(c + 1) * P], sh.ident[:, :])
                m.then_inc(s["tr"], 1)

            def product(it, u):
                i = it * U7 + u
                pe.wait_ge(s["xt"], i + 1)
                for done, used in (("ev", table), ("kept", keep)):
                    if used is not None:
                        pe.wait_ge(s[done], i - 3 if u >= 4 else it * U7)
                for c in range(KC):
                    m = pe.matmul(pO[u % 4][:, :], XT[:, u % 2, c, :], W[:, c, :], start=(c == 0), stop=(c == KC - 1))
                m.then_inc(s["mm"], 1)

            pe.wait_ge(s["fold"] if att else s["w"], 4 * KC if att else 16)
            with pe.Fori(0, NB // U7) as it:
                turn(it, 0)
                for u in range(U7):
                    if u + 1 < U7:
                        turn(it, u + 1)
                    product(it, u)


def load_registers(eng, regs, row, at):
    eng.reg_load(regs, row[0:1, bass.ds(at, len(regs))])
    return [eng.snap(r, min_val=0, max_val=N) for r in regs]


def graph_pass(sh, tag, src_t, dst_t, table, width, acc, gather_done, rounds0, adst=None, gmax=None, weight_t=None):
    nc = sh.nc
    attend = adst is not None
    nch = 3 if attend else 2
    RING = 2 * GRP
    HG = GRP // 2
    RND = NGRP // 2
    names = ["loaded", "drel", "staged", "slot_free", "onehot", "sum", "added", "zeroed"]
    if attend:
        names += ["T", "Tcopied", "ad", "z", "lr", "arg", "p", "gp", "aw0", "aw1", "ps_zeroed"]
    s = {n: sh.sem(f"{tag}_{n}") for n in names}
    n_loads = (3 if attend else 4) * 16
    with Scope(nc) as sc:
        IDX = sc.sb(f"{tag}_IDX", [P, NTE], I32)
        DST = sc.sb(f"{tag}_DST", [P, NTE], I32)
        DREL = sc.sb(f"{tag}_DREL", [P, NTE])
        FIRST = sc.sb(f"{tag}_FIRST", [P, NTE], I32)
        WT = sc.sb(f"{tag}_WT", [P, NTE]) if not attend else None
        STG = sc.sb(f"{tag}_STG", [P, 2, GRP], I32)
        G = sc.sb(f"{tag}_G", [P, RING, width])
        S = sc.sb(f"{tag}_S", [P, 2, GRP, WIN])
        pM = [sc.ps(f"{tag}_pM{j}", [P, 512]) for j in range(4)]
        if attend:
            ST = sc.sb(f"{tag}_ST", [P, GRP, P])
            AW = sc.sb(f"{tag}_AW", [P, 2, GRP, HEADS])
            Z = sc.sb(f"{tag}_Z", [P, 2, 2, GRP, HEADS])
            L = sc.sb(f"{tag}_L", [P, 2, 2, GRP, HEADS])
            ARG = sc.sb(f"{tag}_ARG", [P, 2, GRP, HEADS])
            PR = sc.sb(f"{tag}_PR", [P, 2, GRP, HEADS])
            pT = sc.ps(f"{tag}_pT", [P, GRP, P])
            pA = sc.ps(f"{tag}_pA", [P, 2, GRP, HEADS])
        block = sc.block()

        def M(u):
            return pM[u % 4][:, 0:nch * WIN].rearrange("p (c w) -> p c w", c=nch)

        def over_groups(eng, step):
            step(0, 0)
            with eng.Fori(0, RND - 1) as it:
                step(it, 1)
                step(it + 1, 0)
            step(RND - 1, 1)

        @block.sync
        def _(sp):
            sp.dma_start(IDX[:, :], src_t).then_inc(s["loaded"], 16)
            sp.dma_start(DST[:, :], dst_t).then_inc(s["loaded"], 16)
            sp.dma_start(FIRST[:, :], bcast_rows(dst_t[0, :])).then_inc(s["loaded"], 16)
            if not attend:
                sp.dma_start(WT[:, :], weight_t).then_inc(s["loaded"], 16)
                return
            sp.wait_ge(s["loaded"], n_loads)
            regs = [sp.alloc_register(f"{tag}_sp{u}") for u in range(GRP)]

            def windows(rnd, par):
                k = rnd * 2 + par
                first = load_registers(sp, regs, FIRST, k * GRP)
                at_least(sp, s["ad"], k - 1)
                for u in range(GRP):
                    sp.dma_start(AW[:, par, u, :], adst[bass.ds(first[u], WIN), :]).then_inc(s[f"aw{par}"], 16)

            over_groups(sp, windows)

        @block.gpsimd
        def _(pool):
            for c in range(nch):
                pool.memset(acc[:, c, :], 0.0).then_inc(s["zeroed"], 1)
            pool.wait_ge(s["zeroed"], nch)
            pool.wait_ge(s["loaded"], n_loads)

            def gathers(rnd, par):
                k = rnd * 2 + par
                for u in range(GRP):
                    at_least(pool, gather_done[par * GRP + u], (rnd + rounds0) * 16)
                pool.tensor_copy(STG[:, par, :], IDX[:, bass.ds(k * GRP, GRP)]).then_inc(s["staged"], 1)
                pool.wait_ge(s["staged"], k + 1)
                for u in range(GRP):
                    slot = par * GRP + u
                    at_least(pool, s["sum"], rnd * RING + slot - RING + 1)
                    pool.sem_inc(s["slot_free"], 1)
                    pool.indirect_dma_start(G[:, slot, :], None, table, bass.IndirectOffsetOnAxis(
                        ap=STG[:, par, u:u + 1].bitcast(U32), axis=0)).then_inc(gather_done[slot], 16)

            gathers(0, 0)
            gathers(0, 1)
            with pool.Fori(1, RND) as rnd:
                gathers(rnd, 0)
                gathers(rnd, 1)

        @block.vector
        def _(v):
            if attend:
                for j in range(4):
                    v.memset(pM[j][:, 2 * WIN:3 * WIN], 0.0).then_inc(s["ps_zeroed"], 1)
            v.wait_ge(s["loaded"], n_loads)
            v.tensor_tensor(DREL[:, :], DST[:, :], FIRST[:, :], ALU.subtract).then_inc(s["drel"], 1)
            v.wait_ge(s["drel"], 1)
            v.wait_ge(s["zeroed"], nch)
            regs = [v.alloc_register(f"{tag}_v{u}") for u in range(GRP)]

            def onehot(k, par, u):
                rel = DREL[:, bass.ds(k * GRP + u, 1)]
                if attend:
                    v.tensor_scalar(S[:, par, u, :], sh.iota[:, :], rel, None, ALU.is_equal).then_inc(s["onehot"], 1)
                else:
                    v.tensor_scalar(S[:, par, u, :], sh.iota[:, :], rel, WT[:, bass.ds(k * GRP + u, 1)],
                                    ALU.is_equal, ALU.mult).then_inc(s["onehot"], 1)

            def add(k, u, first):
                t = k * GRP + u
                v.wait_ge(s["sum"], t + 1)
                at_least(v, s["added"], t)
                win = acc[:, 0:nch, bass.ds(first, WIN)]
                v.tensor_tensor(win, M(u), win, ALU.add).then_inc(s["added"], 1)

            def factors(rnd, par):
                k = rnd * 2 + par
                slots = slice(par * GRP, par * GRP + GRP)
                v.wait_ge(s["ad"], k + 1)
                for u in range(GRP):
                    v.wait_ge(gather_done[par * GRP + u], (rnd + rounds0 + 1) * 16)
                v.tensor_tensor(Z[:, par, 0], G[:, slots, D:D + HEADS], pA[:, par], ALU.add).then_inc(s["z"], 1)
                v.tensor_tensor(Z[:, par, 1], gmax[:, :].unsqueeze(1).broadcast_to([P, GRP, HEADS]), pA[:, par],
                                ALU.add).then_inc(s["z"], 1)
                v.wait_ge(s["z"], k * 2 + 2)
                v.scalar_tensor_tensor(L[:, par].rearrange("p a u h -> p (a u h)"), Z[:, par].rearrange("p a u h -> p (a u h)"),
                                       SLOPE, Z[:, par].rearrange("p a u h -> p (a u h)"),
                                       ALU.mult, ALU.max).then_inc(s["lr"], 1)
                v.wait_ge(s["lr"], k + 1)
                v.tensor_tensor(ARG[:, par], L[:, par, 0], L[:, par, 1], ALU.subtract).then_inc(s["arg"], 1)
                v.wait_ge(s["p"], k + 1)
                for hf in range(2):
                    rows = G[:, par * GRP + hf * HG:par * GRP + (hf + 1) * HG, 0:D].rearrange(
                        "p u (h q) -> p u h q", h=HEADS)
                    fac = PR[:, par, hf * HG:(hf + 1) * HG, :].unsqueeze(3).broadcast_to([P, HG, HEADS, D // HEADS])
                    v.tensor_tensor(rows, rows, fac, ALU.mult).then_inc(s["gp"], 1)

            def step(rnd, par):
                k = rnd * 2 + par
                before = not (isinstance(k, int) and k == 0)
                if before:
                    first = load_registers(v, regs, FIRST, (k - 1) * GRP)
                for u in range(HG):
                    onehot(k, par, 2 * u)
                    onehot(k, par, 2 * u + 1)
                    if before:
                        add(k - 1, u, first[u])
                if before:
                    for u in range(HG, GRP):
                        add(k - 1, u, first[u])
                if attend:
                    factors(rnd, par)

            over_groups(v, step)
            first = load_registers(v, regs, FIRST, (NGRP - 1) * GRP)
            for u in range(GRP):
                add(NGRP - 1, u, first[u])
            v.wait_ge(s["added"], NTE)

        if attend:
            @block.scalar
            def _(a):
                def step(rnd, par):
                    k = rnd * 2 + par
                    at_least(a, s["ad"], k)
                    for hf in range(2):
                        sl = slice(hf * HG, (hf + 1) * HG)
                        a.wait_ge(s["T"], k * 2 + hf + 1)
                        a.activation(ST[:, sl, :], pT[:, sl, :], ACT.Copy).then_inc(s["Tcopied"], 1)
                    a.wait_ge(s["arg"], k + 1)
                    a.activation(PR[:, par], ARG[:, par], ACT.Exp).then_inc(s["p"], 1)

                over_groups(a, step)

        @block.tensor
        def _(pe):
            def transposes(rnd, par):
                k = rnd * 2 + par
                for hf in range(2):
                    at_least(pe, s["Tcopied"], k * 2 - 1 + hf)
                    pe.wait_ge(s["onehot"], k * GRP + (hf + 1) * HG)
                    for u in range(hf * HG, (hf + 1) * HG):
                        m = pe.transpose(pT[:, u, :], S[:, par, u, :], sh.ident[:, :])
                    m.then_inc(s["T"], 1)

            def spread(rnd, par):
                pe.wait_ge(s["Tcopied"], (rnd * 2 + par) * 2 + 2)
                pe.wait_ge(s[f"aw{par}"], (rnd + 1) * 16 * GRP)
                for u in range(GRP):
                    m = pe.matmul(pA[:, par, u, :], ST[:, u, :], AW[:, par, u, :], start=True, stop=True)
                m.then_inc(s["ad"], 1)

            def sums(rnd, par, hf):
                k = rnd * 2 + par
                if attend:
                    pe.wait_ge(s["ps_zeroed"], 4)
                    pe.wait_ge(s["gp"], k * 2 + hf + 1)
                for u in range(hf * HG, (hf + 1) * HG):
                    slot = par * GRP + u
                    t = k * GRP + u
                    if not attend:
                        pe.wait_ge(gather_done[slot], (rnd + rounds0 + 1) * 16)
                        pe.wait_ge(s["onehot"], t + 1)
                    at_least(pe, s["added"], t - 3)
                    for c in range(2):
                        m = pe.matmul(M(u)[:, c, :], G[:, slot, c * P:(c + 1) * P], S[:, par, u, :],
                                      start=True, stop=True)
                    if attend:
                        m = pe.matmul(M(u)[0:HEADS, 2, :], PR[:, par, u, :], S[:, par, u, :], start=True, stop=True)
                    m.then_inc(s["sum"], 1)

            def step(rnd, par):
                if attend:
                    transposes(rnd, par)
                    if par == 1:
                        sums(rnd, 0, 1)
                    elif not isinstance(rnd, int):
                        sums(rnd - 1, 1, 1)
                    spread(rnd, par)
                    sums(rnd, par, 0)
                else:
                    sums(rnd, par, 0)
                    sums(rnd, par, 1)

            over_groups(pe, step)
            if attend:
                sums(RND - 1, 1, 1)


def table_maximum(sh, tag, keep, col, gmax):
    nc = sh.nc
    s_m, s_g = sh.sem(f"{tag}_max"), sh.sem(f"{tag}_allmax")
    with Scope(nc) as sc:
        M = sc.sb(f"{tag}_M", [P, HEADS])
        block = sc.block()

        @block.vector
        def _(v):
            v.tensor_reduce(M[:, :], keep[:, 0:NB - 1, col:col + HEADS].rearrange("p i h -> p h i"),
                            AX.X, ALU.max).then_inc(s_m, 1)
            v.wait_ge(s_m, 1)
            v.tensor_tensor(M[0:LAST, :], M[0:LAST, :], keep[0:LAST, NB - 1, col:col + HEADS], ALU.max).then_inc(s_m, 1)

        @block.gpsimd
        def _(pool):
            pool.wait_ge(s_m, 2)
            pool.partition_all_reduce(gmax[:, :], M[:, :], P, RMAX).then_inc(s_g, 1)
            pool.wait_ge(s_g, 1)


def store_adst(sh, tag, keep, col, adst):
    nc = sh.nc
    s_z, s_o = sh.sem(f"{tag}_zero"), sh.sem(f"{tag}_stored")
    with Scope(nc) as sc:
        Z = sc.sb(f"{tag}_Z", [P, HEADS])
        block = sc.block()

        @block.vector
        def _(v):
            v.memset(Z[:, :], 0.0).then_inc(s_z, 1)

        @block.sync
        def _(sp):
            sp.dma_start(adst[0:NP, :].rearrange("(i p) h -> p i h", p=P), keep[:, :, col:col + HEADS]).then_inc(s_o, 16)
            sp.wait_ge(s_z, 1)
            sp.dma_start(adst[NP:NP + WIN, :], Z[:, :]).then_inc(s_o, 16)
            sp.wait_ge(s_o, 32)


def self_factor(sh, v, a, s, keep, col, gmax, Z, PS):
    def on_vector():
        av, dv = keep[:, :, col:col + HEADS], keep[:, :, col + HEADS:col + 2 * HEADS]
        v.tensor_tensor(Z[:, 0], av, dv, ALU.add).then_inc(s, 1)
        v.tensor_tensor(Z[:, 1], gmax[:, :].unsqueeze(1).broadcast_to([P, NB, HEADS]), dv, ALU.add).then_inc(s, 1)
        v.wait_ge(s, 2)
        flat = Z[:, :, :, :].rearrange("p a i h -> p (a i h)")
        v.scalar_tensor_tensor(flat, flat, SLOPE, flat, ALU.mult, ALU.max).then_inc(s, 1)
        v.wait_ge(s, 3)
        v.tensor_tensor(PS[:, :, :], Z[:, 0], Z[:, 1], ALU.subtract).then_inc(s, 1)
    def on_scalar():
        a.wait_ge(s, 4)
        a.activation(PS[:, :, :], PS[:, :, :], ACT.Exp).then_inc(s, 1)
    return on_vector, on_scalar


def finish_attention(sh, tag, acc, table, keep, gmax, bias):
    nc = sh.nc
    s = {n: sh.sem(f"{tag}_{n}") for n in ("self", "bias", "copied", "tr", "op")}
    s_h = [sh.sem(f"{tag}_h{u}") for u in range(U7)]
    OPS = 7
    with Scope(nc) as sc:
        Z = sc.sb(f"{tag}_Z", [P, 2, NB, HEADS])
        PS = sc.sb(f"{tag}_PS", [P, NB, HEADS])
        B = sc.sb(f"{tag}_B", [P, D])
        AR = sc.sb(f"{tag}_AR", [P, 2, 3, P])
        H = sc.sb(f"{tag}_H", [P, U7, D])
        T = sc.sb(f"{tag}_T", [P, U7, D])
        DN = sc.sb(f"{tag}_DN", [P, U7, HEADS])
        pN = sc.ps(f"{tag}_pN", [P, U7, 512])
        block = sc.block()

        @block.sync
        def _(sp):
            sp.dma_start(B[:, :], bcast_rows(bias)).then_inc(s["bias"], 16)
            with sp.Fori(0, NB // U7) as it:
                sp.wait_ge(s["op"], it * OPS)
                for u in range(U7):
                    sp.dma_start(H[:, u, :], table[bass.ds((it * U7 + u) * P, P), 0:D]).then_inc(s_h[u], 16)

        @block.scalar
        def _(a):
            self_factor(sh, None, a, s["self"], keep, 0, gmax, Z, PS)[1]()
            with a.Fori(0, NB // U7) as it:
                for u in range(U7):
                    if u >= 2:
                        a.wait_ge(s["tr"], it * U7 + u - 1)
                    else:
                        a.wait_ge(s["tr"], it * U7)
                    a.activation(AR[:, u % 2], acc[:, :, bass.ds((it * U7 + u) * P, P)], ACT.Copy).then_inc(s["copied"], 1)

        @block.tensor
        def _(pe):
            with pe.Fori(0, NB // U7) as it:
                pe.wait_ge(s["op"], it * OPS)
                for u in range(U7):
                    pe.wait_ge(s["copied"], it * U7 + u + 1)
                    for c in range(KC):
                        pe.transpose(pN[:, u, c * P:(c + 1) * P], AR[:, u % 2, c, :], sh.ident[:, :])
                    pe.transpose(pN[:, u, D:D + HEADS], AR[0:HEADS, u % 2, 2, :],
                                 sh.ident[0:HEADS, 0:HEADS]).then_inc(s["tr"], 1)

        @block.vector
        def _(v):
            self_factor(sh, v, None, s["self"], keep, 0, gmax, Z, PS)[0]()
            v.wait_ge(s["self"], 5)
            v.wait_ge(s["bias"], 16)

            def heads(ap):
                return ap.rearrange("p u (h q) -> p u h q", h=HEADS)

            def spread(ap):
                return ap.unsqueeze(3).broadcast_to([P, U7, HEADS, D // HEADS])

            with v.Fori(0, NB // U7) as it:
                blk = bass.ds(it * U7, U7)
                for u in range(U7):
                    v.wait_ge(s_h[u], (it + 1) * 16)
                v.tensor_tensor(heads(T[:, :, :]), heads(H[:, :, :]), spread(PS[:, blk, :]), ALU.mult).then_inc(s["op"], 1)
                v.wait_ge(s["tr"], it * U7 + U7)
                v.tensor_tensor(DN[:, :, :], PS[:, blk, :], pN[:, :, D:D + HEADS], ALU.add).then_inc(s["op"], 1)
                v.wait_ge(s["op"], it * OPS + 2)
                v.tensor_tensor(T[:, :, :], T[:, :, :], pN[:, :, 0:D], ALU.add).then_inc(s["op"], 1)
                v.reciprocal(DN[:, :, :], DN[:, :, :]).then_inc(s["op"], 1)
                v.wait_ge(s["op"], it * OPS + 4)
                v.tensor_tensor(heads(T[:, :, :]), heads(T[:, :, :]), spread(DN[:, :, :]), ALU.mult).then_inc(s["op"], 1)
                v.wait_ge(s["op"], it * OPS + 5)
                v.tensor_tensor(T[:, :, :], T[:, :, :], B[:, :].unsqueeze(1).broadcast_to([P, U7, D]),
                                ALU.add).then_inc(s["op"], 1)
                v.wait_ge(s["op"], it * OPS + 6)
                v.scalar_tensor_tensor(sh.X[:, blk, :], T[:, :, :], 0.0, sh.X[:, blk, :], ALU.max, ALU.add).then_inc(s["op"], 1)
            v.wait_ge(s["op"], OPS * (NB // U7))


def finish_weighted(sh, tag, acc, stats, w1t, w2t, b1, b2):
    nc = sh.nc
    s = {n: sh.sem(f"{tag}_{n}") for n in ("w", "bias", "xn", "tr", "xt", "side", "mm", "op", "norm")}
    OPS = 8
    with Scope(nc) as sc:
        W = sc.sb(f"{tag}_W", [P, 2, KC, D])
        B = sc.sb(f"{tag}_B", [P, 2, D])
        XR = sc.sb(f"{tag}_XR", [P, U7, D])
        XT = sc.sb(f"{tag}_XT", [P, 2, KC, P])
        ST = sc.sb(f"{tag}_ST", [P, 2, KC, P])
        O = sc.sb(f"{tag}_O", [P, U7, D])
        Q = sc.sb(f"{tag}_Q", [P, U7, D])
        NR = sc.sb(f"{tag}_NR", [P, U7])
        pO = sc.ps(f"{tag}_pO", [P, 4, 2, D])
        pT = [sc.ps(f"{tag}_pT{j}", [P, KC, P]) for j in range(2)]
        block = sc.block()

        def out_of(u):
            return pO[:, u // 2, u % 2, :]

        @block.sync
        def _(sp):
            for j, w in enumerate((w1t, w2t)):
                sp.dma_start(W[:, j], w.rearrange("(c k) n -> k c n", k=P)).then_inc(s["w"], 16)
            for j, b in enumerate((b1, b2)):
                sp.dma_start(B[:, j, :], bcast_rows(b)).then_inc(s["bias"], 16)

        @block.scalar
        def _(a):
            with a.Fori(0, NB // U7) as it:
                for u in range(U7):
                    a.wait_ge(s["tr"], it * U7 + u + 1)
                    if u >= 2:
                        a.wait_ge(s["mm"], it * U7 + u - 1)
                    else:
                        a.wait_ge(s["mm"], it * U7)
                    a.activation(XT[:, u % 2], pT[u % 2][:, :, :], ACT.Copy).then_inc(s["xt"], 1)
                a.wait_ge(s["op"], it * OPS + 4)
                a.activation(NR[:, :], NR[:, :], ACT.Sqrt).then_inc(s["norm"], 1)

        @block.tensor
        def _(pe):
            def turn(it, u):
                pe.wait_ge(s["xn"], it * U7 + u + 1)
                pe.wait_ge(s["xt"], it * U7 + (u - 1 if u >= 2 else 0))
                for c in range(KC):
                    m = pe.transpose(pT[u % 2][:, c, :], XR[:, u, c * P:(c + 1) * P], sh.ident[:, :])
                m.then_inc(s["tr"], 1)

            pe.wait_ge(s["w"], 32)
            with pe.Fori(0, NB // U7) as it:
                pe.wait_ge(s["op"], it * OPS)
                turn(it, 0)
                for u in range(U7):
                    if u + 1 < U7:
                        turn(it, u + 1)
                    pe.wait_ge(s["xt"], it * U7 + u + 1)
                    for c in range(KC):
                        pe.matmul(out_of(u), XT[:, u % 2, c, :], W[:, 0, c, :], start=(c == 0), stop=False)
                    pe.wait_ge(s["side"], it * U7 + u + 1)
                    for c in range(KC):
                        m = pe.matmul(out_of(u), ST[:, u % 2, c, :], W[:, 1, c, :], start=False, stop=(c == KC - 1))
                    m.then_inc(s["mm"], 1)

        @block.vector
        def _(v):
            v.wait_ge(s["bias"], 32)
            v.tensor_tensor(B[:, 0, :], B[:, 0, :], B[:, 1, :], ALU.add).then_inc(s["bias"], 1)
            v.wait_ge(s["bias"], 33)
            with v.Fori(0, NB // U7) as it:
                blk = bass.ds(it * U7, U7)
                v.wait_ge(s["tr"], it * U7)
                for u in range(U7):
                    i = it * U7 + u
                    v.tensor_scalar(XR[:, u, :], sh.X[:, bass.ds(i, 1), :].rearrange("p a d -> p (a d)"),
                                    stats[:, bass.ds(i, 1), 0:1].rearrange("p a b -> p (a b)"),
                                    stats[:, bass.ds(i, 1), 1:2].rearrange("p a b -> p (a b)"),
                                    ALU.subtract, ALU.mult).then_inc(s["xn"], 1)
                for u in range(U7):
                    v.wait_ge(s["xt"], it * U7 + u + 1)
                    v.wait_ge(s["mm"], it * U7 + (u - 1 if u >= 2 else 0))
                    v.scalar_tensor_tensor(ST[:, u % 2], XT[:, u % 2], 1.0,
                                           acc[:, :, bass.ds((it * U7 + u) * P, P)], ALU.add, ALU.mult).then_inc(s["side"], 1)
                v.wait_ge(s["mm"], it * U7 + U7)
                pall = pO[:, :, :, :].rearrange("p a b d -> p (a b) d")[:, 0:U7, :]
                v.tensor_tensor(O[:, :, :], pall, B[:, 0, :].unsqueeze(1).broadcast_to([P, U7, D]), ALU.add).then_inc(s["op"], 1)
                v.wait_ge(s["op"], it * OPS + 1)
                v.scalar_tensor_tensor(O[:, :, :], O[:, :, :], SLOPE, O[:, :, :], ALU.mult, ALU.max).then_inc(s["op"], 1)
                v.wait_ge(s["op"], it * OPS + 2)
                v.tensor_tensor(Q[:, :, :], O[:, :, :], O[:, :, :], ALU.mult).then_inc(s["op"], 1)
                v.wait_ge(s["op"], it * OPS + 3)
                v.tensor_reduce(NR[:, :], Q[:, :, :], AX.X, ALU.add).then_inc(s["op"], 1)
                v.wait_ge(s["norm"], it + 1)
                v.tensor_scalar(NR[:, :], NR[:, :], 1e-12, None, ALU.max).then_inc(s["op"], 1)
                v.wait_ge(s["op"], it * OPS + 5)
                v.reciprocal(NR[:, :], NR[:, :]).then_inc(s["op"], 1)
                v.wait_ge(s["op"], it * OPS + 6)
                v.tensor_tensor(O[:, :, :], O[:, :, :], NR[:, :].unsqueeze(2).broadcast_to([P, U7, D]), ALU.mult).then_inc(s["op"], 1)
                v.wait_ge(s["op"], it * OPS + 7)
                v.tensor_tensor(sh.X[:, blk, :], sh.X[:, blk, :], O[:, :, :], ALU.add).then_inc(s["op"], 1)
            v.wait_ge(s["op"], OPS * (NB // U7))


def free_edges_pass(sh, tag, src_t, dst_t, table, adst, gmax, keep, gather_done, rounds0, b_gat, gamma, beta, scores):
    nc = sh.nc
    EX = 4
    VC = HEADS * EX + HEADS
    NA = 25
    RING = 2 * GRP
    RND = NGRF // 2
    MVR = 4
    s = {n: sh.sem(f"{tag}_{n}") for n in ("loaded", "idx", "staged", "slots_free", "lo", "hi", "ad", "z", "arg", "p", "val", "mv",
                                           "mm", "self", "par", "fin", "var", "sq")}
    with Scope(nc) as sc:
        SRC = sc.sb(f"{tag}_SRC", [P, NTF], I32)
        DST = sc.sb(f"{tag}_DST", [P, NTF], I32)
        DC = sc.sb(f"{tag}_DC", [P, NTF], I32)
        TI = sc.sb(f"{tag}_TI", [P, NTF], I32)
        LO = sc.sb(f"{tag}_LO", [P, NTF])
        HI = sc.sb(f"{tag}_HI", [P, NTF])
        STG = sc.sb(f"{tag}_STG", [P, 2, 2, GRP], I32)
        G = sc.sb(f"{tag}_G", [P, RING, VC])
        A = sc.sb(f"{tag}_A", [P, RING, HEADS])
        OL = sc.sb(f"{tag}_OL", [P, 2, GRP, P])
        OH = sc.sb(f"{tag}_OH", [P, 2, GRP, NB])
        Z = sc.sb(f"{tag}_Z", [P, 2, 2, GRP, HEADS])
        ARG = sc.sb(f"{tag}_ARG", [P, 2, GRP, HEADS])
        V = sc.sb(f"{tag}_V", [P, 2, GRP, VC])
        MV = sc.sb(f"{tag}_MV", [P, MVR, NB, VC])
        ZS = sc.sb(f"{tag}_ZS", [P, 2, NB, HEADS])
        PS = sc.sb(f"{tag}_PS", [P, NB, HEADS])
        R = sc.sb(f"{tag}_R", [P, NB, HEADS * EX])
        R2 = sc.sb(f"{tag}_R2", [P, NB, HEADS * EX])
        DN = sc.sb(f"{tag}_DN", [P, NB, HEADS])
        MU = sc.sb(f"{tag}_MU", [P, NB])
        VR = sc.sb(f"{tag}_VR", [P, NB])
        PAR = sc.sb(f"{tag}_PAR", [P, 3, HEADS * EX])
        pS = [sc.ps(f"{tag}_pS{j}", [P, 512]) for j in range(2)]
        block = sc.block()
        parts = [(0, NA), (NA, NB - NA)]

        def over_groups(eng, step):
            step(0, 0)
            with eng.Fori(0, RND - 1) as it:
                step(it, 1)
                step(it + 1, 0)
            step(RND - 1, 1)

        @block.sync
        def _(sp):
            sp.dma_start(SRC[:, :], src_t).then_inc(s["loaded"], 16)
            sp.dma_start(DST[:, :], dst_t).then_inc(s["loaded"], 16)
            for j, w in enumerate((b_gat, gamma, beta)):
                sp.dma_start(PAR[:, j, :], bcast_rows(w)).then_inc(s["par"], 16)

        @block.gpsimd
        def _(pool):
            pool.wait_ge(s["idx"], 6)

            def gathers(rnd, par):
                k = rnd * 2 + par
                for u in range(GRP):
                    at_least(pool, gather_done[par * GRP + u], rounds0 * 16 + rnd * 32)
                pool.tensor_copy(STG[:, par, 0, :], SRC[:, bass.ds(k * GRP, GRP)]).then_inc(s["staged"], 1)
                pool.tensor_copy(STG[:, par, 1, :], DC[:, bass.ds(k * GRP, GRP)]).then_inc(s["staged"], 1)
                at_least(pool, s["val"], 2 * (k - 1))
                pool.wait_ge(s["staged"], 2 * k + 2)
                pool.sem_inc(s["slots_free"], 1)
                for u in range(GRP):
                    slot = par * GRP + u
                    pool.indirect_dma_start(G[:, slot, :], None, table, bass.IndirectOffsetOnAxis(
                        ap=STG[:, par, 0, u:u + 1].bitcast(U32), axis=0)).then_inc(gather_done[slot], 16)
                    pool.indirect_dma_start(A[:, slot, :], None, adst, bass.IndirectOffsetOnAxis(
                        ap=STG[:, par, 1, u:u + 1].bitcast(U32), axis=0)).then_inc(gather_done[slot], 16)

            gathers(0, 0)
            gathers(0, 1)
            with pool.Fori(1, RND) as rnd:
                gathers(rnd, 0)
                gathers(rnd, 1)

        @block.vector
        def _(v):
            v.wait_ge(s["loaded"], 32)
            v.tensor_scalar(SRC[:, :], SRC[:, :], N - 1, None, ALU.min).then_inc(s["idx"], 1)
            v.tensor_scalar(DC[:, :], DST[:, :], N - 1, None, ALU.min).then_inc(s["idx"], 1)
            v.tensor_scalar(TI[:, :], DST[:, :], P - 1, None, ALU.bitwise_and).then_inc(s["idx"], 1)
            v.wait_ge(s["idx"], 3)
            v.tensor_copy(LO[:, :], TI[:, :]).then_inc(s["idx"], 1)
            v.wait_ge(s["idx"], 4)
            v.tensor_scalar(TI[:, :], DST[:, :], 7, None, ALU.logical_shift_right).then_inc(s["idx"], 1)
            v.wait_ge(s["idx"], 5)
            v.tensor_copy(HI[:, :], TI[:, :]).then_inc(s["idx"], 1)
            v.wait_ge(s["idx"], 6)

            def step(rnd, par):
                k = rnd * 2 + par
                slots = slice(par * GRP, par * GRP + GRP)
                at_least(v, s["mm"], (k - 1) * GRP)
                for u in range(GRP):
                    v.tensor_scalar(OL[:, par, u, :], sh.iota[:, :], LO[:, bass.ds(k * GRP + u, 1)], None,
                                    ALU.is_equal).then_inc(s["lo"], 1)
                v.tensor_tensor(OH[:, par], sh.iota[:, 0:NB].unsqueeze(1).broadcast_to([P, GRP, NB]),
                                HI[:, bass.ds(k * GRP, GRP)].unsqueeze(2).broadcast_to([P, GRP, NB]),
                                ALU.is_equal).then_inc(s["hi"], 1)
                for u in range(GRP):
                    v.wait_ge(gather_done[par * GRP + u], rounds0 * 16 + (rnd + 1) * 32)
                v.tensor_tensor(Z[:, par, 0], G[:, slots, EX * HEADS:VC], A[:, slots, :], ALU.add).then_inc(s["z"], 1)
                v.tensor_tensor(Z[:, par, 1], gmax[:, :].unsqueeze(1).broadcast_to([P, GRP, HEADS]), A[:, slots, :],
                                ALU.add).then_inc(s["z"], 1)
                v.wait_ge(s["z"], k * 3 + 2)
                zf = Z[:, par].rearrange("p a u h -> p (a u h)")
                v.scalar_tensor_tensor(zf, zf, SLOPE, zf, ALU.mult, ALU.max).then_inc(s["z"], 1)
                v.wait_ge(s["z"], k * 3 + 3)
                v.tensor_tensor(ARG[:, par], Z[:, par, 0], Z[:, par, 1], ALU.subtract).then_inc(s["arg"], 1)
                v.wait_ge(s["p"], k + 1)
                v.tensor_tensor(V[:, par, :, 0:EX * HEADS].rearrange("p u (h q) -> p u h q", h=HEADS),
                                G[:, slots, 0:EX * HEADS].rearrange("p u (h q) -> p u h q", h=HEADS),
                                ARG[:, par].unsqueeze(3).broadcast_to([P, GRP, HEADS, EX]), ALU.mult).then_inc(s["val"], 1)
                v.tensor_copy(V[:, par, :, EX * HEADS:VC], ARG[:, par]).then_inc(s["val"], 1)
                v.wait_ge(s["hi"], k + 1)
                v.wait_ge(s["val"], 2 * k + 2)
                for u in range(GRP):
                    at_least(v, s["mm"], k * GRP + u - MVR + 1)
                    v.tensor_tensor(MV[:, u % MVR], OH[:, par, u, :].unsqueeze(2).broadcast_to([P, NB, VC]),
                                    V[:, par, u, :].unsqueeze(1).broadcast_to([P, NB, VC]), ALU.mult).then_inc(s["mv"], 1)

            over_groups(v, step)

            self_factor(sh, v, None, s["self"], keep, EX * HEADS, gmax, ZS, PS)[0]()
            v.wait_ge(s["self"], 5)
            v.wait_ge(s["mm"], NTF)
            v.wait_ge(s["par"], 48)

            then = Chain(v, s["fin"])

            def heads(ap):
                return ap.rearrange("p i (h q) -> p i h q", h=HEADS)

            def all16(ap, j):
                return ap[:, j, :].unsqueeze(1).broadcast_to([P, NB, EX * HEADS])

            def per_head(ap, m=NB):
                return ap.unsqueeze(3).broadcast_to([P, m, HEADS, EX])

            then(v.tensor_tensor(heads(R[:, :, :]), heads(keep[:, :, 0:EX * HEADS]), per_head(PS[:, :, :]), ALU.mult))
            for j, (b0, m) in enumerate(parts):
                sums = pS[j][:, 0:m * VC].rearrange("p (i c) -> p i c", c=VC)
                then(v.tensor_tensor(DN[:, b0:b0 + m, :], PS[:, b0:b0 + m, :], sums[:, :, EX * HEADS:VC], ALU.add))
                then(v.tensor_tensor(R[:, b0:b0 + m, :], R[:, b0:b0 + m, :], sums[:, :, 0:EX * HEADS], ALU.add))
            then(v.reciprocal(DN[:, :, :], DN[:, :, :]))
            then(v.tensor_tensor(heads(R[:, :, :]), heads(R[:, :, :]), per_head(DN[:, :, :]), ALU.mult))
            then(v.tensor_tensor(R[:, :, :], R[:, :, :], all16(PAR, 0), ALU.add))
            then(v.tensor_reduce(MU[:, :], R[:, :, :], AX.X, ALU.add))
            then(v.tensor_scalar(MU[:, :], MU[:, :], 1.0 / (EX * HEADS), None, ALU.mult))
            wide = [P, NB, EX * HEADS]
            then(v.tensor_tensor(R[:, :, :], R[:, :, :], MU[:, :].unsqueeze(2).broadcast_to(wide), ALU.subtract))
            then(v.tensor_tensor(R2[:, :, :], R[:, :, :], R[:, :, :], ALU.mult))
            then(v.tensor_reduce(VR[:, :], R2[:, :, :], AX.X, ALU.add))
            then(v.tensor_scalar(VR[:, :], VR[:, :], 1.0 / (EX * HEADS), EPS, ALU.mult, ALU.add), s["var"])
            v.wait_ge(s["sq"], 1)
            then(v.reciprocal(VR[:, :], VR[:, :]))
            then(v.tensor_tensor(R[:, :, :], R[:, :, :], VR[:, :].unsqueeze(2).broadcast_to(wide), ALU.mult))
            then(v.tensor_tensor(R[:, :, :], R[:, :, :], all16(PAR, 1), ALU.mult))
            then(v.tensor_tensor(R[:, :, :], R[:, :, :], all16(PAR, 2), ALU.add))
            then(v.tensor_reduce(scores[:, :, :], R[:, :, :].rearrange("p i (h q) -> p i q h", h=HEADS), AX.X, ALU.add))
            then(v.tensor_scalar(scores[:, :, :], scores[:, :, :], 1.0 / HEADS, None, ALU.mult))

        @block.scalar
        def _(a):
            def step(rnd, par):
                a.wait_ge(s["arg"], rnd * 2 + par + 1)
                a.activation(ARG[:, par], ARG[:, par], ACT.Exp).then_inc(s["p"], 1)

            over_groups(a, step)
            self_factor(sh, None, a, s["self"], keep, EX * HEADS, gmax, ZS, PS)[1]()
            a.wait_ge(s["var"], 1)
            a.activation(VR[:, :], VR[:, :], ACT.Sqrt).then_inc(s["sq"], 1)

        @block.tensor
        def _(pe):
            def step(rnd, par):
                k = rnd * 2 + par
                last = isinstance(rnd, int) and rnd == RND - 1 and par == 1
                for u in range(GRP):
                    pe.wait_ge(s["lo"], k * GRP + u + 1)
                    pe.wait_ge(s["mv"], k * GRP + u + 1)
                    for j, (b0, m) in enumerate(parts):
                        mm = pe.matmul(pS[j][:, 0:m * VC], OL[:, par, u, :],
                                       MV[:, u % MVR, b0:b0 + m, :].rearrange("p i c -> p (i c)"),
                                       start=(isinstance(k, int) and k == 0 and u == 0), stop=(last and u == GRP - 1),
                                       skip_group_check=True)
                    mm.then_inc(s["mm"], 1)

            over_groups(pe, step)


def route(sh, tag, E, logits, weights, pos, pos_get, expert_of):
    nc = sh.nc
    J = TOP * NB
    NT = tiles_of(E)
    s = {n: sh.sem(f"{tag}_{n}") for n in ("iota", "op", "diff", "onehots", "exp", "mm")}
    with Scope(nc) as sc:
        REV = sc.sb(f"{tag}_REV", [P, E])
        DUMP = sc.sb(f"{tag}_DUMP", [P, TOP])
        NV = sc.sb(f"{tag}_NV", [P, 1])
        Q = sc.sb(f"{tag}_Q", [P, NB, E])
        L2 = sc.sb(f"{tag}_L2", [P, NB, E])
        M = sc.sb(f"{tag}_M", [P, TOP, NB])
        K = sc.sb(f"{tag}_K", [P, NB])
        DD = sc.sb(f"{tag}_DD", [P, NB])
        OH = sc.sb(f"{tag}_OH", [P, TOP, NB, E])
        TOT = sc.sb(f"{tag}_TOT", [P, J, E])
        INC = sc.sb(f"{tag}_INC", [P, J, E])
        TI = sc.sb(f"{tag}_TI", [P, E], I32)
        TF = sc.sb(f"{tag}_TF", [P, E])
        CUM = sc.sb(f"{tag}_CUM", [P, E])
        BASE = sc.sb(f"{tag}_BASE", [P, E])
        PF = sc.sb(f"{tag}_PF", [P, J])
        PG = sc.sb(f"{tag}_PG", [P, J])
        EF = sc.sb(f"{tag}_EF", [1, NT])
        pW = sc.ps(f"{tag}_pW", [P, TOP, 512])
        pC = sc.ps(f"{tag}_pC", [P, TOP, 512])
        block = sc.block()

        @block.gpsimd
        def _(pool):
            pool.iota(DUMP[:, :], [[P, TOP]], base=ROWS, channel_multiplier=1,
                      allow_small_or_imprecise_dtypes=True).then_inc(s["iota"], 1)

        @block.scalar
        def _(a):
            a.wait_ge(s["diff"], 1)
            a.activation(DD[:, :], DD[:, :], ACT.Exp).then_inc(s["exp"], 1)

        @block.tensor
        def _(pe):
            pe.wait_ge(s["onehots"], 1)
            for k in range(TOP):
                rhs = OH[:, k].rearrange("p i e -> p (i e)")
                pe.matmul(pW[:, k, 0:NB * E], sh.tri[:, :], rhs, start=True, stop=True)
                m = pe.matmul(pC[:, k, 0:NB * E], sh.ones[:, :], rhs, start=True, stop=True)
            m.then_inc(s["mm"], 1)

        @block.vector
        def _(v):
            then = Chain(v, s["op"])
            all_e = [P, NB, E]

            def by_e(ap):
                return ap.unsqueeze(1).broadcast_to(all_e)

            def by_i(ap):
                return ap.unsqueeze(2).broadcast_to(all_e)

            then(v.tensor_scalar(REV[:, :], sh.iota[:, 0:E], -1.0, float(E), ALU.mult, ALU.add))
            cur = logits
            for k in range(TOP):
                then(v.tensor_reduce(M[:, k, :], cur[:, :, :], AX.X, ALU.max))
                then(v.tensor_tensor(Q[:, :, :], cur[:, :, :], by_i(M[:, k, :]), ALU.is_equal))
                then(v.tensor_tensor(Q[:, :, :], Q[:, :, :], by_e(REV[:, :]), ALU.mult))
                then(v.tensor_reduce(K[:, :], Q[:, :, :], AX.X, ALU.max))
                then(v.tensor_tensor(OH[:, k], by_e(REV[:, :]), by_i(K[:, :]), ALU.is_equal))
                if k == 0:
                    then(v.scalar_tensor_tensor(L2[:, :, :].rearrange("p i e -> p (i e)"),
                                                OH[:, 0].rearrange("p i e -> p (i e)"), -BIG,
                                                logits[:, :, :].rearrange("p i e -> p (i e)"), ALU.mult, ALU.add))
                    cur = L2
            then(v.tensor_tensor(DD[:, :], M[:, 1, :], M[:, 0, :], ALU.subtract), s["diff"])
            last = OH[:, :, NB - 1, :]
            then(v.tensor_scalar(last, last, sh.valid[:, NB - 1:NB], None, ALU.mult), s["onehots"])
            v.wait_ge(s["exp"], 1)
            then(v.tensor_scalar(weights[:, 0, :], DD[:, :], 1.0, None, ALU.add))
            then(v.reciprocal(weights[:, 0, :], weights[:, 0, :]))
            then(v.tensor_tensor(weights[:, 1, :], weights[:, 0, :], DD[:, :], ALU.mult))
            v.wait_ge(s["mm"], 1)
            counts = TOT[:, :, :].rearrange("p (k i) e -> p k (i e)", k=TOP)
            then(v.tensor_copy(counts, pC[:, :, 0:NB * E]))
            for e in range(E):
                then(v.tensor_tensor_scan(INC[:, :, e], sh.ones[:, 0:J], TOT[:, :, e], 0.0, ALU.mult, ALU.add))
            then(v.tensor_scalar(TI[:, :], INC[:, J - 1, :], float(P - 1), None, ALU.add))
            then(v.tensor_scalar(TI[:, :], TI[:, :], 7, None, ALU.logical_shift_right))
            then(v.tensor_copy(TF[:, :], TI[:, :]))
            then(v.tensor_tensor_scan(CUM[:, :], sh.ones[:, 0:E], TF[:, :], 0.0, ALU.mult, ALU.add))
            then(v.tensor_tensor(BASE[:, :], CUM[:, :], TF[:, :], ALU.subtract))
            then(v.tensor_scalar(BASE[:, :], BASE[:, :], float(P), None, ALU.mult))
            then(v.tensor_tensor(INC[:, :, :], INC[:, :, :], TOT[:, :, :], ALU.subtract))
            inc = INC[:, :, :].rearrange("p (k i) e -> p k (i e)", k=TOP)
            then(v.tensor_tensor(inc, inc, pW[:, :, 0:NB * E], ALU.add))
            then(v.tensor_tensor(INC[:, :, :], INC[:, :, :], BASE[:, :].unsqueeze(1).broadcast_to([P, J, E]), ALU.add))
            then(v.tensor_tensor(INC[:, :, :], INC[:, :, :], OH[:, :, :, :].rearrange("p k i e -> p (k i) e"), ALU.mult))
            then(v.tensor_reduce(PF[:, :], INC[:, :, :], AX.X, ALU.add))
            v.wait_ge(s["iota"], 1)
            then(v.tensor_scalar(NV[:, :], sh.valid[:, NB - 1:NB], -1.0, 1.0, ALU.mult, ALU.add))
            pad = PF[:, NB - 1:J:NB]
            then(v.scalar_tensor_tensor(pad, DUMP[:, :], NV[:, 0:1], pad, ALU.mult, ALU.add))
            then(v.tensor_copy(pos[:, :, :].rearrange("p k i -> p (k i)"), PF[:, :]))
            then(v.tensor_scalar(pos_get[:, :, :].rearrange("p k i -> p (k i)"), PF[:, :], float(NT * P - 1), None, ALU.min))
            then(v.tensor_scalar(EF[:, :], sh.iota[0:1, 0:NT], CUM[0:1, 0:1], None, ALU.is_ge))
            for e in range(1, E - 1):
                then(v.scalar_tensor_tensor(EF[:, :], sh.iota[0:1, 0:NT], CUM[0:1, e:e + 1], EF[:, :], ALU.is_ge, ALU.add))
            then(v.tensor_copy(expert_of[:, 0:NT], EF[:, :]))


def scatter_tokens(sh, tag, stats, stats2, pos, xs):
    nc = sh.nc
    s = {n: sh.sem(f"{tag}_{n}") for n in ("xt", "xn", "staged", "row_ready")}
    s["sent"] = sh.lasting_sem(f"{tag}_sent")
    with Scope(nc) as sc:
        XR = sc.sb(f"{tag}_XR", [P, U7, D])
        STG = sc.sb(f"{tag}_STG", [P, TOP, U7], I32)
        block = sc.block()

        @block.vector
        def _(v):
            def normalise(out, src, stats, i):
                return v.tensor_scalar(out, src, stats[:, bass.ds(i, 1), 0:1].rearrange("p a b -> p (a b)"),
                                       stats[:, bass.ds(i, 1), 1:2].rearrange("p a b -> p (a b)"),
                                       ALU.subtract, ALU.mult)

            with v.Fori(0, NB // U7) as it:
                v.wait_ge(s["sent"], it * U7 * TOP * 16)
                for u in range(U7):
                    i = it * U7 + u
                    row = sh.X[:, bass.ds(i, 1), :].rearrange("p a d -> p (a d)")
                    normalise(XR[:, u, :], row, stats, i).then_inc(s["xn"] if stats2 is None else s["xt"], 1)
                if stats2 is not None:
                    for u in range(U7):
                        v.wait_ge(s["xt"], it * U7 + u + 1)
                        normalise(XR[:, u, :], XR[:, u, :], stats2, it * U7 + u).then_inc(s["xn"], 1)

        @block.gpsimd
        def _(pool):
            pool.wait_ge(sh.rows_zeroed, NT_MAX // 3 * 16)
            with pool.Fori(0, NB // U7) as it:
                pool.wait_ge(s["sent"], it * U7 * TOP * 16)
                pool.tensor_copy(STG[:, :, :], pos[:, :, bass.ds(it * U7, U7)]).then_inc(s["staged"], 1)
                for u in range(U7):
                    pool.wait_ge(s["xn"], it * U7 + u + 1)
                    pool.wait_ge(s["staged"], it + 1)
                    pool.sem_inc(s["row_ready"], 1)
                    for k in range(TOP):
                        pool.indirect_dma_start(xs, bass.IndirectOffsetOnAxis(ap=STG[:, k, u:u + 1].bitcast(U32), axis=0),
                                                XR[:, u, :], None).then_inc(s["sent"], 16)
            pool.wait_ge(s["sent"], NB * TOP * 16)


def experts(sh, tag, E, H, w1, b1, w2, b2, expert_of, xs, ys, y_stored, ln_g=None, ln_b=None):
    nc = sh.nc
    HC = H // P
    NT = tiles_of(E)
    HB = H // 512
    s = {n: sh.sem(f"{tag}_{n}") for n in ("w1", "w2", "rows", "vt", "vc", "bmm", "badd", "scaled", "tin", "xt", "h",
                                           "hc", "tr", "gelu", "y", "yc", "x0", "x1")}
    with Scope(nc) as sc:
        W1 = sc.sb(f"{tag}_W1", [P, E * KC * H])
        W2 = sc.sb(f"{tag}_W2", [P, E * HC * D])
        B2 = sc.sb(f"{tag}_B2", [P, E, D])
        VR = sc.sb(f"{tag}_VR", [P, 3, P])
        VT = sc.sb(f"{tag}_VT", [P, 3, P])
        B1 = sc.sb(f"{tag}_B1", [P, E * HC])
        XI = sc.sb(f"{tag}_XI", [P, 2, D])
        XT = sc.sb(f"{tag}_XT", [P, 2, KC, P])
        HS = sc.sb(f"{tag}_HS", [P, H])
        GT = sc.sb(f"{tag}_GT", [P, HC, P])
        Y = sc.sb(f"{tag}_Y", [P, 2, D])
        pH = [sc.ps(f"{tag}_pH{j}", [P, H]) for j in range(2)]
        pT = sc.ps(f"{tag}_pT", [P, HC, P])
        pI = sc.ps(f"{tag}_pI", [P, KC, P])
        pY = sc.ps(f"{tag}_pY", [P, D])
        block = sc.block()
        vecs = [(b1, E * HC)] + ([(ln_g, E * KC), (ln_b, E * KC)] if ln_g is not None else [])

        def turned(j):
            return pI[:, j, :] if j < 2 else pT[:, 0, :]

        def over_tiles(eng, step):
            step(0, 0)
            with eng.Fori(0, (NT - 3) // 2) as it:
                step(it, 1)
                step(it + 1, 0)
            step((NT - 3) // 2, 1)
            step((NT - 1) // 2, 0)

        def expert(eng, regs, t0):
            eng.reg_load(regs, expert_of[0:1, bass.ds(t0, len(regs))])
            return [eng.snap(r, min_val=0, max_val=E - 1) for r in regs]

        @block.sync
        def _(sp):
            for j, (vec, m) in enumerate(vecs):
                sp.dma_start(VR[0:m, j, :], vec.rearrange("e (c p) -> (e c) p", p=P)).then_inc(s["rows"], 16)
            for e in range(E):
                sp.dma_start(W1[:, e * KC * H:(e + 1) * KC * H].rearrange("p (c n) -> p c n", c=KC),
                             w1[e].rearrange("(c p) n -> p c n", p=P)).then_inc(s["w1"], 16)
            for e in range(E):
                sp.dma_start(B2[:, e, :], bcast_rows(b2[e])).then_inc(s["w2"], 16)
                sp.dma_start(W2[:, e * HC * D:(e + 1) * HC * D].rearrange("p (c n) -> p c n", c=HC),
                             w2[e].rearrange("(c p) n -> p c n", p=P)).then_inc(s["w2"], 16)

            def load(t, b):
                at_least(sp, s["tin"], t - 1)
                sp.dma_start(XI[:, b, :], xs[bass.ds(t * P, P), :]).then_inc(s[f"x{b}"], 16)

            def store(t, b):
                sp.wait_ge(s["yc"], t + 1)
                sp.dma_start(ys[bass.ds(t * P, P), :], Y[:, b, :]).then_inc(y_stored[b], 16)

            load(0, 0)
            load(1, 1)

            def step(rnd, b):
                t = rnd * 2 + b
                if not isinstance(t, int) or t + 2 < NT:
                    load(t + 2, b)
                store(t, b)

            over_tiles(sp, step)
            sp.wait_ge(y_stored[0], (NT + 1) // 2 * 16)
            sp.wait_ge(y_stored[1], NT // 2 * 16)

        @block.scalar
        def _(a):
            regs = [a.alloc_register(f"{tag}_a")]

            def copy_in(t, b):
                a.wait_ge(s["tin"], t + 1)
                at_least(a, s["h"], t - 1)
                a.activation(XT[:, b], pI[:, :, :], ACT.Copy).then_inc(s["xt"], 1)

            copy_in(0, 0)

            def step(rnd, b):
                t = rnd * 2 + b
                if not isinstance(t, int) or t + 1 < NT:
                    copy_in(t + 1, 1 - b)
                e, = expert(a, regs, t)
                a.wait_ge(s["badd"], 1)
                a.wait_ge(s["tr"], t + 1)
                at_least(a, s["y"], t)
                for c in range(HC):
                    m = a.activation(GT[:, c, :], pT[:, c, :], ACT.Gelu, bias=B1[:, bass.ds(e * HC + c, 1)])
                m.then_inc(s["gelu"], 1)

            over_tiles(a, step)

        @block.vector
        def _(v):
            v.wait_ge(s["vt"], 1)
            nv = len(vecs)
            for j, (_, m) in enumerate(vecs):
                v.tensor_copy(VT[:, j, 0:m], turned(j)[:, 0:m]).then_inc(s["vc"], 1)
            v.wait_ge(s["vc"], nv)
            if ln_g is not None:
                v.wait_ge(s["bmm"], 1)
                v.tensor_tensor(B1[:, :], VT[:, 0, 0:E * HC], pY[:, 0:E * HC], ALU.add).then_inc(s["badd"], 1)
                for c in range(E * KC):
                    v.tensor_scalar(W1[:, c * H:(c + 1) * H], W1[:, c * H:(c + 1) * H], VT[:, 1, c:c + 1], None,
                                    ALU.mult).then_inc(s["scaled"], 1)
            else:
                v.tensor_copy(B1[:, :], VT[:, 0, 0:E * HC]).then_inc(s["badd"], 1)
            v.wait_ge(s["w2"], 32 * E)
            regs = [v.alloc_register(f"{tag}_v")]

            def bias_out(rnd, b):
                t = rnd * 2 + b
                e, = expert(v, regs, t)
                v.wait_ge(s["y"], t + 1)
                at_least(v, y_stored[b], rnd * 16)
                v.tensor_tensor(Y[:, b, :], pY[:, :], B2[:, bass.ds(e, 1), :].rearrange("p a d -> p (a d)"),
                                ALU.add).then_inc(s["yc"], 1)

            def step(rnd, b):
                t = rnd * 2 + b
                v.wait_ge(s["h"], t + 1)
                at_least(v, s["tr"], t)
                v.tensor_copy(HS[:, :], pH[b][:, :]).then_inc(s["hc"], 1)
                if not (isinstance(t, int) and t == 0):
                    bias_out(rnd - (1 - b), 1 - b)

            over_tiles(v, step)
            bias_out((NT - 1) // 2, 0)

        @block.tensor
        def _(pe):
            pe.wait_ge(s["rows"], 16 * len(vecs))
            for j, (_, m) in enumerate(vecs):
                t = pe.transpose(turned(j)[:, 0:m], VR[0:m, j, :], sh.ident[0:m, 0:m])
            t.then_inc(s["vt"], 1)
            pe.wait_ge(s["vc"], len(vecs))
            pe.wait_ge(s["w1"], 16 * E)
            if ln_g is not None:
                for e in range(E):
                    for h in range(HC):
                        for c in range(KC):
                            o = (e * KC + c) * H + h * P
                            m = pe.matmul(pY[:, e * HC + h:e * HC + h + 1], W1[:, o:o + P],
                                          VT[:, 2, e * KC + c:e * KC + c + 1], start=(c == 0), stop=(c == KC - 1))
                m.then_inc(s["bmm"], 1)
                pe.wait_ge(s["scaled"], E * KC)
            pe.wait_ge(s["badd"], 1)
            pe.wait_ge(s["w2"], 32 * E)
            regs = [pe.alloc_register(f"{tag}_p{j}") for j in range(2)]

            def turn_in(t, b, rnd):
                pe.wait_ge(s[f"x{b}"], rnd * 16)
                at_least(pe, s["xt"], t)
                for c in range(KC):
                    m = pe.transpose(pI[:, c, :], XI[:, b, c * P:(c + 1) * P], sh.ident[:, :])
                m.then_inc(s["tin"], 1)

            turn_in(0, 0, 1)

            def by_w1(t, b, e):
                pe.wait_ge(s["xt"], t + 1)
                at_least(pe, s["hc"], t - 1)
                for n in range(HB):
                    for c in range(KC):
                        m = pe.matmul(pH[b][:, n * 512:(n + 1) * 512], XT[:, b, c, :],
                                      W1[:, bass.ds(e * (KC * H) + (c * H + n * 512), 512)],
                                      start=(c == 0), stop=(c == KC - 1))
                m.then_inc(s["h"], 1)

            def by_w2(t, e):
                pe.wait_ge(s["gelu"], t + 1)
                at_least(pe, s["yc"], t)
                for c in range(HC):
                    m = pe.matmul(pY[:, :], GT[:, c, :], W2[:, bass.ds(e * (HC * D) + c * D, D)],
                                  start=(c == 0), stop=(c == HC - 1))
                m.then_inc(s["y"], 1)

            def step(rnd, b):
                t = rnd * 2 + b
                if isinstance(t, int) and t == 0:
                    e, = expert(pe, regs[1:], 0)
                    by_w1(t, b, e)
                else:
                    e_before, e = expert(pe, regs, t - 1)
                    by_w1(t, b, e)
                    by_w2(t - 1, e_before)
                if not isinstance(t, int) or t + 1 < NT:
                    turn_in(t + 1, 1 - b, rnd + b + 1)
                pe.wait_ge(s["hc"], t + 1)
                at_least(pe, s["gelu"], t)
                for c in range(HC):
                    m = pe.transpose(pT[:, c, :], HS[:, c * P:(c + 1) * P], sh.ident[:, :])
                m.then_inc(s["tr"], 1)

            over_tiles(pe, step)
            e, = expert(pe, regs[1:], NT - 1)
            by_w2(NT - 1, e)


def combine(sh, tag, weights, pos_get, ys, y_stored, y_counts):
    nc = sh.nc
    s = {n: sh.sem(f"{tag}_{n}") for n in ("staged", "sum", "slot_free")}
    s_got = [sh.lasting_sem(f"{tag}_got{u}") for u in range(U7)]
    with Scope(nc) as sc:
        R = sc.sb(f"{tag}_R", [P, TOP, U7, D])
        STG = sc.sb(f"{tag}_STG", [P, TOP, U7], I32)
        block = sc.block()

        @block.gpsimd
        def _(pool):
            pool.wait_ge(y_stored[0], y_counts[0])
            with pool.Fori(0, NB // U7) as it:
                for u in range(U7):
                    pool.wait_ge(s_got[u], it * TOP * 16)
                pool.tensor_copy(STG[:, :, :], pos_get[:, :, bass.ds(it * U7, U7)]).then_inc(s["staged"], 1)
                pool.wait_ge(s["staged"], it + 1)
                for u in range(U7):
                    pool.wait_ge(s["sum"], it * U7 * TOP)
                    pool.sem_inc(s["slot_free"], 1)
                    for k in range(TOP):
                        pool.indirect_dma_start(R[:, k, u, :], None, ys, bass.IndirectOffsetOnAxis(
                            ap=STG[:, k, u:u + 1].bitcast(U32), axis=0)).then_inc(s_got[u], 16)

        @block.vector
        def _(v):
            with v.Fori(0, NB // U7) as it:
                for k in range(TOP):
                    for u in range(U7):
                        if k == 0:
                            v.wait_ge(s_got[u], (it + 1) * TOP * 16)
                        else:
                            v.wait_ge(s["sum"], it * U7 * TOP + u + 1)
                        i = it * U7 + u
                        row = sh.X[:, bass.ds(i, 1), :].rearrange("p a d -> p (a d)")
                        v.scalar_tensor_tensor(row, R[:, k, u, :], weights[:, k, bass.ds(i, 1)], row,
                                               ALU.mult, ALU.add).then_inc(s["sum"], 1)
            v.wait_ge(s["sum"], NB * TOP)


def store_out(sh, out):
    s_o = sh.sem("out_stored")
    with Scope(sh.nc) as sc:
        block = sc.block()

        @block.sync
        def _(sp):
            full = out[0:(NB - 1) * P, :].rearrange("(i p) d -> p i d", p=P)
            for c in range(6):
                sp.dma_start(full[:, 8 * c:8 * c + 8, :], sh.X[:, 8 * c:8 * c + 8, :]).then_inc(s_o, 16)
            sp.dma_start(out[(NB - 1) * P:N, :], sh.X[0:LAST, NB - 1, :]).then_inc(s_o, 16)
            sp.wait_ge(s_o, 7 * 16)


def add_bias(sh, tag, L, bias, E):
    s_b, s_a = sh.sem(f"{tag}_loaded"), sh.sem(f"{tag}_added")
    with Scope(sh.nc) as sc:
        B = sc.sb(f"{tag}_B", [P, E])
        block = sc.block()

        @block.sync
        def _(sp):
            sp.dma_start(B[:, :], bcast_rows(bias)).then_inc(s_b, 16)

        @block.vector
        def _(v):
            v.wait_ge(s_b, 16)
            v.tensor_tensor(L[:, :, :], L[:, :, :], B[:, :].unsqueeze(1).broadcast_to([P, NB, E]), ALU.add).then_inc(s_a, 1)


def second_stats(sh, tag, stats2):
    s_v, s_q = sh.sem(f"{tag}_var"), sh.sem(f"{tag}_sqrt")
    with Scope(sh.nc) as sc:
        block = sc.block()

        @block.vector
        def _(v):
            v.tensor_scalar(stats2[:, :, 1], stats2[:, :, 1], EPS, None, ALU.add).then_inc(s_v, 1)
            v.wait_ge(s_q, 1)
            v.reciprocal(stats2[:, :, 1], stats2[:, :, 1]).then_inc(s_v, 1)

        @block.scalar
        def _(a):
            a.wait_ge(s_v, 1)
            a.activation(stats2[:, :, 1], stats2[:, :, 1], ACT.Sqrt).then_inc(s_q, 1)


def build(nc, a, out, stop=99):
    def dram(name, shape):
        return nc.dram_tensor(name, shape, F32, kind="Internal").ap()

    with ExitStack() as ctx:
        sh = Shared(nc, ctx)
        table0 = dram("table0", (NP, D + HEADS))
        adst0 = dram("adst0", (NP + WIN, HEADS))
        table1 = dram("table1", (NP, D))
        table2 = dram("table2", (NP, 16 + HEADS))
        adst2 = dram("adst2", (NP + WIN, HEADS))
        xs = dram("xs", (ROWS + TOP * P, D))
        ys = dram("ys", (ROWS, D))
        gather_done = [sh.lasting_sem(f"gather_done{j}") for j in range(2 * GRP)]
        y_stored = [sh.lasting_sem(f"y_stored{j}") for j in range(2)]
        stats = sh.sb("stats", [P, NB, 2])
        rounds = NTE // (2 * GRP)

        setup(sh, a["x"], xs)

        layer_norm_stats(sh, "s0", stats)
        with Scope(nc) as layer:
            keep = layer.sb("keep0", [P, NB, 2 * HEADS])
            gmax = layer.sb("gmax0", [P, HEADS])
            acc = layer.sb("acc0", [P, 3, NACC])
            project_nodes(sh, "p0", stats, a["L0_gnn_W"], D + 2 * HEADS, att=(a["L0_gnn_att_src"], a["L0_gnn_att_dst"]),
                          table=table0, table_cols=D + HEADS, keep=keep, keep_from=D)
            table_maximum(sh, "m0", keep, 0, gmax)
            store_adst(sh, "d0", keep, HEADS, adst0)
            graph_pass(sh, "g0", a["src_t"], a["dst_t"], table0, D + HEADS, acc, gather_done, 0, adst=adst0, gmax=gmax)
            finish_attention(sh, "f0", acc, table0, keep, gmax, a["L0_gnn_bias"])
        if stop == 1:
            return store_out(sh, out)

        sh.end_layer()

        layer_norm_stats(sh, "s1", stats)
        with Scope(nc) as layer:
            weights = layer.sb("weights0", [P, TOP, NB])
            pos = layer.sb("pos0", [P, TOP, NB], I32)
            pos_get = layer.sb("pos_get0", [P, TOP, NB], I32)
            expert_of = layer.sb("expert_of0", [1, NT_MAX], I32)
            with Scope(nc) as inner:
                stats2 = inner.sb("stats2", [P, NB, 2])
                logits = inner.sb("logits0", [P, NB, 8])
                project_nodes(sh, "p1", stats, a["L0_ffn_Wr"], 8, keep=logits, stats2=stats2)
                add_bias(sh, "rb", logits, a["L0_ffn_br"], 8)
                second_stats(sh, "s2", stats2)
                route(sh, "r0", 8, logits, weights, pos, pos_get, expert_of)
                scatter_tokens(sh, "t0", stats, stats2, pos, xs)
            experts(sh, "e0", 8, 1024, a["L0_ffn_W1"], a["L0_ffn_b1"], a["L0_ffn_W2"], a["L0_ffn_b2"], expert_of, xs, ys,
                    y_stored, ln_g=a["L0_ffn_ln_g"], ln_b=a["L0_ffn_ln_b"])
            combine(sh, "c0", weights, pos_get, ys, y_stored, (16 * ((tiles_of(8) + 1) // 2),))
        if stop == 2:
            return store_out(sh, out)

        sh.end_layer()

        layer_norm_stats(sh, "s3", stats)
        with Scope(nc) as layer:
            acc = layer.sb("acc1", [P, 2, NACC])
            store_rows(sh, "p2", stats, table1)
            graph_pass(sh, "g1", a["src_t"], a["dst_t"], table1, D, acc, gather_done, rounds, weight_t=a["weight_t"])
            finish_weighted(sh, "f1", acc, stats, a["L1_gnn_W1t"], a["L1_gnn_W2t"], a["L1_gnn_b1"], a["L1_gnn_b2"])
        if stop == 3:
            return store_out(sh, out)

        sh.end_layer()

        layer_norm_stats(sh, "s4", stats)
        with Scope(nc) as layer:
            weights = layer.sb("weights1", [P, TOP, NB])
            pos = layer.sb("pos1", [P, TOP, NB], I32)
            pos_get = layer.sb("pos_get1", [P, TOP, NB], I32)
            expert_of = layer.sb("expert_of1", [1, NT_MAX], I32)
            with Scope(nc) as inner:
                keep = inner.sb("keep1", [P, NB, 16 + 2 * HEADS])
                gmax = inner.sb("gmax1", [P, HEADS])
                scores = inner.sb("scores", [P, NB, 4])
                project_nodes(sh, "p3", stats, a["L1_ffn_W_gat"], 16 + 2 * HEADS,
                              att=(a["L1_ffn_att_src"], a["L1_ffn_att_dst"]),
                              table=table2, table_cols=16 + HEADS, keep=keep, keep_from=0)
                table_maximum(sh, "m1", keep, 16, gmax)
                store_adst(sh, "d1", keep, 16 + HEADS, adst2)
                free_edges_pass(sh, "q", a["fsrc_t"], a["fdst_t"], table2, adst2, gmax, keep, gather_done, 2 * rounds,
                                a["L1_ffn_b_gat"], a["L1_ffn_ln_gamma"], a["L1_ffn_ln_beta"], scores)
                route(sh, "r1", 4, scores, weights, pos, pos_get, expert_of)
                scatter_tokens(sh, "t1", stats, None, pos, xs)
            y_stored2 = [sh.lasting_sem(f"y1_stored{j}") for j in range(2)]
            experts(sh, "e1", 4, 512, a["L1_ffn_W1"], a["L1_ffn_b1"], a["L1_ffn_W2"], a["L1_ffn_b2"], expert_of, xs, ys,
                    y_stored2)
            combine(sh, "c1", weights, pos_get, ys, y_stored2, (16 * ((tiles_of(4) + 1) // 2),))
        store_out(sh, out)
        sh.layer.close()


def store_rows(sh, tag, stats, table):
    s_xn = sh.sem(f"{tag}_xn")
    s_out = [sh.sem(f"{tag}_out{u}") for u in range(U7)]
    with Scope(sh.nc) as sc:
        XR = sc.sb(f"{tag}_XR", [P, U7, D])
        block = sc.block()

        @block.vector
        def _(v):
            with v.Fori(0, NB // U7) as it:
                for u in range(U7):
                    i = it * U7 + u
                    v.wait_ge(s_out[u], it * 16)
                    v.tensor_scalar(XR[:, u, :], sh.X[:, bass.ds(i, 1), :].rearrange("p a d -> p (a d)"),
                                    stats[:, bass.ds(i, 1), 0:1].rearrange("p a b -> p (a b)"),
                                    stats[:, bass.ds(i, 1), 1:2].rearrange("p a b -> p (a b)"),
                                    ALU.subtract, ALU.mult).then_inc(s_xn, 1)

        @block.sync
        def _(sp):
            with sp.Fori(0, NB // U7) as it:
                for u in range(U7):
                    sp.wait_ge(s_xn, it * U7 + u + 1)
                    sp.dma_start(table[bass.ds((it * U7 + u) * P, P), :], XR[:, u, :]).then_inc(s_out[u], 16)
            for u in range(U7):
                sp.wait_ge(s_out[u], NB // U7 * 16)


def edge_columns(e, tiles, fill):
    import numpy as np
    full = np.full(tiles * P, fill, e.dtype)
    full[:e.shape[0]] = e
    return np.ascontiguousarray(full.reshape(tiles, P).T)


NAMES = ["x", "L0_gnn_W", "L0_gnn_att_src", "L0_gnn_att_dst", "L0_gnn_bias", "L0_ffn_Wr", "L0_ffn_br", "L0_ffn_ln_g",
         "L0_ffn_ln_b", "L0_ffn_W1", "L0_ffn_b1", "L0_ffn_W2", "L0_ffn_b2", "L1_gnn_b1", "L1_gnn_b2", "L1_ffn_W_gat",
         "L1_ffn_att_src", "L1_ffn_att_dst", "L1_ffn_b_gat", "L1_ffn_ln_gamma", "L1_ffn_ln_beta", "L1_ffn_W1",
         "L1_ffn_b1", "L1_ffn_W2", "L1_ffn_b2"]


def kernel(**inputs):
    import concourse.bacc as bacc
    import numpy as np
    from concourse.bass_utils import run_bass_kernel_spmd

    arrays = {n: np.ascontiguousarray(inputs[n]) for n in NAMES}
    arrays["L1_gnn_W1t"] = np.ascontiguousarray(np.asarray(inputs["L1_gnn_W1"]).T)
    arrays["L1_gnn_W2t"] = np.ascontiguousarray(np.asarray(inputs["L1_gnn_W2"]).T)
    arrays["src_t"] = edge_columns(np.asarray(inputs["src"]), NTE, 0)
    arrays["dst_t"] = edge_columns(np.asarray(inputs["dst"]), NTE, N)
    arrays["weight_t"] = edge_columns(np.asarray(inputs["edge_weight"]), NTE, 0)
    fe = np.asarray(inputs["L1_ffn_edge_index"])
    arrays["fsrc_t"] = edge_columns(fe[0], NTF, 0)
    arrays["fdst_t"] = edge_columns(fe[1], NTF, 0)

    nc = bacc.Bacc("TRN2", target_bir_lowering=False, num_devices=1)
    args = {n: nc.dram_tensor(f"in_{n}", v.shape, mybir.dt.from_np(v.dtype), kind="ExternalInput").ap()
            for n, v in arrays.items()}
    out = nc.dram_tensor("out_x", (N, D), F32, kind="ExternalOutput").ap()
    build(nc, args, out)
    r = run_bass_kernel_spmd(nc, [{f"in_{n}": v for n, v in arrays.items()}], core_ids=[0])
    return r.results[0]["out_x"]
```

```python
from contextlib import ExitStack

import concourse.bass as bass
from concourse import mybir

F32 = mybir.dt.float32
I32 = mybir.dt.int32
U32 = mybir.dt.uint32
ALU = mybir.AluOpType
ACT = mybir.ActivationFunctionType
AX = mybir.AxisListType
RMAX = bass.bass_isa.ReduceOp.max

P = 128
N = 6250
D = 256
NB = -(-N // P)
NP = NB * P
LAST = N - (NB - 1) * P
KC = D // P
U7 = 7
HEADS = 4
EPS = 1e-5
SLOPE = 0.2
BIG = 3e38

E_SORTED = 206250
GRP = 8
RINGS = 4
E_TILES = -(-E_SORTED // P)
NS = -(-(E_TILES + NB - 1) // (P)) * P
NTE = NS - (NB - 1)
SCH = NS // P
SG = NS // GRP
E_FREE = 131072
NTF = E_FREE // P
NGRF = NTF // GRP

TOP = 2


def tiles_of(experts):
    most = (TOP * N + experts * (P - 1)) // P
    return most + 1 - most % 2


NT_MAX = tiles_of(8)
ROWS = NT_MAX * P


class Shared:

    def __init__(self, nc, ctx):
        self.nc, self.ctx = nc, ctx
        self.layer, self.sems = ExitStack(), []

    def lasting_sem(self, name):
        return self.ctx.enter_context(self.nc.semaphore(name))

    def sem(self, name):
        self.sems.append(self.layer.enter_context(self.nc.semaphore(name)))
        return self.sems[-1]

    def end_layer(self):
        with self.nc.Block() as block:
            @block.gpsimd
            def _(pool):
                for sem in self.sems:
                    pool.sem_clear(sem)
        self.layer.close()
        self.layer, self.sems = ExitStack(), []

    def sb(self, name, shape, dt=F32):
        return self.ctx.enter_context(self.nc.sbuf_tensor(name, shape, dt))


class Scope:

    def __init__(self, nc):
        self.nc, self.ctx = nc, ExitStack()

    def __enter__(self):
        self.ctx.__enter__()
        return self

    def __exit__(self, *a):
        return self.ctx.__exit__(*a)

    def sb(self, name, shape, dt=F32):
        return self.ctx.enter_context(self.nc.sbuf_tensor(name, shape, dt))

    def ps(self, name, shape, dt=F32):
        return self.ctx.enter_context(self.nc.psum_tensor(name, shape, dt))

    def block(self):
        return self.ctx.enter_context(self.nc.Block())


def at_least(eng, sem, value):
    if not isinstance(value, int) or value > 0:
        eng.wait_ge(sem, value)


def every_round(eng):
    def run(body):
        body(0)
        with eng.Fori(1, NB // U7) as it:
            body(it)
    return run


class Chain:

    def __init__(self, eng, sem):
        self.eng, self.sem, self.n = eng, sem, 0

    def __call__(self, ins, sem=None):
        if sem is None:
            self.n += 1
            ins.then_inc(self.sem, 1)
            self.eng.wait_ge(self.sem, self.n)
        else:
            ins.then_inc(sem, 1)
            self.eng.wait_ge(sem, 1)


def bcast_rows(vec, n=P):
    return vec.partition_broadcast(n)


def setup(sh, x, xs_rows):
    nc = sh.nc
    sh.X = sh.sb("X", [P, NB, D])
    sh.ident = sh.sb("ident", [P, P])
    sh.iota = sh.sb("iota", [P, P])
    sh.ones = sh.sb("ones", [P, P])
    sh.tri = sh.sb("tri", [P, P])
    sh.valid = sh.sb("valid", [P, NB])
    s_x, s_cst, sh.rows_zeroed, s_pre = sh.sem("x_loaded"), sh.sem("constants"), sh.lasting_sem("rows_zeroed"), sh.sem("memsets")
    with Scope(nc) as sc:
        zero = sc.sb("zero", [P, 3, D])
        block = sc.block()

        @block.gpsimd
        def _(pool):
            pool.memset(sh.X[:, NB - 1, :], 0.0).then_inc(s_pre, 1)
            pool.memset(zero[:, :, :], 0.0).then_inc(s_pre, 1)
            pool.memset(sh.ident[:, :], 0.0).then_inc(s_pre, 1)
            pool.memset(sh.ones[:, :], 1.0).then_inc(s_pre, 1)
            pool.memset(sh.valid[:, :], 1.0).then_inc(s_pre, 1)
            pool.iota(sh.iota[:, :], [[1, P]], base=0, channel_multiplier=0,
                      allow_small_or_imprecise_dtypes=True).then_inc(s_cst, 1)
            pool.wait_ge(s_pre, 5)
            pool.affine_select(out=sh.ident[:, :], in_=sh.ident[:, :], compare_op=ALU.not_equal, fill=1.0,
                               base=0, pattern=[[-1, P]], channel_multiplier=1).then_inc(s_cst, 1)
            pool.affine_select(out=sh.tri[:, :], in_=sh.ones[:, :], compare_op=ALU.is_gt, fill=0.0,
                               base=0, pattern=[[1, P]], channel_multiplier=-1).then_inc(s_cst, 1)
            pool.affine_select(out=sh.valid[:, :], in_=sh.valid[:, :], compare_op=ALU.is_ge, fill=0.0,
                               base=N - 1, pattern=[[-P, NB]], channel_multiplier=-1).then_inc(s_cst, 1)

        @block.sync
        def _(sp):
            full = x[0:(NB - 1) * P, :].rearrange("(i p) d -> p i d", p=P)
            for c in range(6):
                sp.dma_start(sh.X[:, 8 * c:8 * c + 8, :], full[:, 8 * c:8 * c + 8, :]).then_inc(s_x, 16)
            sp.wait_ge(s_pre, 1)
            sp.dma_start(sh.X[0:LAST, NB - 1, :], x[(NB - 1) * P:N, :]).then_inc(s_x, 16)
            sp.wait_ge(s_pre, 2)
            rows = xs_rows[0:ROWS, :].rearrange("(a p) d -> p a d", p=P)
            for a in range(NT_MAX // 3):
                sp.dma_start(rows[:, 3 * a:3 * a + 3, :], zero[:, :, :]).then_inc(sh.rows_zeroed, 16)
            sp.wait_ge(s_x, 7 * 16)
            sp.wait_ge(sh.rows_zeroed, NT_MAX // 3 * 16)


def layer_norm_stats(sh, tag, mean_rstd):
    nc = sh.nc
    s_st, s_ag, s_sq, s_ve, s_r = (sh.sem(f"{tag}_{n}") for n in ("bn_stats", "bn_aggr", "sqrt", "eps", "rstd"))
    with Scope(nc) as sc:
        st = sc.sb(f"{tag}_st", [P, 8, 6])
        block = sc.block()

        @block.vector
        def _(v):
            for i in range(NB):
                if i >= 8:
                    v.wait_ge(s_ag, i - 7)
                v.bn_stats(st[:, i % 8, :], sh.X[:, i, :]).then_inc(s_st, 1)
                if i >= 4:
                    at_least(v, s_st, i - 3)
                    v.bn_aggr(mean_rstd[:, i - 4, :], st[:, (i - 4) % 8, :]).then_inc(s_ag, 1)
            for i in range(NB - 4, NB):
                v.wait_ge(s_st, i + 1)
                v.bn_aggr(mean_rstd[:, i, :], st[:, i % 8, :]).then_inc(s_ag, 1)
            v.wait_ge(s_ag, NB)
            v.tensor_scalar(mean_rstd[:, :, 1], mean_rstd[:, :, 1], EPS, None, ALU.add).then_inc(s_ve, 1)
            v.wait_ge(s_sq, 1)
            v.reciprocal(mean_rstd[:, :, 1], mean_rstd[:, :, 1]).then_inc(s_r, 1)
            v.wait_ge(s_r, 1)

        @block.scalar
        def _(a):
            a.wait_ge(s_ve, 1)
            a.activation(mean_rstd[:, :, 1], mean_rstd[:, :, 1], ACT.Sqrt).then_inc(s_sq, 1)


def project_nodes(sh, tag, stats, weight, ncols, att=None, table=None, table_cols=0, keep=None, keep_from=0,
                  stats2=None, zero=None):
    nc = sh.nc
    wc = weight.shape[1]
    per = wc // HEADS
    s = {n: sh.sem(f"{tag}_{n}") for n in ("w", "att", "fold", "xn", "xrfree", "tr", "xt", "mm", "ev", "kept", "st", "st_seen", "ag", "agc")}
    s_tab = [sh.sem(f"{tag}_tab{u}") for u in range(U7)] if table is not None else None
    with Scope(nc) as sc:
        W = sc.sb(f"{tag}_W", [P, KC, ncols])
        XR = sc.sb(f"{tag}_XR", [P, U7, D])
        XT = sc.sb(f"{tag}_XT", [P, 2, KC, P])
        OUT = sc.sb(f"{tag}_OUT", [P, U7, table_cols]) if table is not None else None
        ATT = sc.sb(f"{tag}_ATT", [P, 2, wc]) if att else None
        FT = sc.sb(f"{tag}_FT", [P, KC, 2, wc]) if att else None
        ST = sc.sb(f"{tag}_ST", [P, U7, 6]) if stats2 is not None else None
        AG = sc.sb(f"{tag}_AG", [P, U7, 2]) if stats2 is not None else None
        pT = [sc.ps(f"{tag}_pT{j}", [P, KC, P]) for j in range(2)]
        pO = [sc.ps(f"{tag}_pO{j}", [P, ncols]) for j in range(4)]
        block = sc.block()

        if zero is not None:
            @block.gpsimd
            def _(pool):
                zero_blocks(pool, zero)

        @block.sync
        def _(sp):
            sp.dma_start(W[:, :, 0:wc], weight.rearrange("(c k) n -> k c n", k=P)).then_inc(s["w"], 16)
            if att:
                for a in range(2):
                    sp.dma_start(ATT[:, a, :], bcast_rows(att[a].rearrange("h c -> (h c)"))).then_inc(s["att"], 16)
            if table is not None:
                @every_round(sp)
                def _(it):
                    for u in range(U7):
                        at_least(sp, s["ev"], it * U7 + u + 1)
                        sp.dma_start(table[bass.ds((it * U7 + u) * P, P), :], OUT[:, u, :]).then_inc(s_tab[u], 16)
                for u in range(U7):
                    sp.wait_ge(s_tab[u], 16 * (NB // U7))

        @block.vector
        def _(v):
            v.wait_ge(s["w"], 16)
            if att:
                v.wait_ge(s["att"], 32)
                for c in range(KC):
                    for a in range(2):
                        v.tensor_tensor(FT[:, c, a, :], W[:, c, 0:wc], ATT[:, a, :], ALU.mult).then_inc(s["fold"], 1)
                v.wait_ge(s["fold"], 2 * KC)
                for c in range(KC):
                    for a in range(2):
                        v.tensor_reduce(W[:, c, wc + a * HEADS:wc + (a + 1) * HEADS],
                                        FT[:, c, a, :].rearrange("p (h q) -> p h q", q=per),
                                        AX.X, ALU.add).then_inc(s["fold"], 1)
            @every_round(v)
            def _(it):
                for u in range(U7):
                    i = it * U7 + u
                    at_least(v, s["tr"], it * U7)
                    v.tensor_scalar(XR[:, u, :], sh.X[:, bass.ds(i, 1), :].rearrange("p a d -> p (a d)"),
                                    stats[:, bass.ds(i, 1), 0:1].rearrange("p a b -> p (a b)"),
                                    stats[:, bass.ds(i, 1), 1:2].rearrange("p a b -> p (a b)"),
                                    ALU.subtract, ALU.mult).then_inc(s["xn"], 1)
                if stats2 is not None:
                    at_least(v, s["agc"], it)
                    for u in range(U7):
                        at_least(v, s["xn"], it * U7 + u + 1)
                        v.bn_stats(ST[:, u, :], XR[:, u, :]).then_inc(s["st"], 1)
                    at_least(v, s["st"], (it + 1) * U7)
                    v.sem_inc(s["st_seen"], 1)
                    for u in range(U7):
                        v.bn_aggr(AG[:, u, :], ST[:, u, :]).then_inc(s["ag"], 1)
                    at_least(v, s["ag"], (it + 1) * U7)
                    v.tensor_copy(stats2[:, bass.ds(it * U7, U7), :], AG[:, :, :]).then_inc(s["agc"], 1)
                for u in range(U7):
                    i = it * U7 + u
                    v.wait_ge(s["mm"], i + 1)
                    if table is not None:
                        at_least(v, s_tab[u], it * 16)
                        v.tensor_copy(OUT[:, u, :], pO[u % 4][:, 0:table_cols]).then_inc(s["ev"], 1)
                    if keep is not None:
                        v.tensor_copy(keep[:, bass.ds(i, 1), :].rearrange("p a b -> p (a b)"),
                                      pO[u % 4][:, keep_from:ncols]).then_inc(s["kept"], 1)

        @block.scalar
        def _(a):
            @every_round(a)
            def _(it):
                for u in range(U7):
                    i = it * U7 + u
                    a.wait_ge(s["tr"], i + 1)
                    if u >= 2:
                        at_least(a, s["mm"], i - 1)
                    else:
                        at_least(a, s["mm"], it * U7)
                    a.activation(XT[:, u % 2, :, :], pT[u % 2][:, :, :], ACT.Copy).then_inc(s["xt"], 1)

        @block.tensor
        def _(pe):
            def turn(it, u):
                at_least(pe, s["xn"], it * U7 + u + 1)
                if u >= 2:
                    at_least(pe, s["xt"], it * U7 + u - 1)
                else:
                    at_least(pe, s["xt"], it * U7)
                for c in range(KC):
                    m = pe.transpose(pT[u % 2][:, c, :], XR[:, u, c * P:(c + 1) * P], sh.ident[:, :])
                m.then_inc(s["tr"], 1)

            def product(it, u):
                i = it * U7 + u
                pe.wait_ge(s["xt"], i + 1)
                for done, used in (("ev", table), ("kept", keep)):
                    if used is not None:
                        at_least(pe, s[done], i - 3 if u >= 4 else it * U7)
                for c in range(KC):
                    m = pe.matmul(pO[u % 4][:, :], XT[:, u % 2, c, :], W[:, c, :], start=(c == 0), stop=(c == KC - 1))
                m.then_inc(s["mm"], 1)

            pe.wait_ge(s["fold"] if att else s["w"], 4 * KC if att else 16)
            @every_round(pe)
            def _(it):
                turn(it, 0)
                for u in range(U7):
                    if u + 1 < U7:
                        turn(it, u + 1)
                    product(it, u)


def load_registers(eng, regs, row, at):
    eng.reg_load(regs, row[0:1, bass.ds(at, len(regs))])
    return [eng.snap(r, min_val=0, max_val=NB - 1) for r in regs]


def plan_steps(sh, first_dst, edges, planned, planned_block):
    nc = sh.nc
    s = {n: sh.sem(f"plan_{n}") for n in ("first", "iota", "op", "start", "sums", "tile", "float", "turned", "out",
                                          "stored")}
    NA = 3
    BK = 4
    NBK = -(-SCH // BK)
    s_got = [sh.lasting_sem(f"plan_rows{j}") for j in range(NBK)]
    HB = NS // 4
    with Scope(nc) as sc:
        F = sc.sb("plan_F", [P, NTE], I32)
        FF = sc.sb("plan_FF", [P, NTE])
        PI = sc.sb("plan_PI", [P, 1])
        ROW = sc.sb("plan_ROW", [P, NS])
        COL = sc.sb("plan_COL", [P, SCH])
        START = sc.sb("plan_START", [P, 1])
        DIAG = sc.sb("plan_DIAG", [P, P])
        GE = sc.sb("plan_GE", [P, NS])
        TF = sc.sb("plan_TF", [P, SCH])
        T = sc.sb("plan_T", [P, SCH], I32)
        BF = sc.sb("plan_BF", [P, NS])
        BI = sc.sb("plan_BI", [P, NS], I32)
        RAW = sc.sb("plan_RAW", [P, NA, SCH, P], I32)
        RF = sc.sb("plan_RF", [P, 2, SCH, P])
        OUT = sc.sb("plan_OUT", [P, 2, NS])
        OSRC = sc.sb("plan_OSRC", [P, NS], I32)
        pJ = sc.ps("plan_pJ", [P, P])
        pB = sc.ps("plan_pB", [P, 4, 512])
        pT = [sc.ps(f"plan_pT{j}", [P, BK * P]) for j in range(2)]
        block = sc.block()

        @block.sync
        def _(sp):
            sp.dma_start(F[:, :], bcast_rows(first_dst[0, :])).then_inc(s["first"], 16)
            sp.wait_ge(s["out"], NA * NBK)
            for a, o in enumerate((OSRC[:, :], OUT[:, 0, :], OUT[:, 1, :])):
                sp.dma_start(planned[a], o).then_inc(s["stored"], 16)
            sp.dma_start(planned_block, BI[0:1, :]).then_inc(s["stored"], 16)
            sp.wait_ge(s["stored"], 16 * (NA + 1))

        @block.gpsimd
        def _(pool):
            for out, pattern, mult in ((PI, [[0, 1]], 1), (ROW, [[1, NS]], 0), (COL, [[P, SCH]], 1)):
                pool.iota(out[:, :], pattern, base=0, channel_multiplier=mult,
                          allow_small_or_imprecise_dtypes=True).then_inc(s["iota"], 1)
            pool.wait_ge(s["tile"], 1)
            for c in range(SCH):
                for a in range(NA):
                    rows = RAW[:, a, c, :] if a < 2 else RAW[:, a, c, :].bitcast(F32)
                    pool.indirect_dma_start(rows, None, edges[a], bass.IndirectOffsetOnAxis(
                        ap=T[:, c:c + 1].bitcast(U32), axis=0)).then_inc(s_got[c // BK], 16)

        @block.vector
        def _(v):
            then = Chain(v, s["op"])
            v.wait_ge(s["first"], 16)
            then(v.tensor_scalar(F[:, :], F[:, :], 7, None, ALU.logical_shift_right))
            then(v.tensor_copy(FF[:, :], F[:, :]))
            v.wait_ge(s["iota"], 3)
            then(v.tensor_scalar(FF[:, :], FF[:, :], PI[:, 0:1], None, ALU.is_lt))
            then(v.tensor_reduce(START[:, :], FF[:, :], AX.X, ALU.add))
            then(v.scalar_tensor_tensor(START[:, :], START[:, :], -1.0, PI[:, :], ALU.add, ALU.add))
            then(v.tensor_scalar(DIAG[:, :], sh.ident[:, :], START[:, 0:1], None, ALU.mult))
            then(v.tensor_scalar(GE[:, :], ROW[:, :], START[:, 0:1], None, ALU.is_ge), s["start"])
            v.wait_ge(s["sums"], 1)
            hit = RF[:, 0].rearrange("p c m -> p (c m)").rearrange("p (c m) -> p c m", m=P)
            then(v.tensor_tensor(hit, COL[:, :].unsqueeze(2).broadcast_to([P, SCH, P]),
                                 pJ[:, :].unsqueeze(1).broadcast_to([P, SCH, P]), ALU.is_ge))
            then(v.tensor_reduce(TF[:, :], hit, AX.X, ALU.add))
            then(v.scalar_tensor_tensor(TF[:, :], TF[:, :], -1.0, COL[:, :], ALU.mult, ALU.add))
            then(v.tensor_scalar(T[:, :], TF[:, :], 1.0, None, ALU.add), s["tile"])
            flat = pB[:, :, 0:HB]
            then(v.tensor_scalar(BI[:, :].rearrange("p (a b) -> p a b", a=4), flat, -1.0, None, ALU.add))
            then(v.tensor_scalar(BF[:, :].rearrange("p (a b) -> p a b", a=4), flat, -1.0, None, ALU.add))
            for bk in range(NBK):
                c0, c1 = bk * BK, min(SCH, bk * BK + BK)
                cols = slice(c0 * P, c1 * P)
                v.wait_ge(s_got[bk], 16 * NA * (c1 - c0))
                for a in range(2):
                    v.tensor_copy(RF[:, a, c0:c1, :], RAW[:, a, c0:c1, :]).then_inc(s["float"], 1)
                for a in range(NA):
                    v.wait_ge(s["turned"], bk * NA + a + 1)
                    out = pT[(bk * NA + a) % 2][:, 0:(c1 - c0) * P]
                    if a == 0:
                        v.tensor_copy(OSRC[:, cols], out).then_inc(s["out"], 1)
                    elif a == 1:
                        v.scalar_tensor_tensor(OUT[:, 0, cols], BF[:, cols], -float(P), out, ALU.mult,
                                               ALU.add).then_inc(s["out"], 1)
                    else:
                        v.tensor_copy(OUT[:, 1, cols], out).then_inc(s["out"], 1)

        @block.tensor
        def _(pe):
            pe.wait_ge(s["start"], 1)
            pe.matmul(pJ[:, :], sh.ones[:, :], DIAG[:, :], start=True, stop=True)
            for q in range(4):
                m = pe.matmul(pB[:, q, 0:HB], sh.ones[:, :], GE[:, q * HB:(q + 1) * HB], start=True, stop=True)
            m.then_inc(s["sums"], 1)
            for bk in range(NBK):
                for a in range(NA):
                    n = bk * NA + a
                    if n >= 2:
                        pe.wait_ge(s["out"], n - 1)
                    if a < 2:
                        pe.wait_ge(s["float"], bk * 2 + a + 1)
                    else:
                        pe.wait_ge(s_got[bk], 16 * NA * (min(SCH, (bk + 1) * BK) - bk * BK))
                    for c in range(bk * BK, min(SCH, bk * BK + BK)):
                        rows = RF[:, a, c, :] if a < 2 else RAW[:, a, c, :].bitcast(F32)
                        m = pe.transpose(pT[n % 2][:, (c - bk * BK) * P:(c - bk * BK + 1) * P], rows, sh.ident[:, :])
                    m.then_inc(s["turned"], 1)


def graph_pass(sh, tag, planned, planned_block, table, width, acc, acc_zeroed, gather_done, rounds0, keep=None, gmax=None):
    nc = sh.nc
    attend = keep is not None
    RND = SG // RINGS
    HG = GRP // 2
    BANKS = 4
    names = ["loaded", "staged", "slots_free", "onehot", "sum", "added"]
    if attend:
        names += ["turned", "copied", "ad", "z", "lr", "arg", "p", "gp"]
    s = {n: sh.sem(f"{tag}_{n}") for n in names}
    with Scope(nc) as sc:
        IDX = sc.sb(f"{tag}_IDX", [P, NS], I32)
        REL = sc.sb(f"{tag}_REL", [P, NS])
        BLK = sc.sb(f"{tag}_BLK", [1, NS], I32)
        WT = sc.sb(f"{tag}_WT", [P, NS]) if not attend else None
        STG = sc.sb(f"{tag}_STG", [P, RINGS, GRP], I32)
        G = sc.sb(f"{tag}_G", [P, RINGS, GRP, width])
        S = sc.sb(f"{tag}_S", [P, RINGS, GRP, P])
        pM = [sc.ps(f"{tag}_pM{j}", [P, 512]) for j in range(BANKS)]
        if attend:
            ST = sc.sb(f"{tag}_ST", [P, GRP, P])
            Z = sc.sb(f"{tag}_Z", [P, 2, 2, GRP, HEADS])
            L = sc.sb(f"{tag}_L", [P, 2, 2, GRP, HEADS])
            ARG = sc.sb(f"{tag}_ARG", [P, 2, GRP, HEADS])
            pT = sc.ps(f"{tag}_pT", [P, GRP, P])
            pA = sc.ps(f"{tag}_pA", [P, 2, GRP, HEADS])
        block = sc.block()
        n_loads = (3 if attend else 4) * 16

        def over_groups(eng, step):
            for r in range(RINGS):
                step(0, r)
            with eng.Fori(1, RND - 1) as it:
                for r in range(RINGS):
                    step(it, r)
            for r in range(RINGS):
                step(RND - 1, r)

        def last(rnd, r):
            return isinstance(rnd, int) and rnd * RINGS + r == SG - 1

        def first(rnd, r):
            return isinstance(rnd, int) and rnd * RINGS + r == 0

        def gathered(eng, rnd, r):
            eng.wait_ge(gather_done[r], (rnd + rounds0 + 1) * 16 * GRP)

        @block.sync
        def _(sp):
            sp.dma_start(IDX[:, :], planned[0]).then_inc(s["loaded"], 16)
            sp.dma_start(REL[:, :], planned[1]).then_inc(s["loaded"], 16)
            sp.dma_start(BLK[:, :], planned_block).then_inc(s["loaded"], 16)
            if not attend:
                sp.dma_start(WT[:, :], planned[2]).then_inc(s["loaded"], 16)

        @block.gpsimd
        def _(pool):
            pool.wait_ge(s["loaded"], n_loads)

            def stage(rnd, r):
                at_least(pool, gather_done[r], (rnd + rounds0) * 16 * GRP)
                pool.tensor_copy(STG[:, r, :], IDX[:, bass.ds((rnd * RINGS + r) * GRP, GRP)]).then_inc(s["staged"], 1)

            def gathers(rnd, r):
                k = rnd * RINGS + r
                pool.wait_ge(s["staged"], k + 1)
                at_least(pool, s["sum"], (k - RINGS + 1) * GRP)
                pool.sem_inc(s["slots_free"], 1)
                for u in range(GRP):
                    pool.indirect_dma_start(G[:, r, u, :], None, table, bass.IndirectOffsetOnAxis(
                        ap=STG[:, r, u:u + 1].bitcast(U32), axis=0)).then_inc(gather_done[r], 16)

            def step(rnd, r):
                if not last(rnd, r):
                    stage(rnd + (r + 1) // RINGS, (r + 1) % RINGS)
                gathers(rnd, r)

            stage(0, 0)
            over_groups(pool, step)

        @block.vector
        def _(v):
            v.wait_ge(s["loaded"], n_loads)
            v.wait_ge(*acc_zeroed)
            regs = [v.alloc_register(f"{tag}_v{u}") for u in range(GRP)]

            def onehot(rnd, r, u):
                j = (rnd * RINGS + r) * GRP + u
                rel = REL[:, bass.ds(j, 1)]
                if u == 0:
                    at_least(v, s["sum"], (rnd * RINGS + r - RINGS + 1) * GRP)
                if attend:
                    v.tensor_scalar(S[:, r, u, :], sh.iota[:, :], rel, None, ALU.is_equal).then_inc(s["onehot"], 1)
                else:
                    v.tensor_scalar(S[:, r, u, :], sh.iota[:, :], rel, WT[:, bass.ds(j, 1)],
                                    ALU.is_equal, ALU.mult).then_inc(s["onehot"], 1)

            def add(k, u, blk):
                j = k * GRP + u
                v.wait_ge(s["sum"], j + 1)
                at_least(v, s["added"], j)
                sums = acc[:, bass.ds(blk, 1), :].rearrange("p a d -> p (a d)")
                v.tensor_tensor(sums, pM[u % BANKS][:, 0:width], sums, ALU.add).then_inc(s["added"], 1)

            def after(rnd, r):
                return rnd + (r + 1) // RINGS, (r + 1) % RINGS

            def step_attend(rnd, r):
                k = rnd * RINGS + r
                par = r % 2
                before = not first(rnd, r)
                if before:
                    blk = load_registers(v, regs, BLK, (k - 1) * GRP)

                def next_onehots(us):
                    if not last(rnd, r):
                        for u in us:
                            onehot(*after(rnd, r), u)

                def add_before(u):
                    if before:
                        add(k - 1, u, blk[u])

                v.wait_ge(s["ad"], k + 1)
                gathered(v, rnd, r)
                v.tensor_tensor(Z[:, par, 0], G[:, r, :, D:D + HEADS], pA[:, par], ALU.add).then_inc(s["z"], 1)
                v.tensor_tensor(Z[:, par, 1], gmax[:, :].unsqueeze(1).broadcast_to([P, GRP, HEADS]), pA[:, par],
                                ALU.add).then_inc(s["z"], 1)
                next_onehots((0, 1))
                v.wait_ge(s["z"], k * 2 + 2)
                v.scalar_tensor_tensor(L[:, par].rearrange("p a u h -> p (a u h)"), Z[:, par].rearrange("p a u h -> p (a u h)"),
                                       SLOPE, Z[:, par].rearrange("p a u h -> p (a u h)"),
                                       ALU.mult, ALU.max).then_inc(s["lr"], 1)
                next_onehots((2, 3))
                v.wait_ge(s["lr"], k + 1)
                v.tensor_tensor(ARG[:, par], L[:, par, 0], L[:, par, 1], ALU.subtract).then_inc(s["arg"], 1)
                for u in range(HG):
                    add_before(u)
                    next_onehots((HG + u,))
                v.wait_ge(s["p"], k + 1)
                for q in range(HG):
                    rows = G[:, r, 2 * q:2 * q + 2, 0:D].rearrange("p u (h q) -> p u h q", h=HEADS)
                    fac = G[:, r, 2 * q:2 * q + 2, D:D + HEADS].unsqueeze(3).broadcast_to([P, 2, HEADS, D // HEADS])
                    v.tensor_tensor(rows, rows, fac, ALU.mult).then_inc(s["gp"], 1)
                    add_before(HG + q)

            def step_weighted(rnd, r):
                blk = load_registers(v, regs, BLK, (rnd * RINGS + r) * GRP)
                for u in range(GRP):
                    if not last(rnd, r):
                        onehot(*after(rnd, r), u)
                    add(rnd * RINGS + r, u, blk[u])

            for u in range(GRP):
                onehot(0, 0, u)
            if attend:
                over_groups(v, step_attend)
                blk = load_registers(v, regs, BLK, (SG - 1) * GRP)
                for u in range(GRP):
                    add(SG - 1, u, blk[u])
            else:
                over_groups(v, step_weighted)
            v.wait_ge(s["added"], NS)

        if attend:
            @block.scalar
            def _(a):
                def copy(k, hf):
                    a.wait_ge(s["turned"], 2 * k + hf + 1)
                    at_least(a, s["ad"], k)
                    sl = slice(hf * HG, (hf + 1) * HG)
                    a.activation(ST[:, sl, :], pT[:, sl, :], ACT.Copy).then_inc(s["copied"], 1)

                def step(rnd, r):
                    k = rnd * RINGS + r
                    if not last(rnd, r):
                        copy(k + 1, 0)
                    a.wait_ge(s["arg"], k + 1)
                    a.activation(G[:, r, :, D:D + HEADS], ARG[:, r % 2], ACT.Exp).then_inc(s["p"], 1)
                    if not last(rnd, r):
                        copy(k + 1, 1)

                copy(0, 0)
                copy(0, 1)
                over_groups(a, step)

        @block.tensor
        def _(pe):
            regs = [pe.alloc_register(f"{tag}_p{u}") for u in range(GRP)] if attend else None

            def transposes(k, r, hf):
                at_least(pe, s["copied"], 2 * k - 1 + hf)
                pe.wait_ge(s["onehot"], k * GRP + (hf + 1) * HG)
                for u in range(hf * HG, (hf + 1) * HG):
                    m = pe.transpose(pT[:, u, :], S[:, r, u, :], sh.ident[:, :])
                m.then_inc(s["turned"], 1)

            def spread(k, r):
                blk = load_registers(pe, regs, BLK, k * GRP)
                at_least(pe, s["z"], 2 * k - 2)
                for u in range(GRP):
                    if u % HG == 0:
                        pe.wait_ge(s["copied"], 2 * k + u // HG + 1)
                    nodes = keep[:, bass.ds(blk[u], 1), HEADS:2 * HEADS].rearrange("p a h -> p (a h)")
                    m = pe.matmul(pA[:, r % 2, u, :], ST[:, u, :], nodes, start=True, stop=True)
                m.then_inc(s["ad"], 1)

            def sums(k, r, us):
                for u in us:
                    j = k * GRP + u
                    if attend and u % 2 == 0:
                        pe.wait_ge(s["gp"], k * HG + u // 2 + 1)
                    if not attend and u == 0:
                        pe.wait_ge(s["onehot"], (k + 1) * GRP)
                    at_least(pe, s["added"], j + 1 - BANKS)
                    pe.matmul(pM[u % BANKS][:, 0:width], S[:, r, u, :], G[:, r, u, :], start=True,
                              stop=True).then_inc(s["sum"], 1)

            def step_attend(rnd, r):
                k = rnd * RINGS + r
                if not last(rnd, r):
                    transposes(k + 1, (r + 1) % RINGS, 0)
                if not first(rnd, r):
                    sums(k - 1, (r - 1) % RINGS, range(HG, GRP))
                if not last(rnd, r):
                    transposes(k + 1, (r + 1) % RINGS, 1)
                    spread(k + 1, (r + 1) % RINGS)
                sums(k, r, range(HG))

            def step_weighted(rnd, r):
                gathered(pe, rnd, r)
                sums(rnd * RINGS + r, r, range(GRP))

            pe.wait_ge(s["loaded"], n_loads)
            if attend:
                transposes(0, 0, 0)
                transposes(0, 0, 1)
                spread(0, 0)
                over_groups(pe, step_attend)
                sums(SG - 1, RINGS - 1, range(HG, GRP))
            else:
                over_groups(pe, step_weighted)


def table_maximum(sh, tag, keep, col, gmax):
    nc = sh.nc
    s_m, s_g = sh.sem(f"{tag}_max"), sh.sem(f"{tag}_allmax")
    with Scope(nc) as sc:
        M = sc.sb(f"{tag}_M", [P, HEADS])
        block = sc.block()

        @block.vector
        def _(v):
            v.tensor_reduce(M[:, :], keep[:, 0:NB - 1, col:col + HEADS].rearrange("p i h -> p h i"),
                            AX.X, ALU.max).then_inc(s_m, 1)
            v.wait_ge(s_m, 1)
            v.tensor_tensor(M[0:LAST, :], M[0:LAST, :], keep[0:LAST, NB - 1, col:col + HEADS], ALU.max).then_inc(s_m, 1)

        @block.gpsimd
        def _(pool):
            pool.wait_ge(s_m, 2)
            pool.partition_all_reduce(gmax[:, :], M[:, :], P, RMAX).then_inc(s_g, 1)
            pool.wait_ge(s_g, 1)


def store_adst(sh, tag, keep, col, adst):
    s_o = sh.sem(f"{tag}_stored")
    with Scope(sh.nc) as sc:
        block = sc.block()

        @block.sync
        def _(sp):
            sp.dma_start(adst.rearrange("(i p) h -> p i h", p=P), keep[:, :, col:col + HEADS]).then_inc(s_o, 16)
            sp.wait_ge(s_o, 16)


def self_factor(sh, v, a, s, keep, col, gmax, Z, PS):
    def on_vector():
        av, dv = keep[:, :, col:col + HEADS], keep[:, :, col + HEADS:col + 2 * HEADS]
        v.tensor_tensor(Z[:, 0], av, dv, ALU.add).then_inc(s, 1)
        v.tensor_tensor(Z[:, 1], gmax[:, :].unsqueeze(1).broadcast_to([P, NB, HEADS]), dv, ALU.add).then_inc(s, 1)
        v.wait_ge(s, 2)
        flat = Z[:, :, :, :].rearrange("p a i h -> p (a i h)")
        v.scalar_tensor_tensor(flat, flat, SLOPE, flat, ALU.mult, ALU.max).then_inc(s, 1)
        v.wait_ge(s, 3)
        v.tensor_tensor(PS[:, :, :], Z[:, 0], Z[:, 1], ALU.subtract).then_inc(s, 1)
    def on_scalar():
        a.wait_ge(s, 4)
        a.activation(PS[:, :, :], PS[:, :, :], ACT.Exp).then_inc(s, 1)
    return on_vector, on_scalar


def finish_attention(sh, tag, acc, table, keep, gmax, bias):
    nc = sh.nc
    s = {n: sh.sem(f"{tag}_{n}") for n in ("self", "bias", "op", "own")}
    s_h = [sh.sem(f"{tag}_h{j}") for j in range(2)]
    OPS = 4
    RND = NB // U7
    with Scope(nc) as sc:
        Z = sc.sb(f"{tag}_Z", [P, 2, NB, HEADS])
        PS = sc.sb(f"{tag}_PS", [P, NB, HEADS])
        B = sc.sb(f"{tag}_B", [P, D])
        H = sc.sb(f"{tag}_H", [P, 2, U7, D])
        block = sc.block()

        @block.sync
        def _(sp):
            sp.dma_start(B[:, :], bcast_rows(bias)).then_inc(s["bias"], 16)
            for it in range(RND):
                if it >= 2:
                    at_least(sp, s["own"], it - 1)
                sp.dma_start(H[:, it % 2], table[it * U7 * P:(it + 1) * U7 * P, 0:D].rearrange(
                    "(u p) d -> p u d", p=P)).then_inc(s_h[it % 2], 16)

        @block.scalar
        def _(a):
            self_factor(sh, None, a, s["self"], keep, 0, gmax, Z, PS)[1]()

        @block.vector
        def _(v):
            self_factor(sh, v, None, s["self"], keep, 0, gmax, Z, PS)[0]()
            v.wait_ge(s["self"], 5)
            v.wait_ge(s["bias"], 16)

            def heads(ap):
                return ap.rearrange("p u (h q) -> p u h q", h=HEADS)

            def spread(ap):
                return ap.unsqueeze(3).broadcast_to([P, U7, HEADS, D // HEADS])

            v.tensor_tensor(acc[:, :, D:D + HEADS], acc[:, :, D:D + HEADS], PS[:, :, :], ALU.add).then_inc(s["self"], 1)
            v.wait_ge(s["self"], 6)
            v.reciprocal(acc[:, :, D:D + HEADS], acc[:, :, D:D + HEADS]).then_inc(s["self"], 1)
            v.wait_ge(s["self"], 7)

            def stage(it, n):
                blk = slice(it * U7, it * U7 + U7)
                sums = acc[:, blk, 0:D]
                if n == 0:
                    at_least(v, s_h[it % 2], (it // 2 + 1) * 16)
                    h = H[:, it % 2]
                    v.tensor_tensor(heads(h), heads(h), spread(PS[:, blk, :]), ALU.mult).then_inc(s["op"], 1)
                elif n == 1:
                    v.tensor_tensor(sums, sums, H[:, it % 2], ALU.add).then_inc(s["own"], 1)
                elif n == 2:
                    at_least(v, s["own"], it + 1)
                    v.tensor_tensor(heads(sums), heads(sums), spread(acc[:, blk, D:D + HEADS]), ALU.mult).then_inc(s["op"], 1)
                elif n == 3:
                    v.tensor_tensor(sums, sums, B[:, :].unsqueeze(1).broadcast_to([P, U7, D]), ALU.add).then_inc(s["op"], 1)
                else:
                    v.scalar_tensor_tensor(sh.X[:, blk, :], sums, 0.0, sh.X[:, blk, :], ALU.max, ALU.add).then_inc(s["op"], 1)

            for it in range(RND):
                for n in range(OPS + 1):
                    if n in (1, 3, 4):
                        at_least(v, s["op"], it * OPS + (1 if n == 1 else n - 1))
                    stage(it, n)
            v.wait_ge(s["op"], OPS * RND)


def finish_weighted(sh, tag, acc, stats, w1t, w2t, b1, b2):
    nc = sh.nc
    s = {n: sh.sem(f"{tag}_{n}") for n in ("w", "bias", "xn", "tr", "xt", "side", "mm", "op", "norm")}
    OPS = 8
    with Scope(nc) as sc:
        W = sc.sb(f"{tag}_W", [P, 2, KC, D])
        B = sc.sb(f"{tag}_B", [P, 2, D])
        XR = sc.sb(f"{tag}_XR", [P, U7, D])
        SR = sc.sb(f"{tag}_SR", [P, U7, D])
        XT = sc.sb(f"{tag}_XT", [P, 2, 2, KC, P])
        O = sc.sb(f"{tag}_O", [P, U7, D])
        Q = sc.sb(f"{tag}_Q", [P, U7, D])
        NR = sc.sb(f"{tag}_NR", [P, U7])
        pO = sc.ps(f"{tag}_pO", [P, 4, 2, D])
        pT = [sc.ps(f"{tag}_pT{j}", [P, 2, KC, P]) for j in range(2)]
        block = sc.block()

        def out_of(u):
            return pO[:, u // 2, u % 2, :]

        @block.sync
        def _(sp):
            for j, w in enumerate((w1t, w2t)):
                sp.dma_start(W[:, j], w.rearrange("(c k) n -> k c n", k=P)).then_inc(s["w"], 16)
            for j, b in enumerate((b1, b2)):
                sp.dma_start(B[:, j, :], bcast_rows(b)).then_inc(s["bias"], 16)

        @block.scalar
        def _(a):
            @every_round(a)
            def _(it):
                for u in range(U7):
                    at_least(a, s["tr"], it * U7 + u + 1)
                    if u >= 2:
                        at_least(a, s["mm"], it * U7 + u - 1)
                    else:
                        at_least(a, s["mm"], it * U7)
                    a.activation(XT[:, u % 2], pT[u % 2][:, :, :, :], ACT.Copy).then_inc(s["xt"], 1)
                at_least(a, s["op"], it * OPS + 4)
                a.activation(NR[:, :], NR[:, :], ACT.Sqrt).then_inc(s["norm"], 1)

        @block.tensor
        def _(pe):
            def turn(it, u):
                at_least(pe, s["xn"], it * U7 + u + 1)
                at_least(pe, s["xt"], it * U7 + (u - 1 if u >= 2 else 0))
                at_least(pe, s["side"], it * U7 + u + 1)
                for j, rows in enumerate((XR, SR)):
                    for c in range(KC):
                        m = pe.transpose(pT[u % 2][:, j, c, :], rows[:, u, c * P:(c + 1) * P], sh.ident[:, :])
                m.then_inc(s["tr"], 1)

            pe.wait_ge(s["w"], 32)
            @every_round(pe)
            def _(it):
                at_least(pe, s["op"], it * OPS)
                turn(it, 0)
                for u in range(U7):
                    if u + 1 < U7:
                        turn(it, u + 1)
                    at_least(pe, s["xt"], it * U7 + u + 1)
                    for j in range(2):
                        for c in range(KC):
                            m = pe.matmul(out_of(u), XT[:, u % 2, j, c, :], W[:, j, c, :],
                                          start=(j == 0 and c == 0), stop=(j == 1 and c == KC - 1))
                    m.then_inc(s["mm"], 1)

        @block.vector
        def _(v):
            v.wait_ge(s["bias"], 32)
            v.tensor_tensor(B[:, 0, :], B[:, 0, :], B[:, 1, :], ALU.add).then_inc(s["bias"], 1)
            v.wait_ge(s["bias"], 33)
            @every_round(v)
            def _(it):
                blk = bass.ds(it * U7, U7)
                at_least(v, s["tr"], it * U7)
                for u in range(U7):
                    i = it * U7 + u
                    v.tensor_scalar(XR[:, u, :], sh.X[:, bass.ds(i, 1), :].rearrange("p a d -> p (a d)"),
                                    stats[:, bass.ds(i, 1), 0:1].rearrange("p a b -> p (a b)"),
                                    stats[:, bass.ds(i, 1), 1:2].rearrange("p a b -> p (a b)"),
                                    ALU.subtract, ALU.mult).then_inc(s["xn"], 1)
                for u in range(U7):
                    at_least(v, s["xn"], it * U7 + u + 1)
                    v.scalar_tensor_tensor(SR[:, u, :], XR[:, u, :], 1.0,
                                           acc[:, bass.ds(it * U7 + u, 1), :].rearrange("p a d -> p (a d)"),
                                           ALU.add, ALU.mult).then_inc(s["side"], 1)
                at_least(v, s["mm"], it * U7 + U7)
                pall = pO[:, :, :, :].rearrange("p a b d -> p (a b) d")[:, 0:U7, :]
                v.tensor_tensor(O[:, :, :], pall, B[:, 0, :].unsqueeze(1).broadcast_to([P, U7, D]), ALU.add).then_inc(s["op"], 1)
                at_least(v, s["op"], it * OPS + 1)
                v.scalar_tensor_tensor(O[:, :, :], O[:, :, :], SLOPE, O[:, :, :], ALU.mult, ALU.max).then_inc(s["op"], 1)
                at_least(v, s["op"], it * OPS + 2)
                v.tensor_tensor(Q[:, :, :], O[:, :, :], O[:, :, :], ALU.mult).then_inc(s["op"], 1)
                at_least(v, s["op"], it * OPS + 3)
                v.tensor_reduce(NR[:, :], Q[:, :, :], AX.X, ALU.add).then_inc(s["op"], 1)
                at_least(v, s["norm"], it + 1)
                v.tensor_scalar(NR[:, :], NR[:, :], 1e-12, None, ALU.max).then_inc(s["op"], 1)
                at_least(v, s["op"], it * OPS + 5)
                v.reciprocal(NR[:, :], NR[:, :]).then_inc(s["op"], 1)
                at_least(v, s["op"], it * OPS + 6)
                v.tensor_tensor(O[:, :, :], O[:, :, :], NR[:, :].unsqueeze(2).broadcast_to([P, U7, D]), ALU.mult).then_inc(s["op"], 1)
                at_least(v, s["op"], it * OPS + 7)
                v.tensor_tensor(sh.X[:, blk, :], sh.X[:, blk, :], O[:, :, :], ALU.add).then_inc(s["op"], 1)
            v.wait_ge(s["op"], OPS * (NB // U7))


def free_edges_pass(sh, tag, src_t, dst_t, table, adst, gmax, keep, gather_done, rounds0, b_gat, gamma, beta, scores):
    nc = sh.nc
    EX = 4
    VC = HEADS * EX + HEADS
    NA = 25
    RND = NGRF // RINGS
    MVR = 4
    TWO = 2
    s = {n: sh.sem(f"{tag}_{n}") for n in ("loaded", "idx", "staged", "slots_free", "lo", "hi", "ad", "z", "arg", "p", "val", "mv",
                                           "mm", "self", "par", "fin", "var", "sq")}
    with Scope(nc) as sc:
        SRC = sc.sb(f"{tag}_SRC", [P, NTF], I32)
        DST = sc.sb(f"{tag}_DST", [P, NTF], I32)
        DC = sc.sb(f"{tag}_DC", [P, NTF], I32)
        TI = sc.sb(f"{tag}_TI", [P, NTF], I32)
        LO = sc.sb(f"{tag}_LO", [P, NTF])
        HI = sc.sb(f"{tag}_HI", [P, NTF])
        STG = sc.sb(f"{tag}_STG", [P, RINGS, 2, GRP], I32)
        G = sc.sb(f"{tag}_G", [P, RINGS, GRP, VC])
        A = sc.sb(f"{tag}_A", [P, RINGS, GRP, HEADS])
        OL = sc.sb(f"{tag}_OL", [P, 2, GRP, P])
        OH = sc.sb(f"{tag}_OH", [P, 2, GRP, NB])
        Z = sc.sb(f"{tag}_Z", [P, 2, 2, GRP, HEADS])
        ARG = sc.sb(f"{tag}_ARG", [P, 2, GRP, HEADS])
        V = sc.sb(f"{tag}_V", [P, 2, GRP, VC])
        MV = sc.sb(f"{tag}_MV", [P, MVR, NB, VC])
        ZS = sc.sb(f"{tag}_ZS", [P, 2, NB, HEADS])
        PS = sc.sb(f"{tag}_PS", [P, NB, HEADS])
        R = sc.sb(f"{tag}_R", [P, NB, HEADS * EX])
        R2 = sc.sb(f"{tag}_R2", [P, NB, HEADS * EX])
        DN = sc.sb(f"{tag}_DN", [P, NB, HEADS])
        MU = sc.sb(f"{tag}_MU", [P, NB])
        VR = sc.sb(f"{tag}_VR", [P, NB])
        PAR = sc.sb(f"{tag}_PAR", [P, 3, HEADS * EX])
        pS = [sc.ps(f"{tag}_pS{j}", [P, 512]) for j in range(2)]
        block = sc.block()
        parts = [(0, NA), (NA, NB - NA)]

        def over_groups(eng, step):
            for r in range(RINGS):
                step(0, r)
            with eng.Fori(1, RND - 1) as it:
                for r in range(RINGS):
                    step(it, r)
            for r in range(RINGS):
                step(RND - 1, r)

        @block.sync
        def _(sp):
            sp.dma_start(SRC[:, :], src_t).then_inc(s["loaded"], 16)
            sp.dma_start(DST[:, :], dst_t).then_inc(s["loaded"], 16)
            for j, w in enumerate((b_gat, gamma, beta)):
                sp.dma_start(PAR[:, j, :], bcast_rows(w)).then_inc(s["par"], 16)

        @block.gpsimd
        def _(pool):
            pool.wait_ge(s["idx"], 6)

            def stage(rnd, r):
                k = rnd * RINGS + r
                at_least(pool, gather_done[r], (rounds0 + rnd * TWO) * 16 * GRP)
                at_least(pool, s["val"], 2 * (k - RINGS + 1))
                pool.tensor_copy(STG[:, r, 0, :], SRC[:, bass.ds(k * GRP, GRP)]).then_inc(s["staged"], 1)
                pool.tensor_copy(STG[:, r, 1, :], DC[:, bass.ds(k * GRP, GRP)]).then_inc(s["staged"], 1)

            def gathers(rnd, r):
                k = rnd * RINGS + r
                pool.wait_ge(s["staged"], 2 * k + 2)
                pool.sem_inc(s["slots_free"], 1)
                for u in range(GRP):
                    pool.indirect_dma_start(G[:, r, u, :], None, table, bass.IndirectOffsetOnAxis(
                        ap=STG[:, r, 0, u:u + 1].bitcast(U32), axis=0)).then_inc(gather_done[r], 16)
                    pool.indirect_dma_start(A[:, r, u, :], None, adst, bass.IndirectOffsetOnAxis(
                        ap=STG[:, r, 1, u:u + 1].bitcast(U32), axis=0)).then_inc(gather_done[r], 16)

            def step(rnd, r):
                if not (isinstance(rnd, int) and rnd * RINGS + r == NGRF - 1):
                    stage(rnd + (r + 1) // RINGS, (r + 1) % RINGS)
                gathers(rnd, r)

            stage(0, 0)
            over_groups(pool, step)

        @block.vector
        def _(v):
            v.wait_ge(s["loaded"], 32)
            v.tensor_scalar(SRC[:, :], SRC[:, :], N - 1, None, ALU.min).then_inc(s["idx"], 1)
            v.tensor_scalar(DC[:, :], DST[:, :], N - 1, None, ALU.min).then_inc(s["idx"], 1)
            v.tensor_scalar(TI[:, :], DST[:, :], P - 1, None, ALU.bitwise_and).then_inc(s["idx"], 1)
            v.wait_ge(s["idx"], 3)
            v.tensor_copy(LO[:, :], TI[:, :]).then_inc(s["idx"], 1)
            v.wait_ge(s["idx"], 4)
            v.tensor_scalar(TI[:, :], DST[:, :], 7, None, ALU.logical_shift_right).then_inc(s["idx"], 1)
            v.wait_ge(s["idx"], 5)
            v.tensor_copy(HI[:, :], TI[:, :]).then_inc(s["idx"], 1)
            v.wait_ge(s["idx"], 6)

            def step(rnd, r):
                k = rnd * RINGS + r
                par = r % 2
                at_least(v, s["mm"], (k - 1) * GRP)
                for u in range(GRP):
                    v.tensor_scalar(OL[:, par, u, :], sh.iota[:, :], LO[:, bass.ds(k * GRP + u, 1)], None,
                                    ALU.is_equal).then_inc(s["lo"], 1)
                v.tensor_tensor(OH[:, par], sh.iota[:, 0:NB].unsqueeze(1).broadcast_to([P, GRP, NB]),
                                HI[:, bass.ds(k * GRP, GRP)].unsqueeze(2).broadcast_to([P, GRP, NB]),
                                ALU.is_equal).then_inc(s["hi"], 1)
                v.wait_ge(gather_done[r], (rounds0 + (rnd + 1) * TWO) * 16 * GRP)
                v.tensor_tensor(Z[:, par, 0], G[:, r, :, EX * HEADS:VC], A[:, r, :, :], ALU.add).then_inc(s["z"], 1)
                v.tensor_tensor(Z[:, par, 1], gmax[:, :].unsqueeze(1).broadcast_to([P, GRP, HEADS]), A[:, r, :, :],
                                ALU.add).then_inc(s["z"], 1)
                v.wait_ge(s["z"], k * 3 + 2)
                zf = Z[:, par].rearrange("p a u h -> p (a u h)")
                v.scalar_tensor_tensor(zf, zf, SLOPE, zf, ALU.mult, ALU.max).then_inc(s["z"], 1)
                v.wait_ge(s["z"], k * 3 + 3)
                v.tensor_tensor(ARG[:, par], Z[:, par, 0], Z[:, par, 1], ALU.subtract).then_inc(s["arg"], 1)
                v.wait_ge(s["p"], k + 1)
                v.tensor_tensor(V[:, par, :, 0:EX * HEADS].rearrange("p u (h q) -> p u h q", h=HEADS),
                                G[:, r, :, 0:EX * HEADS].rearrange("p u (h q) -> p u h q", h=HEADS),
                                ARG[:, par].unsqueeze(3).broadcast_to([P, GRP, HEADS, EX]), ALU.mult).then_inc(s["val"], 1)
                v.tensor_copy(V[:, par, :, EX * HEADS:VC], ARG[:, par]).then_inc(s["val"], 1)
                v.wait_ge(s["hi"], k + 1)
                v.wait_ge(s["val"], 2 * k + 2)
                for u in range(GRP):
                    at_least(v, s["mm"], k * GRP + u - MVR + 1)
                    v.tensor_tensor(MV[:, u % MVR], OH[:, par, u, :].unsqueeze(2).broadcast_to([P, NB, VC]),
                                    V[:, par, u, :].unsqueeze(1).broadcast_to([P, NB, VC]), ALU.mult).then_inc(s["mv"], 1)

            over_groups(v, step)

            self_factor(sh, v, None, s["self"], keep, EX * HEADS, gmax, ZS, PS)[0]()
            v.wait_ge(s["self"], 5)
            v.wait_ge(s["mm"], NTF)
            v.wait_ge(s["par"], 48)

            then = Chain(v, s["fin"])

            def heads(ap):
                return ap.rearrange("p i (h q) -> p i h q", h=HEADS)

            def all16(ap, j):
                return ap[:, j, :].unsqueeze(1).broadcast_to([P, NB, EX * HEADS])

            def per_head(ap, m=NB):
                return ap.unsqueeze(3).broadcast_to([P, m, HEADS, EX])

            then(v.tensor_tensor(heads(R[:, :, :]), heads(keep[:, :, 0:EX * HEADS]), per_head(PS[:, :, :]), ALU.mult))
            for j, (b0, m) in enumerate(parts):
                sums = pS[j][:, 0:m * VC].rearrange("p (i c) -> p i c", c=VC)
                then(v.tensor_tensor(DN[:, b0:b0 + m, :], PS[:, b0:b0 + m, :], sums[:, :, EX * HEADS:VC], ALU.add))
                then(v.tensor_tensor(R[:, b0:b0 + m, :], R[:, b0:b0 + m, :], sums[:, :, 0:EX * HEADS], ALU.add))
            then(v.reciprocal(DN[:, :, :], DN[:, :, :]))
            then(v.tensor_tensor(heads(R[:, :, :]), heads(R[:, :, :]), per_head(DN[:, :, :]), ALU.mult))
            then(v.tensor_tensor(R[:, :, :], R[:, :, :], all16(PAR, 0), ALU.add))
            then(v.tensor_reduce(MU[:, :], R[:, :, :], AX.X, ALU.add))
            then(v.tensor_scalar(MU[:, :], MU[:, :], 1.0 / (EX * HEADS), None, ALU.mult))
            wide = [P, NB, EX * HEADS]
            then(v.tensor_tensor(R[:, :, :], R[:, :, :], MU[:, :].unsqueeze(2).broadcast_to(wide), ALU.subtract))
            then(v.tensor_tensor(R2[:, :, :], R[:, :, :], R[:, :, :], ALU.mult))
            then(v.tensor_reduce(VR[:, :], R2[:, :, :], AX.X, ALU.add))
            then(v.tensor_scalar(VR[:, :], VR[:, :], 1.0 / (EX * HEADS), EPS, ALU.mult, ALU.add), s["var"])
            v.wait_ge(s["sq"], 1)
            then(v.reciprocal(VR[:, :], VR[:, :]))
            then(v.tensor_tensor(R[:, :, :], R[:, :, :], VR[:, :].unsqueeze(2).broadcast_to(wide), ALU.mult))
            then(v.tensor_tensor(R[:, :, :], R[:, :, :], all16(PAR, 1), ALU.mult))
            then(v.tensor_tensor(R[:, :, :], R[:, :, :], all16(PAR, 2), ALU.add))
            then(v.tensor_reduce(scores[:, :, :], R[:, :, :].rearrange("p i (h q) -> p i q h", h=HEADS), AX.X, ALU.add))
            then(v.tensor_scalar(scores[:, :, :], scores[:, :, :], 1.0 / HEADS, None, ALU.mult))

        @block.scalar
        def _(a):
            def step(rnd, r):
                par = r % 2
                a.wait_ge(s["arg"], rnd * RINGS + r + 1)
                a.activation(ARG[:, par], ARG[:, par], ACT.Exp).then_inc(s["p"], 1)

            over_groups(a, step)
            self_factor(sh, None, a, s["self"], keep, EX * HEADS, gmax, ZS, PS)[1]()
            a.wait_ge(s["var"], 1)
            a.activation(VR[:, :], VR[:, :], ACT.Sqrt).then_inc(s["sq"], 1)

        @block.tensor
        def _(pe):
            def step(rnd, r):
                k = rnd * RINGS + r
                par = r % 2
                last = isinstance(k, int) and k == NGRF - 1
                for u in range(GRP):
                    pe.wait_ge(s["lo"], k * GRP + u + 1)
                    pe.wait_ge(s["mv"], k * GRP + u + 1)
                    for j, (b0, m) in enumerate(parts):
                        mm = pe.matmul(pS[j][:, 0:m * VC], OL[:, par, u, :],
                                       MV[:, u % MVR, b0:b0 + m, :].rearrange("p i c -> p (i c)"),
                                       start=(isinstance(k, int) and k == 0 and u == 0), stop=(last and u == GRP - 1),
                                       skip_group_check=True)
                    mm.then_inc(s["mm"], 1)

            over_groups(pe, step)


def route(sh, tag, E, logits, weights, pos, pos_get, expert_of):
    nc = sh.nc
    J = TOP * NB
    NT = tiles_of(E)
    s = {n: sh.sem(f"{tag}_{n}") for n in ("iota", "op", "diff", "onehots", "exp", "mm")}
    with Scope(nc) as sc:
        REV = sc.sb(f"{tag}_REV", [P, E])
        DUMP = sc.sb(f"{tag}_DUMP", [P, TOP])
        NV = sc.sb(f"{tag}_NV", [P, 1])
        Q = sc.sb(f"{tag}_Q", [P, NB, E])
        L2 = sc.sb(f"{tag}_L2", [P, NB, E])
        M = sc.sb(f"{tag}_M", [P, TOP, NB])
        K = sc.sb(f"{tag}_K", [P, NB])
        DD = sc.sb(f"{tag}_DD", [P, NB])
        OH = sc.sb(f"{tag}_OH", [P, TOP, NB, E])
        TOT = sc.sb(f"{tag}_TOT", [P, J, E])
        INC = sc.sb(f"{tag}_INC", [P, J, E])
        TI = sc.sb(f"{tag}_TI", [P, E], I32)
        TF = sc.sb(f"{tag}_TF", [P, E])
        CUM = sc.sb(f"{tag}_CUM", [P, E])
        BASE = sc.sb(f"{tag}_BASE", [P, E])
        PF = sc.sb(f"{tag}_PF", [P, J])
        PG = sc.sb(f"{tag}_PG", [P, J])
        EF = sc.sb(f"{tag}_EF", [1, NT])
        pW = sc.ps(f"{tag}_pW", [P, TOP, 512])
        pC = sc.ps(f"{tag}_pC", [P, TOP, 512])
        block = sc.block()

        @block.gpsimd
        def _(pool):
            pool.iota(DUMP[:, :], [[P, TOP]], base=ROWS, channel_multiplier=1,
                      allow_small_or_imprecise_dtypes=True).then_inc(s["iota"], 1)

        @block.scalar
        def _(a):
            a.wait_ge(s["diff"], 1)
            a.activation(DD[:, :], DD[:, :], ACT.Exp).then_inc(s["exp"], 1)

        @block.tensor
        def _(pe):
            pe.wait_ge(s["onehots"], 1)
            for k in range(TOP):
                rhs = OH[:, k].rearrange("p i e -> p (i e)")
                pe.matmul(pW[:, k, 0:NB * E], sh.tri[:, :], rhs, start=True, stop=True)
                m = pe.matmul(pC[:, k, 0:NB * E], sh.ones[:, :], rhs, start=True, stop=True)
            m.then_inc(s["mm"], 1)

        @block.vector
        def _(v):
            then = Chain(v, s["op"])
            all_e = [P, NB, E]

            def by_e(ap):
                return ap.unsqueeze(1).broadcast_to(all_e)

            def by_i(ap):
                return ap.unsqueeze(2).broadcast_to(all_e)

            then(v.tensor_scalar(REV[:, :], sh.iota[:, 0:E], -1.0, float(E), ALU.mult, ALU.add))
            cur = logits
            for k in range(TOP):
                then(v.tensor_reduce(M[:, k, :], cur[:, :, :], AX.X, ALU.max))
                then(v.tensor_tensor(Q[:, :, :], cur[:, :, :], by_i(M[:, k, :]), ALU.is_equal))
                then(v.tensor_tensor(Q[:, :, :], Q[:, :, :], by_e(REV[:, :]), ALU.mult))
                then(v.tensor_reduce(K[:, :], Q[:, :, :], AX.X, ALU.max))
                then(v.tensor_tensor(OH[:, k], by_e(REV[:, :]), by_i(K[:, :]), ALU.is_equal))
                if k == 0:
                    then(v.scalar_tensor_tensor(L2[:, :, :].rearrange("p i e -> p (i e)"),
                                                OH[:, 0].rearrange("p i e -> p (i e)"), -BIG,
                                                logits[:, :, :].rearrange("p i e -> p (i e)"), ALU.mult, ALU.add))
                    cur = L2
            then(v.tensor_tensor(DD[:, :], M[:, 1, :], M[:, 0, :], ALU.subtract), s["diff"])
            last = OH[:, :, NB - 1, :]
            then(v.tensor_scalar(last, last, sh.valid[:, NB - 1:NB], None, ALU.mult), s["onehots"])
            v.wait_ge(s["exp"], 1)
            then(v.tensor_scalar(weights[:, 0, :], DD[:, :], 1.0, None, ALU.add))
            then(v.reciprocal(weights[:, 0, :], weights[:, 0, :]))
            then(v.tensor_tensor(weights[:, 1, :], weights[:, 0, :], DD[:, :], ALU.mult))
            v.wait_ge(s["mm"], 1)
            counts = TOT[:, :, :].rearrange("p (k i) e -> p k (i e)", k=TOP)
            then(v.tensor_copy(counts, pC[:, :, 0:NB * E]))
            for e in range(E):
                then(v.tensor_tensor_scan(INC[:, :, e], sh.ones[:, 0:J], TOT[:, :, e], 0.0, ALU.mult, ALU.add))
            then(v.tensor_scalar(TI[:, :], INC[:, J - 1, :], float(P - 1), None, ALU.add))
            then(v.tensor_scalar(TI[:, :], TI[:, :], 7, None, ALU.logical_shift_right))
            then(v.tensor_copy(TF[:, :], TI[:, :]))
            then(v.tensor_tensor_scan(CUM[:, :], sh.ones[:, 0:E], TF[:, :], 0.0, ALU.mult, ALU.add))
            then(v.tensor_tensor(BASE[:, :], CUM[:, :], TF[:, :], ALU.subtract))
            then(v.tensor_scalar(BASE[:, :], BASE[:, :], float(P), None, ALU.mult))
            then(v.tensor_tensor(INC[:, :, :], INC[:, :, :], TOT[:, :, :], ALU.subtract))
            inc = INC[:, :, :].rearrange("p (k i) e -> p k (i e)", k=TOP)
            then(v.tensor_tensor(inc, inc, pW[:, :, 0:NB * E], ALU.add))
            then(v.tensor_tensor(INC[:, :, :], INC[:, :, :], BASE[:, :].unsqueeze(1).broadcast_to([P, J, E]), ALU.add))
            then(v.tensor_tensor(INC[:, :, :], INC[:, :, :], OH[:, :, :, :].rearrange("p k i e -> p (k i) e"), ALU.mult))
            then(v.tensor_reduce(PF[:, :], INC[:, :, :], AX.X, ALU.add))
            v.wait_ge(s["iota"], 1)
            then(v.tensor_scalar(NV[:, :], sh.valid[:, NB - 1:NB], -1.0, 1.0, ALU.mult, ALU.add))
            pad = PF[:, NB - 1:J:NB]
            then(v.scalar_tensor_tensor(pad, DUMP[:, :], NV[:, 0:1], pad, ALU.mult, ALU.add))
            then(v.tensor_copy(pos[:, :, :].rearrange("p k i -> p (k i)"), PF[:, :]))
            then(v.tensor_scalar(pos_get[:, :, :].rearrange("p k i -> p (k i)"), PF[:, :], float(NT * P - 1), None, ALU.min))
            then(v.tensor_scalar(EF[:, :], sh.iota[0:1, 0:NT], CUM[0:1, 0:1], None, ALU.is_ge))
            for e in range(1, E - 1):
                then(v.scalar_tensor_tensor(EF[:, :], sh.iota[0:1, 0:NT], CUM[0:1, e:e + 1], EF[:, :], ALU.is_ge, ALU.add))
            then(v.tensor_copy(expert_of[:, 0:NT], EF[:, :]))


def scatter_tokens(sh, tag, stats, stats2, pos, xs):
    nc = sh.nc
    s = {n: sh.sem(f"{tag}_{n}") for n in ("xt", "xn", "staged", "row_ready")}
    s["sent"] = sh.lasting_sem(f"{tag}_sent")
    with Scope(nc) as sc:
        XR = sc.sb(f"{tag}_XR", [P, U7, D])
        STG = sc.sb(f"{tag}_STG", [P, TOP, U7], I32)
        block = sc.block()

        @block.vector
        def _(v):
            def normalise(out, src, stats, i):
                return v.tensor_scalar(out, src, stats[:, bass.ds(i, 1), 0:1].rearrange("p a b -> p (a b)"),
                                       stats[:, bass.ds(i, 1), 1:2].rearrange("p a b -> p (a b)"),
                                       ALU.subtract, ALU.mult)

            @every_round(v)
            def _(it):
                at_least(v, s["sent"], it * U7 * TOP * 16)
                for u in range(U7):
                    i = it * U7 + u
                    row = sh.X[:, bass.ds(i, 1), :].rearrange("p a d -> p (a d)")
                    normalise(XR[:, u, :], row, stats, i).then_inc(s["xn"] if stats2 is None else s["xt"], 1)
                if stats2 is not None:
                    for u in range(U7):
                        at_least(v, s["xt"], it * U7 + u + 1)
                        normalise(XR[:, u, :], XR[:, u, :], stats2, it * U7 + u).then_inc(s["xn"], 1)

        @block.gpsimd
        def _(pool):
            pool.wait_ge(sh.rows_zeroed, NT_MAX // 3 * 16)
            @every_round(pool)
            def _(it):
                at_least(pool, s["sent"], it * U7 * TOP * 16)
                pool.tensor_copy(STG[:, :, :], pos[:, :, bass.ds(it * U7, U7)]).then_inc(s["staged"], 1)
                for u in range(U7):
                    at_least(pool, s["xn"], it * U7 + u + 1)
                    at_least(pool, s["staged"], it + 1)
                    pool.sem_inc(s["row_ready"], 1)
                    for k in range(TOP):
                        pool.indirect_dma_start(xs, bass.IndirectOffsetOnAxis(ap=STG[:, k, u:u + 1].bitcast(U32), axis=0),
                                                XR[:, u, :], None).then_inc(s["sent"], 16)
            pool.wait_ge(s["sent"], NB * TOP * 16)


def experts(sh, tag, E, H, w1, b1, w2, b2, expert_of, xs, ys, y_stored, ln_g=None, ln_b=None):
    nc = sh.nc
    HC = H // P
    NT = tiles_of(E)
    HB = H // 512
    s = {n: sh.sem(f"{tag}_{n}") for n in ("w1", "w2", "rows", "vt", "vc", "bmm", "badd", "scaled", "tin", "xt", "h",
                                           "hc", "tr", "gelu", "y", "yc", "x0", "x1")}
    with Scope(nc) as sc:
        W1 = sc.sb(f"{tag}_W1", [P, E * KC * H])
        W2 = sc.sb(f"{tag}_W2", [P, E * HC * D])
        B2 = sc.sb(f"{tag}_B2", [P, E, D])
        VR = sc.sb(f"{tag}_VR", [P, 3, P])
        VT = sc.sb(f"{tag}_VT", [P, 3, P])
        B1 = sc.sb(f"{tag}_B1", [P, E * HC])
        XI = sc.sb(f"{tag}_XI", [P, 2, D])
        XT = sc.sb(f"{tag}_XT", [P, 2, KC, P])
        HS = sc.sb(f"{tag}_HS", [P, H])
        GT = sc.sb(f"{tag}_GT", [P, HC, P])
        Y = sc.sb(f"{tag}_Y", [P, 2, D])
        pH = [sc.ps(f"{tag}_pH{j}", [P, H]) for j in range(2)]
        pT = sc.ps(f"{tag}_pT", [P, HC, P])
        pI = sc.ps(f"{tag}_pI", [P, KC, P])
        pY = sc.ps(f"{tag}_pY", [P, D])
        block = sc.block()
        vecs = [(b1, E * HC)] + ([(ln_g, E * KC), (ln_b, E * KC)] if ln_g is not None else [])

        def turned(j):
            return pI[:, j, :] if j < 2 else pT[:, 0, :]

        def over_tiles(eng, step):
            step(0, 0)
            step(0, 1)
            with eng.Fori(1, (NT - 3) // 2) as it:
                step(it, 0)
                step(it, 1)
            step((NT - 3) // 2, 0)
            step((NT - 3) // 2, 1)
            step((NT - 1) // 2, 0)

        def expert(eng, regs, t0):
            eng.reg_load(regs, expert_of[0:1, bass.ds(t0, len(regs))])
            return [eng.snap(r, min_val=0, max_val=E - 1) for r in regs]

        @block.sync
        def _(sp):
            for j, (vec, m) in enumerate(vecs):
                sp.dma_start(VR[0:m, j, :], vec.rearrange("e (c p) -> (e c) p", p=P)).then_inc(s["rows"], 16)
            for e in range(E):
                sp.dma_start(W1[:, e * KC * H:(e + 1) * KC * H].rearrange("p (c n) -> p c n", c=KC),
                             w1[e].rearrange("(c p) n -> p c n", p=P)).then_inc(s["w1"], 16)
            for e in range(E):
                sp.dma_start(B2[:, e, :], bcast_rows(b2[e])).then_inc(s["w2"], 16)
                sp.dma_start(W2[:, e * HC * D:(e + 1) * HC * D].rearrange("p (c n) -> p c n", c=HC),
                             w2[e].rearrange("(c p) n -> p c n", p=P)).then_inc(s["w2"], 16)

            def load(t, b):
                at_least(sp, s["tin"], t - 1)
                sp.dma_start(XI[:, b, :], xs[bass.ds(t * P, P), :]).then_inc(s[f"x{b}"], 16)

            def store(t, b):
                sp.wait_ge(s["yc"], t + 1)
                sp.dma_start(ys[bass.ds(t * P, P), :], Y[:, b, :]).then_inc(y_stored[b], 16)

            load(0, 0)
            load(1, 1)

            def step(rnd, b):
                t = rnd * 2 + b
                if not isinstance(t, int) or t + 2 < NT:
                    load(t + 2, b)
                store(t, b)

            over_tiles(sp, step)
            sp.wait_ge(y_stored[0], (NT + 1) // 2 * 16)
            sp.wait_ge(y_stored[1], NT // 2 * 16)

        @block.scalar
        def _(a):
            regs = [a.alloc_register(f"{tag}_a")]

            def copy_in(t, b):
                a.wait_ge(s["tin"], t + 1)
                at_least(a, s["h"], t - 1)
                a.activation(XT[:, b], pI[:, :, :], ACT.Copy).then_inc(s["xt"], 1)

            copy_in(0, 0)

            def step(rnd, b):
                t = rnd * 2 + b
                if not isinstance(t, int) or t + 1 < NT:
                    copy_in(t + 1, 1 - b)
                e, = expert(a, regs, t)
                a.wait_ge(s["badd"], 1)
                a.wait_ge(s["tr"], t + 1)
                at_least(a, s["y"], t)
                for c in range(HC):
                    m = a.activation(GT[:, c, :], pT[:, c, :], ACT.Gelu, bias=B1[:, bass.ds(e * HC + c, 1)])
                m.then_inc(s["gelu"], 1)

            over_tiles(a, step)

        @block.vector
        def _(v):
            v.wait_ge(s["vt"], 1)
            nv = len(vecs)
            for j, (_, m) in enumerate(vecs):
                v.tensor_copy(VT[:, j, 0:m], turned(j)[:, 0:m]).then_inc(s["vc"], 1)
            v.wait_ge(s["vc"], nv)
            if ln_g is not None:
                v.wait_ge(s["bmm"], 1)
                v.tensor_tensor(B1[:, :], VT[:, 0, 0:E * HC], pY[:, 0:E * HC], ALU.add).then_inc(s["badd"], 1)
                for c in range(E * KC):
                    v.tensor_scalar(W1[:, c * H:(c + 1) * H], W1[:, c * H:(c + 1) * H], VT[:, 1, c:c + 1], None,
                                    ALU.mult).then_inc(s["scaled"], 1)
            else:
                v.tensor_copy(B1[:, :], VT[:, 0, 0:E * HC]).then_inc(s["badd"], 1)
            v.wait_ge(s["w2"], 32 * E)
            regs = [v.alloc_register(f"{tag}_v")]

            def bias_out(rnd, b):
                t = rnd * 2 + b
                e, = expert(v, regs, t)
                v.wait_ge(s["y"], t + 1)
                at_least(v, y_stored[b], rnd * 16)
                v.tensor_tensor(Y[:, b, :], pY[:, :], B2[:, bass.ds(e, 1), :].rearrange("p a d -> p (a d)"),
                                ALU.add).then_inc(s["yc"], 1)

            def step(rnd, b):
                t = rnd * 2 + b
                v.wait_ge(s["h"], t + 1)
                at_least(v, s["tr"], t)
                v.tensor_copy(HS[:, :], pH[b][:, :]).then_inc(s["hc"], 1)
                if not (isinstance(t, int) and t == 0):
                    bias_out(rnd - (1 - b), 1 - b)

            over_tiles(v, step)
            bias_out((NT - 1) // 2, 0)

        @block.tensor
        def _(pe):
            pe.wait_ge(s["rows"], 16 * len(vecs))
            for j, (_, m) in enumerate(vecs):
                t = pe.transpose(turned(j)[:, 0:m], VR[0:m, j, :], sh.ident[0:m, 0:m])
            t.then_inc(s["vt"], 1)
            pe.wait_ge(s["vc"], len(vecs))
            pe.wait_ge(s["w1"], 16 * E)
            if ln_g is not None:
                for e in range(E):
                    for h in range(HC):
                        for c in range(KC):
                            o = (e * KC + c) * H + h * P
                            m = pe.matmul(pY[:, e * HC + h:e * HC + h + 1], W1[:, o:o + P],
                                          VT[:, 2, e * KC + c:e * KC + c + 1], start=(c == 0), stop=(c == KC - 1))
                m.then_inc(s["bmm"], 1)
                pe.wait_ge(s["scaled"], E * KC)
            pe.wait_ge(s["badd"], 1)
            pe.wait_ge(s["w2"], 32 * E)
            regs = [pe.alloc_register(f"{tag}_p{j}") for j in range(2)]

            def turn_in(t, b, rnd):
                pe.wait_ge(s[f"x{b}"], rnd * 16)
                at_least(pe, s["xt"], t)
                for c in range(KC):
                    m = pe.transpose(pI[:, c, :], XI[:, b, c * P:(c + 1) * P], sh.ident[:, :])
                m.then_inc(s["tin"], 1)

            turn_in(0, 0, 1)

            def by_w1(t, b, e):
                pe.wait_ge(s["xt"], t + 1)
                at_least(pe, s["hc"], t - 1)
                for n in range(HB):
                    for c in range(KC):
                        m = pe.matmul(pH[b][:, n * 512:(n + 1) * 512], XT[:, b, c, :],
                                      W1[:, bass.ds(e * (KC * H) + (c * H + n * 512), 512)],
                                      start=(c == 0), stop=(c == KC - 1))
                m.then_inc(s["h"], 1)

            def by_w2(t, e):
                pe.wait_ge(s["gelu"], t + 1)
                at_least(pe, s["yc"], t)
                for c in range(HC):
                    m = pe.matmul(pY[:, :], GT[:, c, :], W2[:, bass.ds(e * (HC * D) + c * D, D)],
                                  start=(c == 0), stop=(c == HC - 1))
                m.then_inc(s["y"], 1)

            def step(rnd, b):
                t = rnd * 2 + b
                if isinstance(t, int) and t == 0:
                    e, = expert(pe, regs[1:], 0)
                    by_w1(t, b, e)
                else:
                    e_before, e = expert(pe, regs, t - 1)
                    by_w1(t, b, e)
                    by_w2(t - 1, e_before)
                if not isinstance(t, int) or t + 1 < NT:
                    turn_in(t + 1, 1 - b, rnd + b + 1)
                pe.wait_ge(s["hc"], t + 1)
                at_least(pe, s["gelu"], t)
                for c in range(HC):
                    m = pe.transpose(pT[:, c, :], HS[:, c * P:(c + 1) * P], sh.ident[:, :])
                m.then_inc(s["tr"], 1)

            over_tiles(pe, step)
            e, = expert(pe, regs[1:], NT - 1)
            by_w2(NT - 1, e)


def combine(sh, tag, weights, pos_get, ys, y_stored, y_counts):
    nc = sh.nc
    s = {n: sh.sem(f"{tag}_{n}") for n in ("staged", "sum", "slot_free")}
    s_got = [sh.lasting_sem(f"{tag}_got{u}") for u in range(U7)]
    with Scope(nc) as sc:
        R = sc.sb(f"{tag}_R", [P, TOP, U7, D])
        STG = sc.sb(f"{tag}_STG", [P, TOP, U7], I32)
        block = sc.block()

        @block.gpsimd
        def _(pool):
            pool.wait_ge(y_stored[0], y_counts[0])
            @every_round(pool)
            def _(it):
                for u in range(U7):
                    at_least(pool, s_got[u], it * TOP * 16)
                pool.tensor_copy(STG[:, :, :], pos_get[:, :, bass.ds(it * U7, U7)]).then_inc(s["staged"], 1)
                at_least(pool, s["staged"], it + 1)
                for u in range(U7):
                    at_least(pool, s["sum"], it * U7 * TOP)
                    pool.sem_inc(s["slot_free"], 1)
                    for k in range(TOP):
                        pool.indirect_dma_start(R[:, k, u, :], None, ys, bass.IndirectOffsetOnAxis(
                            ap=STG[:, k, u:u + 1].bitcast(U32), axis=0)).then_inc(s_got[u], 16)

        @block.vector
        def _(v):
            @every_round(v)
            def _(it):
                for k in range(TOP):
                    for u in range(U7):
                        if k == 0:
                            at_least(v, s_got[u], (it + 1) * TOP * 16)
                        else:
                            at_least(v, s["sum"], it * U7 * TOP + u + 1)
                        i = it * U7 + u
                        row = sh.X[:, bass.ds(i, 1), :].rearrange("p a d -> p (a d)")
                        v.scalar_tensor_tensor(row, R[:, k, u, :], weights[:, k, bass.ds(i, 1)], row,
                                               ALU.mult, ALU.add).then_inc(s["sum"], 1)
            v.wait_ge(s["sum"], NB * TOP)


def store_out(sh, out):
    s_o = sh.sem("out_stored")
    with Scope(sh.nc) as sc:
        block = sc.block()

        @block.sync
        def _(sp):
            full = out[0:(NB - 1) * P, :].rearrange("(i p) d -> p i d", p=P)
            for c in range(6):
                sp.dma_start(full[:, 8 * c:8 * c + 8, :], sh.X[:, 8 * c:8 * c + 8, :]).then_inc(s_o, 16)
            sp.dma_start(out[(NB - 1) * P:N, :], sh.X[0:LAST, NB - 1, :]).then_inc(s_o, 16)
            sp.wait_ge(s_o, 7 * 16)


def add_bias(sh, tag, L, bias, E):
    s_b, s_a = sh.sem(f"{tag}_loaded"), sh.sem(f"{tag}_added")
    with Scope(sh.nc) as sc:
        B = sc.sb(f"{tag}_B", [P, E])
        block = sc.block()

        @block.sync
        def _(sp):
            sp.dma_start(B[:, :], bcast_rows(bias)).then_inc(s_b, 16)

        @block.vector
        def _(v):
            v.wait_ge(s_b, 16)
            v.tensor_tensor(L[:, :, :], L[:, :, :], B[:, :].unsqueeze(1).broadcast_to([P, NB, E]), ALU.add).then_inc(s_a, 1)


def second_stats(sh, tag, stats2):
    s_v, s_q = sh.sem(f"{tag}_var"), sh.sem(f"{tag}_sqrt")
    with Scope(sh.nc) as sc:
        block = sc.block()

        @block.vector
        def _(v):
            v.tensor_scalar(stats2[:, :, 1], stats2[:, :, 1], EPS, None, ALU.add).then_inc(s_v, 1)
            v.wait_ge(s_q, 1)
            v.reciprocal(stats2[:, :, 1], stats2[:, :, 1]).then_inc(s_v, 1)

        @block.scalar
        def _(a):
            a.wait_ge(s_v, 1)
            a.activation(stats2[:, :, 1], stats2[:, :, 1], ACT.Sqrt).then_inc(s_q, 1)


def build(nc, a, out, stop=99):
    def dram(name, shape):
        return nc.dram_tensor(name, shape, F32, kind="Internal").ap()

    with ExitStack() as ctx:
        sh = Shared(nc, ctx)
        table0 = dram("table0", (NP, D + HEADS))
        table1 = dram("table1", (NP, D))
        table2 = dram("table2", (NP, 16 + HEADS))
        adst2 = dram("adst2", (NP, HEADS))
        xs = dram("xs", (ROWS + TOP * P, D))
        ys = dram("ys", (ROWS, D))
        planned = [sh.nc.dram_tensor(f"planned{j}", (P, NS), dt, kind="Internal").ap() for j, dt in enumerate((I32, F32, F32))]
        planned_block = nc.dram_tensor("planned_block", (1, NS), I32, kind="Internal").ap()
        gather_done = [sh.lasting_sem(f"gather_done{j}") for j in range(RINGS)]
        acc_zeroed = [sh.lasting_sem(f"acc_zeroed{j}") for j in range(2)]
        y_stored = [sh.lasting_sem(f"y_stored{j}") for j in range(2)]
        stats = sh.sb("stats", [P, NB, 2])
        graph_rounds = SG // RINGS

        setup(sh, a["x"], xs)
        plan_steps(sh, a["first_dst"], (a["src_rows"], a["dst_rows"], a["weight_rows"]), planned, planned_block)

        layer_norm_stats(sh, "s0", stats)
        with Scope(nc) as layer:
            keep = layer.sb("keep0", [P, NB, 2 * HEADS])
            gmax = layer.sb("gmax0", [P, HEADS])
            acc = layer.sb("acc0", [P, NB, D + HEADS])
            project_nodes(sh, "p0", stats, a["L0_gnn_W"], D + 2 * HEADS, att=(a["L0_gnn_att_src"], a["L0_gnn_att_dst"]),
                          table=table0, table_cols=D + HEADS, keep=keep, keep_from=D, zero=(acc, acc_zeroed[0]))
            table_maximum(sh, "m0", keep, 0, gmax)
            graph_pass(sh, "g0", planned, planned_block, table0, D + HEADS, acc, (acc_zeroed[0], NB), gather_done, 0,
                       keep=keep, gmax=gmax)
            finish_attention(sh, "f0", acc, table0, keep, gmax, a["L0_gnn_bias"])
        if stop == 1:
            return store_out(sh, out)

        sh.end_layer()

        layer_norm_stats(sh, "s1", stats)
        with Scope(nc) as layer:
            weights = layer.sb("weights0", [P, TOP, NB])
            pos = layer.sb("pos0", [P, TOP, NB], I32)
            pos_get = layer.sb("pos_get0", [P, TOP, NB], I32)
            expert_of = layer.sb("expert_of0", [1, NT_MAX], I32)
            with Scope(nc) as inner:
                stats2 = inner.sb("stats2", [P, NB, 2])
                logits = inner.sb("logits0", [P, NB, 8])
                project_nodes(sh, "p1", stats, a["L0_ffn_Wr"], 8, keep=logits, stats2=stats2)
                add_bias(sh, "rb", logits, a["L0_ffn_br"], 8)
                second_stats(sh, "s2", stats2)
                route(sh, "r0", 8, logits, weights, pos, pos_get, expert_of)
                scatter_tokens(sh, "t0", stats, stats2, pos, xs)
            experts(sh, "e0", 8, 1024, a["L0_ffn_W1"], a["L0_ffn_b1"], a["L0_ffn_W2"], a["L0_ffn_b2"], expert_of, xs, ys,
                    y_stored, ln_g=a["L0_ffn_ln_g"], ln_b=a["L0_ffn_ln_b"])
            combine(sh, "c0", weights, pos_get, ys, y_stored, (16 * ((tiles_of(8) + 1) // 2),))
        if stop == 2:
            return store_out(sh, out)

        sh.end_layer()

        layer_norm_stats(sh, "s3", stats)
        with Scope(nc) as layer:
            acc = layer.sb("acc1", [P, NB, D])
            store_rows(sh, "p2", stats, table1, zero=(acc, acc_zeroed[1]))
            graph_pass(sh, "g1", planned, planned_block, table1, D, acc, (acc_zeroed[1], NB), gather_done, graph_rounds)
            finish_weighted(sh, "f1", acc, stats, a["L1_gnn_W1t"], a["L1_gnn_W2t"], a["L1_gnn_b1"], a["L1_gnn_b2"])
        if stop == 3:
            return store_out(sh, out)

        sh.end_layer()

        layer_norm_stats(sh, "s4", stats)
        with Scope(nc) as layer:
            weights = layer.sb("weights1", [P, TOP, NB])
            pos = layer.sb("pos1", [P, TOP, NB], I32)
            pos_get = layer.sb("pos_get1", [P, TOP, NB], I32)
            expert_of = layer.sb("expert_of1", [1, NT_MAX], I32)
            with Scope(nc) as inner:
                keep = inner.sb("keep1", [P, NB, 16 + 2 * HEADS])
                gmax = inner.sb("gmax1", [P, HEADS])
                scores = inner.sb("scores", [P, NB, 4])
                project_nodes(sh, "p3", stats, a["L1_ffn_W_gat"], 16 + 2 * HEADS,
                              att=(a["L1_ffn_att_src"], a["L1_ffn_att_dst"]),
                              table=table2, table_cols=16 + HEADS, keep=keep, keep_from=0)
                table_maximum(sh, "m1", keep, 16, gmax)
                store_adst(sh, "d1", keep, 16 + HEADS, adst2)
                free_edges_pass(sh, "q", a["fsrc_t"], a["fdst_t"], table2, adst2, gmax, keep, gather_done, 2 * graph_rounds,
                                a["L1_ffn_b_gat"], a["L1_ffn_ln_gamma"], a["L1_ffn_ln_beta"], scores)
                route(sh, "r1", 4, scores, weights, pos, pos_get, expert_of)
                scatter_tokens(sh, "t1", stats, None, pos, xs)
            y_stored2 = [sh.lasting_sem(f"y1_stored{j}") for j in range(2)]
            experts(sh, "e1", 4, 512, a["L1_ffn_W1"], a["L1_ffn_b1"], a["L1_ffn_W2"], a["L1_ffn_b2"], expert_of, xs, ys,
                    y_stored2)
            combine(sh, "c1", weights, pos_get, ys, y_stored2, (16 * ((tiles_of(4) + 1) // 2),))
        store_out(sh, out)
        sh.layer.close()


def zero_blocks(pool, zero):
    acc, zeroed = zero
    for i in range(NB):
        pool.memset(acc[:, i, :], 0.0).then_inc(zeroed, 1)


def store_rows(sh, tag, stats, table, zero):
    s_xn = sh.sem(f"{tag}_xn")
    s_out = [sh.sem(f"{tag}_out{u}") for u in range(U7)]
    with Scope(sh.nc) as sc:
        XR = sc.sb(f"{tag}_XR", [P, U7, D])
        block = sc.block()

        @block.gpsimd
        def _(pool):
            zero_blocks(pool, zero)

        @block.vector
        def _(v):
            @every_round(v)
            def _(it):
                for u in range(U7):
                    i = it * U7 + u
                    at_least(v, s_out[u], it * 16)
                    v.tensor_scalar(XR[:, u, :], sh.X[:, bass.ds(i, 1), :].rearrange("p a d -> p (a d)"),
                                    stats[:, bass.ds(i, 1), 0:1].rearrange("p a b -> p (a b)"),
                                    stats[:, bass.ds(i, 1), 1:2].rearrange("p a b -> p (a b)"),
                                    ALU.subtract, ALU.mult).then_inc(s_xn, 1)

        @block.sync
        def _(sp):
            @every_round(sp)
            def _(it):
                for u in range(U7):
                    at_least(sp, s_xn, it * U7 + u + 1)
                    sp.dma_start(table[bass.ds((it * U7 + u) * P, P), :], XR[:, u, :]).then_inc(s_out[u], 16)
            for u in range(U7):
                sp.wait_ge(s_out[u], NB // U7 * 16)


def edge_rows(e, fill):
    import numpy as np
    full = np.full(NTE * P, fill, e.dtype)
    full[:e.shape[0]] = e
    return full.reshape(NTE, P)


def edge_columns(e, tiles, fill):
    import numpy as np
    full = np.full(tiles * P, fill, e.dtype)
    full[:e.shape[0]] = e
    return np.ascontiguousarray(full.reshape(tiles, P).T)


NAMES = ["x", "L0_gnn_W", "L0_gnn_att_src", "L0_gnn_att_dst", "L0_gnn_bias", "L0_ffn_Wr", "L0_ffn_br", "L0_ffn_ln_g",
         "L0_ffn_ln_b", "L0_ffn_W1", "L0_ffn_b1", "L0_ffn_W2", "L0_ffn_b2", "L1_gnn_b1", "L1_gnn_b2", "L1_ffn_W_gat",
         "L1_ffn_att_src", "L1_ffn_att_dst", "L1_ffn_b_gat", "L1_ffn_ln_gamma", "L1_ffn_ln_beta", "L1_ffn_W1",
         "L1_ffn_b1", "L1_ffn_W2", "L1_ffn_b2"]


def kernel(**inputs):
    import concourse.bacc as bacc
    import numpy as np
    from concourse.bass_utils import run_bass_kernel_spmd

    arrays = {n: np.ascontiguousarray(inputs[n]) for n in NAMES}
    arrays["L1_gnn_W1t"] = np.ascontiguousarray(np.asarray(inputs["L1_gnn_W1"]).T)
    arrays["L1_gnn_W2t"] = np.ascontiguousarray(np.asarray(inputs["L1_gnn_W2"]).T)
    arrays["src_rows"] = edge_rows(np.asarray(inputs["src"]), 0)
    arrays["dst_rows"] = edge_rows(np.asarray(inputs["dst"]), N)
    arrays["weight_rows"] = edge_rows(np.asarray(inputs["edge_weight"]), 0)
    arrays["first_dst"] = np.ascontiguousarray(arrays["dst_rows"][:, 0]).reshape(1, NTE)
    fe = np.asarray(inputs["L1_ffn_edge_index"])
    arrays["fsrc_t"] = edge_columns(fe[0], NTF, 0)
    arrays["fdst_t"] = edge_columns(fe[1], NTF, 0)

    nc = bacc.Bacc("TRN2", target_bir_lowering=False, num_devices=1)
    args = {n: nc.dram_tensor(f"in_{n}", v.shape, mybir.dt.from_np(v.dtype), kind="ExternalInput").ap()
            for n, v in arrays.items()}
    out = nc.dram_tensor("out_x", (N, D), F32, kind="ExternalOutput").ap()
    build(nc, args, out)
    r = run_bass_kernel_spmd(nc, [{f"in_{n}": v for n, v in arrays.items()}], core_ids=[0])
    return r.results[0]["out_x"]
```

```python
from contextlib import ExitStack

import concourse.bass as bass
from concourse import mybir

F32 = mybir.dt.float32
I32 = mybir.dt.int32
U32 = mybir.dt.uint32
ALU = mybir.AluOpType
ACT = mybir.ActivationFunctionType
AX = mybir.AxisListType

P = 128
N = 6250
D = 256
NB = -(-N // P)
NP = NB * P
LAST = N - (NB - 1) * P
KC = D // P
U7 = 7
HEADS = 4
EPS = 1e-5
SLOPE = 0.2
BIG = 3e38

E_SORTED = 206250
GRP = 8
RINGS = 4
E_TILES = -(-E_SORTED // P)
NS = -(-(E_TILES + NB - 1) // (P)) * P
NTE = NS - (NB - 1)
SCH = NS // P
SG = NS // GRP
E_FREE = 131072
NTF = E_FREE // P
NGRF = NTF // GRP

TOP = 2


def tiles_of(experts):
    most = (TOP * N + experts * (P - 1)) // P
    return most + 1 - most % 2


NT_MAX = tiles_of(8)
ROWS = NT_MAX * P


class Shared:

    def __init__(self, nc, ctx):
        self.nc, self.ctx = nc, ctx
        self.layer, self.sems = ExitStack(), []

    def lasting_sem(self, name):
        return self.ctx.enter_context(self.nc.semaphore(name))

    def sem(self, name):
        self.sems.append(self.layer.enter_context(self.nc.semaphore(name)))
        return self.sems[-1]

    def end_layer(self):
        with self.nc.Block() as block:
            @block.gpsimd
            def _(pool):
                for sem in self.sems:
                    pool.sem_clear(sem)
        self.layer.close()
        self.layer, self.sems = ExitStack(), []

    def sb(self, name, shape, dt=F32):
        return self.ctx.enter_context(self.nc.sbuf_tensor(name, shape, dt))


class Scope:

    def __init__(self, nc):
        self.nc, self.ctx = nc, ExitStack()

    def __enter__(self):
        self.ctx.__enter__()
        return self

    def __exit__(self, *a):
        return self.ctx.__exit__(*a)

    def sb(self, name, shape, dt=F32):
        return self.ctx.enter_context(self.nc.sbuf_tensor(name, shape, dt))

    def ps(self, name, shape, dt=F32):
        return self.ctx.enter_context(self.nc.psum_tensor(name, shape, dt))

    def block(self):
        return self.ctx.enter_context(self.nc.Block())


def at_least(eng, sem, value):
    if not isinstance(value, int) or value > 0:
        eng.wait_ge(sem, value)


def every_round(eng):
    def run(body):
        body(0)
        with eng.Fori(1, NB // U7 - 1) as it:
            body(it)
        body(NB // U7 - 1)
    return run


def every_pair(eng, step):
    rnds = NB // U7 // 2
    step(0, 0)
    step(0, 1)
    with eng.Fori(1, rnds) as it:
        step(it, 0)
        step(it, 1)
    step(rnds, 0)


class Chain:

    def __init__(self, eng, sem):
        self.eng, self.sem, self.n = eng, sem, 0

    def __call__(self, ins, sem=None):
        if sem is None:
            self.n += 1
            ins.then_inc(self.sem, 1)
            self.eng.wait_ge(self.sem, self.n)
        else:
            ins.then_inc(sem, 1)
            self.eng.wait_ge(sem, 1)


def bcast_rows(vec, n=P):
    return vec.partition_broadcast(n)


def setup(sh, x):
    nc = sh.nc
    sh.X = sh.sb("X", [P, NB, D])
    sh.ident = sh.sb("ident", [P, P])
    sh.iota = sh.sb("iota", [P, P])
    sh.ones = sh.sb("ones", [P, P])
    sh.tri = sh.sb("tri", [P, P])
    sh.valid = sh.sb("valid", [P, NB])
    s_x, s_cst, s_pre = sh.sem("x_loaded"), sh.sem("constants"), sh.sem("memsets")
    sh.x_ready = (s_x, 7 * 16)
    with Scope(nc) as sc:
        block = sc.block()

        @block.gpsimd
        def _(pool):
            pool.memset(sh.X[:, NB - 1, :], 0.0).then_inc(s_pre, 1)
            pool.memset(sh.ident[:, :], 0.0).then_inc(s_pre, 1)
            pool.memset(sh.ones[:, :], 1.0).then_inc(s_pre, 1)
            pool.memset(sh.valid[:, :], 1.0).then_inc(s_pre, 1)
            pool.iota(sh.iota[:, :], [[1, P]], base=0, channel_multiplier=0,
                      allow_small_or_imprecise_dtypes=True).then_inc(s_cst, 1)
            pool.wait_ge(s_pre, 4)
            pool.affine_select(out=sh.ident[:, :], in_=sh.ident[:, :], compare_op=ALU.not_equal, fill=1.0,
                               base=0, pattern=[[-1, P]], channel_multiplier=1).then_inc(s_cst, 1)
            pool.affine_select(out=sh.tri[:, :], in_=sh.ones[:, :], compare_op=ALU.is_gt, fill=0.0,
                               base=0, pattern=[[1, P]], channel_multiplier=-1).then_inc(s_cst, 1)
            pool.affine_select(out=sh.valid[:, :], in_=sh.valid[:, :], compare_op=ALU.is_ge, fill=0.0,
                               base=N - 1, pattern=[[-P, NB]], channel_multiplier=-1).then_inc(s_cst, 1)

        @block.sync
        def _(sp):
            full = x[0:(NB - 1) * P, :].rearrange("(i p) d -> p i d", p=P)
            for c in range(6):
                sp.dma_start(sh.X[:, 8 * c:8 * c + 8, :], full[:, 8 * c:8 * c + 8, :]).then_inc(s_x, 16)
            sp.wait_ge(s_pre, 1)
            sp.dma_start(sh.X[0:LAST, NB - 1, :], x[(NB - 1) * P:N, :]).then_inc(s_x, 16)


class LayerNormStats:

    def __init__(self, sh, sc, tag, mean_rstd, x_ready=None):
        self.sh, self.out, self.x_ready = sh, mean_rstd, x_ready
        self.st = sc.sb(f"{tag}_st", [P, 8, 6])
        self.sems = [sh.sem(f"{tag}_{n}") for n in ("bn_stats", "bn_aggr", "sqrt", "eps", "rstd")]

    def on_vector(self, v):
        s_st, s_ag, s_sq, s_ve, s_r = self.sems
        st, mean_rstd = self.st, self.out
        if self.x_ready is not None:
            v.wait_ge(*self.x_ready)
        for i in range(NB):
            if i >= 8:
                v.wait_ge(s_ag, i - 7)
            v.bn_stats(st[:, i % 8, :], self.sh.X[:, i, :]).then_inc(s_st, 1)
            if i >= 4:
                v.wait_ge(s_st, i - 3)
                v.bn_aggr(mean_rstd[:, i - 4, :], st[:, (i - 4) % 8, :]).then_inc(s_ag, 1)
        for i in range(NB - 4, NB):
            v.wait_ge(s_st, i + 1)
            v.bn_aggr(mean_rstd[:, i, :], st[:, i % 8, :]).then_inc(s_ag, 1)
        v.wait_ge(s_ag, NB)
        v.tensor_scalar(mean_rstd[:, :, 1], mean_rstd[:, :, 1], EPS, None, ALU.add).then_inc(s_ve, 1)
        v.wait_ge(s_sq, 1)
        v.reciprocal(mean_rstd[:, :, 1], mean_rstd[:, :, 1]).then_inc(s_r, 1)
        v.wait_ge(s_r, 1)

    def on_scalar(self, a):
        _, _, s_sq, s_ve, _ = self.sems
        a.wait_ge(s_ve, 1)
        a.activation(self.out[:, :, 1], self.out[:, :, 1], ACT.Sqrt).then_inc(s_sq, 1)


def layer_norm_stats(sh, tag, mean_rstd):
    with Scope(sh.nc) as sc:
        stats = LayerNormStats(sh, sc, tag, mean_rstd)
        block = sc.block()
        block.vector(stats.on_vector)
        block.scalar(stats.on_scalar)


def project_nodes(sh, tag, stats, weight, ncols, att=None, table=None, table_cols=0, keep=None, keep_from=0,
                  stats2=None, zero=None):
    nc = sh.nc
    wc = weight.shape[1]
    per = wc // HEADS
    s = {n: sh.sem(f"{tag}_{n}") for n in ("w", "att", "fold", "xn", "xrfree", "tr", "xt", "mm", "ev", "kept", "st", "st_seen", "ag", "agc")}
    s_tab = [sh.sem(f"{tag}_tab{u}") for u in range(U7)] if table is not None else None
    with Scope(nc) as sc:
        W = sc.sb(f"{tag}_W", [P, KC, ncols])
        XR = sc.sb(f"{tag}_XR", [P, U7, D])
        XT = sc.sb(f"{tag}_XT", [P, 2, KC, P])
        OUT = sc.sb(f"{tag}_OUT", [P, U7, table_cols]) if table is not None else None
        ATT = sc.sb(f"{tag}_ATT", [P, 2, wc]) if att else None
        FT = sc.sb(f"{tag}_FT", [P, KC, 2, wc]) if att else None
        ST = sc.sb(f"{tag}_ST", [P, U7, 6]) if stats2 is not None else None
        AG = sc.sb(f"{tag}_AG", [P, U7, 2]) if stats2 is not None else None
        pT = [sc.ps(f"{tag}_pT{j}", [P, KC, P]) for j in range(2)]
        pO = [sc.ps(f"{tag}_pO{j}", [P, ncols]) for j in range(4)]
        block = sc.block()

        if zero is not None:
            @block.gpsimd
            def _(pool):
                zero_blocks(pool, zero)

        @block.sync
        def _(sp):
            sp.dma_start(W[:, :, 0:wc], weight.rearrange("(c k) n -> k c n", k=P)).then_inc(s["w"], 16)
            if att:
                for a in range(2):
                    sp.dma_start(ATT[:, a, :], bcast_rows(att[a].rearrange("h c -> (h c)"))).then_inc(s["att"], 16)
            if table is not None:
                @every_round(sp)
                def _(it):
                    for u in range(U7):
                        at_least(sp, s["ev"], it * U7 + u + 1)
                        sp.dma_start(table[bass.ds((it * U7 + u) * P, P), :], OUT[:, u, :]).then_inc(s_tab[u], 16)
                for u in range(U7):
                    sp.wait_ge(s_tab[u], 16 * (NB // U7))

        @block.vector
        def _(v):
            v.wait_ge(s["w"], 16)
            if att:
                v.wait_ge(s["att"], 32)
                for c in range(KC):
                    for a in range(2):
                        v.tensor_tensor(FT[:, c, a, :], W[:, c, 0:wc], ATT[:, a, :], ALU.mult).then_inc(s["fold"], 1)
                v.wait_ge(s["fold"], 2 * KC)
                for c in range(KC):
                    for a in range(2):
                        v.tensor_reduce(W[:, c, wc + a * HEADS:wc + (a + 1) * HEADS],
                                        FT[:, c, a, :].rearrange("p (h q) -> p h q", q=per),
                                        AX.X, ALU.add).then_inc(s["fold"], 1)
            def normalise(it, u):
                i = it * U7 + u
                at_least(v, s["tr"], (it - 1) * U7 + u + 1)
                v.tensor_scalar(XR[:, u, :], sh.X[:, bass.ds(i, 1), :].rearrange("p a d -> p (a d)"),
                                stats[:, bass.ds(i, 1), 0:1].rearrange("p a b -> p (a b)"),
                                stats[:, bass.ds(i, 1), 1:2].rearrange("p a b -> p (a b)"),
                                ALU.subtract, ALU.mult).then_inc(s["xn"], 1)

            def row_stats(it):
                at_least(v, s["agc"], it)
                for u in range(U7):
                    v.wait_ge(s["xn"], it * U7 + u + 1)
                    v.bn_stats(ST[:, u, :], XR[:, u, :]).then_inc(s["st"], 1)
                v.wait_ge(s["st"], (it + 1) * U7)
                v.sem_inc(s["st_seen"], 1)
                for u in range(U7):
                    v.bn_aggr(AG[:, u, :], ST[:, u, :]).then_inc(s["ag"], 1)
                v.wait_ge(s["ag"], (it + 1) * U7)
                v.tensor_copy(stats2[:, bass.ds(it * U7, U7), :], AG[:, :, :]).then_inc(s["agc"], 1)

            def output(it, u):
                i = it * U7 + u
                v.wait_ge(s["mm"], i + 1)
                if table is not None:
                    at_least(v, s_tab[u], it * 16)
                    v.tensor_copy(OUT[:, u, :], pO[u % 4][:, 0:table_cols]).then_inc(s["ev"], 1)
                if keep is not None:
                    v.tensor_copy(keep[:, bass.ds(i, 1), :].rearrange("p a b -> p (a b)"),
                                  pO[u % 4][:, keep_from:ncols]).then_inc(s["kept"], 1)

            for u in range(U7):
                normalise(0, u)
            if stats2 is not None:
                row_stats(0)

            @every_round(v)
            def _(it):
                more = not (isinstance(it, int) and it == NB // U7 - 1)
                for u in range(U7):
                    output(it, u)
                    if more:
                        normalise(it + 1, u)
                if more and stats2 is not None:
                    row_stats(it + 1)

        @block.scalar
        def _(a):
            @every_round(a)
            def _(it):
                for u in range(U7):
                    i = it * U7 + u
                    a.wait_ge(s["tr"], i + 1)
                    if u >= 2:
                        at_least(a, s["mm"], i - 1)
                    else:
                        at_least(a, s["mm"], it * U7)
                    a.activation(XT[:, u % 2, :, :], pT[u % 2][:, :, :], ACT.Copy).then_inc(s["xt"], 1)

        @block.tensor
        def _(pe):
            def turn(it, u):
                at_least(pe, s["xn"], it * U7 + u + 1)
                if u >= 2:
                    at_least(pe, s["xt"], it * U7 + u - 1)
                else:
                    at_least(pe, s["xt"], it * U7)
                for c in range(KC):
                    m = pe.transpose(pT[u % 2][:, c, :], XR[:, u, c * P:(c + 1) * P], sh.ident[:, :])
                m.then_inc(s["tr"], 1)

            def product(it, u):
                i = it * U7 + u
                pe.wait_ge(s["xt"], i + 1)
                for done, used in (("ev", table), ("kept", keep)):
                    if used is not None:
                        at_least(pe, s[done], i - 3 if u >= 4 else it * U7)
                for c in range(KC):
                    m = pe.matmul(pO[u % 4][:, :], XT[:, u % 2, c, :], W[:, c, :], start=(c == 0), stop=(c == KC - 1))
                m.then_inc(s["mm"], 1)

            pe.wait_ge(s["fold"] if att else s["w"], 4 * KC if att else 16)
            @every_round(pe)
            def _(it):
                turn(it, 0)
                for u in range(U7):
                    if u + 1 < U7:
                        turn(it, u + 1)
                    product(it, u)


def load_registers(eng, regs, row, at):
    eng.reg_load(regs, row[0:1, bass.ds(at, len(regs))])
    return [eng.snap(r, min_val=0, max_val=NB - 1) for r in regs]


def plan_steps(sh, first_dst, edges, planned, planned_block, stats):
    nc = sh.nc
    s = {n: sh.sem(f"plan_{n}") for n in ("first", "iota", "op", "start", "sums", "tile", "float", "turned", "out",
                                          "stored")}
    NA = 3
    BK = 4
    NBK = -(-SCH // BK)
    s_got = [sh.lasting_sem(f"plan_rows{j}") for j in range(NBK)]
    HB = NS // 4
    with Scope(nc) as sc:
        F = sc.sb("plan_F", [P, NTE], I32)
        FF = sc.sb("plan_FF", [P, NTE])
        PI = sc.sb("plan_PI", [P, 1])
        ROW = sc.sb("plan_ROW", [P, NS])
        COL = sc.sb("plan_COL", [P, SCH])
        START = sc.sb("plan_START", [P, 1])
        DIAG = sc.sb("plan_DIAG", [P, P])
        GE = sc.sb("plan_GE", [P, NS])
        TF = sc.sb("plan_TF", [P, SCH])
        T = sc.sb("plan_T", [P, SCH], I32)
        BF = sc.sb("plan_BF", [P, NS])
        BI = sc.sb("plan_BI", [P, NS], I32)
        RAW = sc.sb("plan_RAW", [P, NA, SCH, P], I32)
        RF = sc.sb("plan_RF", [P, 2, SCH, P])
        OUT = sc.sb("plan_OUT", [P, 2, NS])
        OSRC = sc.sb("plan_OSRC", [P, NS], I32)
        norm = LayerNormStats(sh, sc, "s0", stats, sh.x_ready)
        pJ = sc.ps("plan_pJ", [P, P])
        pB = sc.ps("plan_pB", [P, 4, 512])
        pT = [sc.ps(f"plan_pT{j}", [P, BK * P]) for j in range(2)]
        block = sc.block()

        @block.sync
        def _(sp):
            sp.dma_start(F[:, :], bcast_rows(first_dst[0, :])).then_inc(s["first"], 16)
            sp.wait_ge(s["out"], NA * NBK)
            for a, o in enumerate((OSRC[:, :], OUT[:, 0, :], OUT[:, 1, :])):
                sp.dma_start(planned[a], o).then_inc(s["stored"], 16)
            sp.dma_start(planned_block, BI[0:1, :]).then_inc(s["stored"], 16)
            sp.wait_ge(s["stored"], 16 * (NA + 1))

        @block.gpsimd
        def _(pool):
            for out, pattern, mult in ((PI, [[0, 1]], 1), (ROW, [[1, NS]], 0), (COL, [[P, SCH]], 1)):
                pool.iota(out[:, :], pattern, base=0, channel_multiplier=mult,
                          allow_small_or_imprecise_dtypes=True).then_inc(s["iota"], 1)
            pool.wait_ge(s["tile"], 1)
            for c in range(SCH):
                for a in range(NA):
                    rows = RAW[:, a, c, :] if a < 2 else RAW[:, a, c, :].bitcast(F32)
                    pool.indirect_dma_start(rows, None, edges[a], bass.IndirectOffsetOnAxis(
                        ap=T[:, c:c + 1].bitcast(U32), axis=0)).then_inc(s_got[c // BK], 16)

        @block.vector
        def _(v):
            then = Chain(v, s["op"])
            v.wait_ge(s["first"], 16)
            then(v.tensor_scalar(F[:, :], F[:, :], 7, None, ALU.logical_shift_right))
            then(v.tensor_copy(FF[:, :], F[:, :]))
            v.wait_ge(s["iota"], 3)
            then(v.tensor_scalar(FF[:, :], FF[:, :], PI[:, 0:1], None, ALU.is_lt))
            then(v.tensor_reduce(START[:, :], FF[:, :], AX.X, ALU.add))
            then(v.scalar_tensor_tensor(START[:, :], START[:, :], -1.0, PI[:, :], ALU.add, ALU.add))
            then(v.tensor_scalar(DIAG[:, :], sh.ident[:, :], START[:, 0:1], None, ALU.mult))
            then(v.tensor_scalar(GE[:, :], ROW[:, :], START[:, 0:1], None, ALU.is_ge), s["start"])
            v.wait_ge(s["sums"], 1)
            hit = RF[:, 0].rearrange("p c m -> p (c m)").rearrange("p (c m) -> p c m", m=P)
            then(v.tensor_tensor(hit, COL[:, :].unsqueeze(2).broadcast_to([P, SCH, P]),
                                 pJ[:, :].unsqueeze(1).broadcast_to([P, SCH, P]), ALU.is_ge))
            then(v.tensor_reduce(TF[:, :], hit, AX.X, ALU.add))
            then(v.scalar_tensor_tensor(TF[:, :], TF[:, :], -1.0, COL[:, :], ALU.mult, ALU.add))
            then(v.tensor_scalar(T[:, :], TF[:, :], 1.0, None, ALU.add), s["tile"])
            flat = pB[:, :, 0:HB]
            then(v.tensor_scalar(BI[:, :].rearrange("p (a b) -> p a b", a=4), flat, -1.0, None, ALU.add))
            then(v.tensor_scalar(BF[:, :].rearrange("p (a b) -> p a b", a=4), flat, -1.0, None, ALU.add))
            norm.on_vector(v)
            for bk in range(NBK):
                c0, c1 = bk * BK, min(SCH, bk * BK + BK)
                cols = slice(c0 * P, c1 * P)
                v.wait_ge(s_got[bk], 16 * NA * (c1 - c0))
                for a in range(2):
                    v.tensor_copy(RF[:, a, c0:c1, :], RAW[:, a, c0:c1, :]).then_inc(s["float"], 1)
                for a in range(NA):
                    v.wait_ge(s["turned"], bk * NA + a + 1)
                    out = pT[(bk * NA + a) % 2][:, 0:(c1 - c0) * P]
                    if a == 0:
                        v.tensor_copy(OSRC[:, cols], out).then_inc(s["out"], 1)
                    elif a == 1:
                        v.scalar_tensor_tensor(OUT[:, 0, cols], BF[:, cols], -float(P), out, ALU.mult,
                                               ALU.add).then_inc(s["out"], 1)
                    else:
                        v.tensor_copy(OUT[:, 1, cols], out).then_inc(s["out"], 1)

        block.scalar(norm.on_scalar)

        @block.tensor
        def _(pe):
            pe.wait_ge(s["start"], 1)
            pe.matmul(pJ[:, :], sh.ones[:, :], DIAG[:, :], start=True, stop=True)
            for q in range(4):
                m = pe.matmul(pB[:, q, 0:HB], sh.ones[:, :], GE[:, q * HB:(q + 1) * HB], start=True, stop=True)
            m.then_inc(s["sums"], 1)
            for bk in range(NBK):
                for a in range(NA):
                    n = bk * NA + a
                    if n >= 2:
                        pe.wait_ge(s["out"], n - 1)
                    if a < 2:
                        pe.wait_ge(s["float"], bk * 2 + a + 1)
                    else:
                        pe.wait_ge(s_got[bk], 16 * NA * (min(SCH, (bk + 1) * BK) - bk * BK))
                    for c in range(bk * BK, min(SCH, bk * BK + BK)):
                        rows = RF[:, a, c, :] if a < 2 else RAW[:, a, c, :].bitcast(F32)
                        m = pe.transpose(pT[n % 2][:, (c - bk * BK) * P:(c - bk * BK + 1) * P], rows, sh.ident[:, :])
                    m.then_inc(s["turned"], 1)


def graph_pass(sh, tag, planned, planned_block, table, width, acc, acc_zeroed, gather_done, rounds0, keep=None, gmax=None):
    nc = sh.nc
    attend = keep is not None
    RND = SG // RINGS
    HG = GRP // 2
    BANKS = 4
    names = ["loaded", "staged", "slots_free", "onehot", "sum", "added"]
    if attend:
        names += ["turned", "copied", "ad", "z", "lr", "arg", "p", "gp"]
    s = {n: sh.sem(f"{tag}_{n}") for n in names}
    with Scope(nc) as sc:
        IDX = sc.sb(f"{tag}_IDX", [P, NS], I32)
        REL = sc.sb(f"{tag}_REL", [P, NS])
        BLK = sc.sb(f"{tag}_BLK", [1, NS], I32)
        WT = sc.sb(f"{tag}_WT", [P, NS]) if not attend else None
        STG = sc.sb(f"{tag}_STG", [P, RINGS, GRP], I32)
        G = sc.sb(f"{tag}_G", [P, RINGS, GRP, width])
        S = sc.sb(f"{tag}_S", [P, RINGS, GRP, P])
        pM = [sc.ps(f"{tag}_pM{j}", [P, 512]) for j in range(BANKS)]
        if attend:
            ST = sc.sb(f"{tag}_ST", [P, GRP, P])
            Z = sc.sb(f"{tag}_Z", [P, 2, 2, GRP, HEADS])
            L = sc.sb(f"{tag}_L", [P, 2, 2, GRP, HEADS])
            ARG = sc.sb(f"{tag}_ARG", [P, 2, GRP, HEADS])
            pT = sc.ps(f"{tag}_pT", [P, GRP, P])
            pA = sc.ps(f"{tag}_pA", [P, 2, GRP, HEADS])
        block = sc.block()
        n_loads = (3 if attend else 4) * 16

        def over_groups(eng, step):
            for r in range(RINGS):
                step(0, r)
            with eng.Fori(1, RND - 1) as it:
                for r in range(RINGS):
                    step(it, r)
            for r in range(RINGS):
                step(RND - 1, r)

        def last(rnd, r):
            return isinstance(rnd, int) and rnd * RINGS + r == SG - 1

        def first(rnd, r):
            return isinstance(rnd, int) and rnd * RINGS + r == 0

        def gathered(eng, rnd, r):
            eng.wait_ge(gather_done[r], (rnd + rounds0 + 1) * 16 * GRP)

        @block.sync
        def _(sp):
            sp.dma_start(IDX[:, :], planned[0]).then_inc(s["loaded"], 16)
            sp.dma_start(REL[:, :], planned[1]).then_inc(s["loaded"], 16)
            sp.dma_start(BLK[:, :], planned_block).then_inc(s["loaded"], 16)
            if not attend:
                sp.dma_start(WT[:, :], planned[2]).then_inc(s["loaded"], 16)

        @block.gpsimd
        def _(pool):
            pool.wait_ge(s["loaded"], n_loads)

            def stage(rnd, r):
                at_least(pool, gather_done[r], (rnd + rounds0) * 16 * GRP)
                pool.tensor_copy(STG[:, r, :], IDX[:, bass.ds((rnd * RINGS + r) * GRP, GRP)]).then_inc(s["staged"], 1)

            def gathers(rnd, r):
                k = rnd * RINGS + r
                pool.wait_ge(s["staged"], k + 1)
                at_least(pool, s["sum"], (k - RINGS + 1) * GRP)
                pool.sem_inc(s["slots_free"], 1)
                for u in range(GRP):
                    pool.indirect_dma_start(G[:, r, u, :], None, table, bass.IndirectOffsetOnAxis(
                        ap=STG[:, r, u:u + 1].bitcast(U32), axis=0)).then_inc(gather_done[r], 16)

            def step(rnd, r):
                if not last(rnd, r):
                    stage(rnd + (r + 1) // RINGS, (r + 1) % RINGS)
                gathers(rnd, r)

            stage(0, 0)
            over_groups(pool, step)

        @block.vector
        def _(v):
            v.wait_ge(s["loaded"], n_loads)
            v.wait_ge(*acc_zeroed)
            regs = [v.alloc_register(f"{tag}_v{u}") for u in range(GRP)]

            def onehot(rnd, r, u):
                j = (rnd * RINGS + r) * GRP + u
                rel = REL[:, bass.ds(j, 1)]
                if u == 0:
                    at_least(v, s["sum"], (rnd * RINGS + r - RINGS + 1) * GRP)
                if attend:
                    v.tensor_scalar(S[:, r, u, :], sh.iota[:, :], rel, None, ALU.is_equal).then_inc(s["onehot"], 1)
                else:
                    v.tensor_scalar(S[:, r, u, :], sh.iota[:, :], rel, WT[:, bass.ds(j, 1)],
                                    ALU.is_equal, ALU.mult).then_inc(s["onehot"], 1)

            def add(k, u, blk):
                j = k * GRP + u
                v.wait_ge(s["sum"], j + 1)
                at_least(v, s["added"], j)
                sums = acc[:, bass.ds(blk, 1), :].rearrange("p a d -> p (a d)")
                v.tensor_tensor(sums, pM[u % BANKS][:, 0:width], sums, ALU.add).then_inc(s["added"], 1)

            def after(rnd, r):
                return rnd + (r + 1) // RINGS, (r + 1) % RINGS

            def step_attend(rnd, r):
                k = rnd * RINGS + r
                par = r % 2
                before = not first(rnd, r)
                if before:
                    blk = load_registers(v, regs, BLK, (k - 1) * GRP)

                def next_onehots(us):
                    if not last(rnd, r):
                        for u in us:
                            onehot(*after(rnd, r), u)

                def add_before(u):
                    if before:
                        add(k - 1, u, blk[u])

                v.wait_ge(s["ad"], k + 1)
                gathered(v, rnd, r)
                v.tensor_tensor(Z[:, par, 0], G[:, r, :, D:D + HEADS], pA[:, par], ALU.add).then_inc(s["z"], 1)
                v.tensor_tensor(Z[:, par, 1], gmax[:, :].unsqueeze(1).broadcast_to([P, GRP, HEADS]), pA[:, par],
                                ALU.add).then_inc(s["z"], 1)
                next_onehots((0, 1))
                v.wait_ge(s["z"], k * 2 + 2)
                v.scalar_tensor_tensor(L[:, par].rearrange("p a u h -> p (a u h)"), Z[:, par].rearrange("p a u h -> p (a u h)"),
                                       SLOPE, Z[:, par].rearrange("p a u h -> p (a u h)"),
                                       ALU.mult, ALU.max).then_inc(s["lr"], 1)
                next_onehots((2, 3))
                v.wait_ge(s["lr"], k + 1)
                v.tensor_tensor(ARG[:, par], L[:, par, 0], L[:, par, 1], ALU.subtract).then_inc(s["arg"], 1)
                for u in range(HG):
                    add_before(u)
                    next_onehots((HG + u,))
                v.wait_ge(s["p"], k + 1)
                for q in range(HG):
                    rows = G[:, r, 2 * q:2 * q + 2, 0:D].rearrange("p u (h q) -> p u h q", h=HEADS)
                    fac = G[:, r, 2 * q:2 * q + 2, D:D + HEADS].unsqueeze(3).broadcast_to([P, 2, HEADS, D // HEADS])
                    v.tensor_tensor(rows, rows, fac, ALU.mult).then_inc(s["gp"], 1)
                    add_before(HG + q)

            def step_weighted(rnd, r):
                blk = load_registers(v, regs, BLK, (rnd * RINGS + r) * GRP)
                for u in range(GRP):
                    if not last(rnd, r):
                        onehot(*after(rnd, r), u)
                    add(rnd * RINGS + r, u, blk[u])

            for u in range(GRP):
                onehot(0, 0, u)
            if attend:
                over_groups(v, step_attend)
                blk = load_registers(v, regs, BLK, (SG - 1) * GRP)
                for u in range(GRP):
                    add(SG - 1, u, blk[u])
            else:
                over_groups(v, step_weighted)
            v.wait_ge(s["added"], NS)

        if attend:
            @block.scalar
            def _(a):
                def copy(k, hf):
                    a.wait_ge(s["turned"], 2 * k + hf + 1)
                    at_least(a, s["ad"], k)
                    sl = slice(hf * HG, (hf + 1) * HG)
                    a.activation(ST[:, sl, :], pT[:, sl, :], ACT.Copy).then_inc(s["copied"], 1)

                def step(rnd, r):
                    k = rnd * RINGS + r
                    if not last(rnd, r):
                        copy(k + 1, 0)
                    a.wait_ge(s["arg"], k + 1)
                    a.activation(G[:, r, :, D:D + HEADS], ARG[:, r % 2], ACT.Exp).then_inc(s["p"], 1)
                    if not last(rnd, r):
                        copy(k + 1, 1)

                copy(0, 0)
                copy(0, 1)
                over_groups(a, step)

        @block.tensor
        def _(pe):
            regs = [pe.alloc_register(f"{tag}_p{u}") for u in range(GRP)] if attend else None

            def transposes(k, r, hf):
                at_least(pe, s["copied"], 2 * k - 1 + hf)
                pe.wait_ge(s["onehot"], k * GRP + (hf + 1) * HG)
                for u in range(hf * HG, (hf + 1) * HG):
                    m = pe.transpose(pT[:, u, :], S[:, r, u, :], sh.ident[:, :])
                m.then_inc(s["turned"], 1)

            def spread(k, r):
                blk = load_registers(pe, regs, BLK, k * GRP)
                at_least(pe, s["z"], 2 * k - 2)
                for u in range(GRP):
                    if u % HG == 0:
                        pe.wait_ge(s["copied"], 2 * k + u // HG + 1)
                    nodes = keep[:, bass.ds(blk[u], 1), HEADS:2 * HEADS].rearrange("p a h -> p (a h)")
                    m = pe.matmul(pA[:, r % 2, u, :], ST[:, u, :], nodes, start=True, stop=True)
                m.then_inc(s["ad"], 1)

            def sums(k, r, us):
                for u in us:
                    j = k * GRP + u
                    if attend and u % 2 == 0:
                        pe.wait_ge(s["gp"], k * HG + u // 2 + 1)
                    if not attend and u == 0:
                        pe.wait_ge(s["onehot"], (k + 1) * GRP)
                    at_least(pe, s["added"], j + 1 - BANKS)
                    pe.matmul(pM[u % BANKS][:, 0:width], S[:, r, u, :], G[:, r, u, :], start=True,
                              stop=True).then_inc(s["sum"], 1)

            def step_attend(rnd, r):
                k = rnd * RINGS + r
                if not last(rnd, r):
                    transposes(k + 1, (r + 1) % RINGS, 0)
                if not first(rnd, r):
                    sums(k - 1, (r - 1) % RINGS, range(HG, GRP))
                if not last(rnd, r):
                    transposes(k + 1, (r + 1) % RINGS, 1)
                    spread(k + 1, (r + 1) % RINGS)
                sums(k, r, range(HG))

            def step_weighted(rnd, r):
                gathered(pe, rnd, r)
                sums(rnd * RINGS + r, r, range(GRP))

            pe.wait_ge(s["loaded"], n_loads)
            if attend:
                transposes(0, 0, 0)
                transposes(0, 0, 1)
                spread(0, 0)
                over_groups(pe, step_attend)
                sums(SG - 1, RINGS - 1, range(HG, GRP))
            else:
                over_groups(pe, step_weighted)


def table_maximum(sh, tag, keep, col, gmax):
    nc = sh.nc
    s = {n: sh.sem(f"{tag}_{n}") for n in ("max", "turned", "diag", "spread", "done")}
    with Scope(nc) as sc:
        M = sc.sb(f"{tag}_M", [P, HEADS])
        MH = sc.sb(f"{tag}_MH", [HEADS, 1])
        DG = sc.sb(f"{tag}_DG", [HEADS, HEADS])
        pM = sc.ps(f"{tag}_pM", [HEADS, P])
        pG = sc.ps(f"{tag}_pG", [P, HEADS])
        block = sc.block()

        @block.vector
        def _(v):
            v.tensor_reduce(M[:, :], keep[:, 0:NB - 1, col:col + HEADS].rearrange("p i h -> p h i"),
                            AX.X, ALU.max).then_inc(s["max"], 1)
            v.wait_ge(s["max"], 1)
            v.tensor_tensor(M[0:LAST, :], M[0:LAST, :], keep[0:LAST, NB - 1, col:col + HEADS],
                            ALU.max).then_inc(s["max"], 1)
            v.wait_ge(s["turned"], 1)
            v.tensor_reduce(MH[:, :], pM[:, :], AX.X, ALU.max).then_inc(s["diag"], 1)
            v.wait_ge(s["diag"], 1)
            v.tensor_scalar(DG[:, :], sh.ident[0:HEADS, 0:HEADS], MH[:, 0:1], None, ALU.mult).then_inc(s["diag"], 1)
            v.wait_ge(s["spread"], 1)
            v.tensor_copy(gmax[:, :], pG[:, :]).then_inc(s["done"], 1)
            v.wait_ge(s["done"], 1)

        @block.tensor
        def _(pe):
            pe.wait_ge(s["max"], 2)
            pe.transpose(pM[:, :], M[:, :], sh.ident[:, :]).then_inc(s["turned"], 1)
            pe.wait_ge(s["diag"], 2)
            pe.matmul(pG[:, :], sh.ones[0:HEADS, :], DG[:, :], start=True, stop=True).then_inc(s["spread"], 1)


def store_adst(sh, tag, keep, col, adst):
    s_o = sh.sem(f"{tag}_stored")
    with Scope(sh.nc) as sc:
        block = sc.block()

        @block.sync
        def _(sp):
            sp.dma_start(adst.rearrange("(i p) h -> p i h", p=P), keep[:, :, col:col + HEADS]).then_inc(s_o, 16)
            sp.wait_ge(s_o, 16)


def self_factor(sh, v, a, s, keep, col, gmax, Z, PS):
    def on_vector():
        av, dv = keep[:, :, col:col + HEADS], keep[:, :, col + HEADS:col + 2 * HEADS]
        v.tensor_tensor(Z[:, 0], av, dv, ALU.add).then_inc(s, 1)
        v.tensor_tensor(Z[:, 1], gmax[:, :].unsqueeze(1).broadcast_to([P, NB, HEADS]), dv, ALU.add).then_inc(s, 1)
        v.wait_ge(s, 2)
        flat = Z[:, :, :, :].rearrange("p a i h -> p (a i h)")
        v.scalar_tensor_tensor(flat, flat, SLOPE, flat, ALU.mult, ALU.max).then_inc(s, 1)
        v.wait_ge(s, 3)
        v.tensor_tensor(PS[:, :, :], Z[:, 0], Z[:, 1], ALU.subtract).then_inc(s, 1)
    def on_scalar():
        a.wait_ge(s, 4)
        a.activation(PS[:, :, :], PS[:, :, :], ACT.Exp).then_inc(s, 1)
    return on_vector, on_scalar


def finish_attention(sh, tag, acc, table, keep, gmax, bias):
    nc = sh.nc
    s = {n: sh.sem(f"{tag}_{n}") for n in ("self", "bias", "op", "own")}
    s_h = [sh.sem(f"{tag}_h{j}") for j in range(2)]
    OPS = 4
    RND = NB // U7
    with Scope(nc) as sc:
        Z = sc.sb(f"{tag}_Z", [P, 2, NB, HEADS])
        PS = sc.sb(f"{tag}_PS", [P, NB, HEADS])
        B = sc.sb(f"{tag}_B", [P, D])
        H = sc.sb(f"{tag}_H", [P, 2, U7, D])
        block = sc.block()

        @block.sync
        def _(sp):
            sp.dma_start(B[:, :], bcast_rows(bias)).then_inc(s["bias"], 16)
            for it in range(RND):
                if it >= 2:
                    at_least(sp, s["own"], it - 1)
                sp.dma_start(H[:, it % 2], table[it * U7 * P:(it + 1) * U7 * P, 0:D].rearrange(
                    "(u p) d -> p u d", p=P)).then_inc(s_h[it % 2], 16)

        @block.scalar
        def _(a):
            self_factor(sh, None, a, s["self"], keep, 0, gmax, Z, PS)[1]()

        @block.vector
        def _(v):
            self_factor(sh, v, None, s["self"], keep, 0, gmax, Z, PS)[0]()
            v.wait_ge(s["self"], 5)
            v.wait_ge(s["bias"], 16)

            def heads(ap):
                return ap.rearrange("p u (h q) -> p u h q", h=HEADS)

            def spread(ap):
                return ap.unsqueeze(3).broadcast_to([P, U7, HEADS, D // HEADS])

            v.tensor_tensor(acc[:, :, D:D + HEADS], acc[:, :, D:D + HEADS], PS[:, :, :], ALU.add).then_inc(s["self"], 1)
            v.wait_ge(s["self"], 6)
            v.reciprocal(acc[:, :, D:D + HEADS], acc[:, :, D:D + HEADS]).then_inc(s["self"], 1)
            v.wait_ge(s["self"], 7)

            def stage(it, n):
                blk = slice(it * U7, it * U7 + U7)
                sums = acc[:, blk, 0:D]
                if n == 0:
                    at_least(v, s_h[it % 2], (it // 2 + 1) * 16)
                    h = H[:, it % 2]
                    v.tensor_tensor(heads(h), heads(h), spread(PS[:, blk, :]), ALU.mult).then_inc(s["op"], 1)
                elif n == 1:
                    v.tensor_tensor(sums, sums, H[:, it % 2], ALU.add).then_inc(s["own"], 1)
                elif n == 2:
                    at_least(v, s["own"], it + 1)
                    v.tensor_tensor(heads(sums), heads(sums), spread(acc[:, blk, D:D + HEADS]), ALU.mult).then_inc(s["op"], 1)
                elif n == 3:
                    v.tensor_tensor(sums, sums, B[:, :].unsqueeze(1).broadcast_to([P, U7, D]), ALU.add).then_inc(s["op"], 1)
                else:
                    v.scalar_tensor_tensor(sh.X[:, blk, :], sums, 0.0, sh.X[:, blk, :], ALU.max, ALU.add).then_inc(s["op"], 1)

            for it in range(RND):
                for n in range(OPS + 1):
                    if n in (1, 3, 4):
                        at_least(v, s["op"], it * OPS + (1 if n == 1 else n - 1))
                    stage(it, n)
            v.wait_ge(s["op"], OPS * RND)


def finish_weighted(sh, tag, acc, stats, w1t, w2t, b1, b2):
    nc = sh.nc
    s = {n: sh.sem(f"{tag}_{n}") for n in ("w", "bias", "xn", "tr", "xt", "side", "mm", "op", "squared", "norm")}
    OPS = 5 + U7
    with Scope(nc) as sc:
        W = sc.sb(f"{tag}_W", [P, 2, KC, D])
        B = sc.sb(f"{tag}_B", [P, 2, D])
        XR = sc.sb(f"{tag}_XR", [P, U7, D])
        SR = sc.sb(f"{tag}_SR", [P, U7, D])
        XT = sc.sb(f"{tag}_XT", [P, 2, 2, KC, P])
        O = sc.sb(f"{tag}_O", [P, U7, D])
        Q = sc.sb(f"{tag}_Q", [P, U7, D])
        NR = sc.sb(f"{tag}_NR", [P, U7])
        pO = sc.ps(f"{tag}_pO", [P, 4, 2, D])
        pT = [sc.ps(f"{tag}_pT{j}", [P, 2, KC, P]) for j in range(2)]
        block = sc.block()

        def out_of(u):
            return pO[:, u // 2, u % 2, :]

        @block.sync
        def _(sp):
            for j, w in enumerate((w1t, w2t)):
                sp.dma_start(W[:, j], w.rearrange("(c k) n -> k c n", k=P)).then_inc(s["w"], 16)
            for j, b in enumerate((b1, b2)):
                sp.dma_start(B[:, j, :], bcast_rows(b)).then_inc(s["bias"], 16)

        @block.scalar
        def _(a):
            def square(it):
                a.wait_ge(s["op"], it * OPS + 2)
                a.activation(Q[:, :, :], O[:, :, :], ACT.Square).then_inc(s["squared"], 1)

            def root(it):
                a.wait_ge(s["op"], it * OPS + 3)
                a.activation(NR[:, :], NR[:, :], ACT.Sqrt).then_inc(s["norm"], 1)

            @every_round(a)
            def _(it):
                for u in range(U7):
                    if u == 2 and not (isinstance(it, int) and it == 0):
                        square(it - 1)
                        root(it - 1)
                    at_least(a, s["tr"], it * U7 + u + 1)
                    if u >= 2:
                        at_least(a, s["mm"], it * U7 + u - 1)
                    else:
                        at_least(a, s["mm"], it * U7)
                    a.activation(XT[:, u % 2], pT[u % 2][:, :, :, :], ACT.Copy).then_inc(s["xt"], 1)

            square(NB // U7 - 1)
            root(NB // U7 - 1)

        @block.tensor
        def _(pe):
            def turn(it, u):
                at_least(pe, s["xn"], it * U7 + u + 1)
                at_least(pe, s["xt"], it * U7 + (u - 1 if u >= 2 else 0))
                at_least(pe, s["side"], it * U7 + u + 1)
                for j, rows in enumerate((XR, SR)):
                    for c in range(KC):
                        m = pe.transpose(pT[u % 2][:, j, c, :], rows[:, u, c * P:(c + 1) * P], sh.ident[:, :])
                m.then_inc(s["tr"], 1)

            pe.wait_ge(s["w"], 32)
            @every_round(pe)
            def _(it):
                turn(it, 0)
                at_least(pe, s["op"], (it - 1) * OPS + 1)
                for u in range(U7):
                    if u + 1 < U7:
                        turn(it, u + 1)
                    at_least(pe, s["xt"], it * U7 + u + 1)
                    for j in range(2):
                        for c in range(KC):
                            m = pe.matmul(out_of(u), XT[:, u % 2, j, c, :], W[:, j, c, :],
                                          start=(j == 0 and c == 0), stop=(j == 1 and c == KC - 1))
                    m.then_inc(s["mm"], 1)

        @block.vector
        def _(v):
            v.wait_ge(s["bias"], 32)
            v.tensor_tensor(B[:, 0, :], B[:, 0, :], B[:, 1, :], ALU.add).then_inc(s["bias"], 1)
            v.wait_ge(s["bias"], 33)
            def inputs(it):
                for u in range(U7):
                    i = it * U7 + u
                    at_least(v, s["tr"], (it - 1) * U7 + u + 1)
                    v.tensor_scalar(XR[:, u, :], sh.X[:, bass.ds(i, 1), :].rearrange("p a d -> p (a d)"),
                                    stats[:, bass.ds(i, 1), 0:1].rearrange("p a b -> p (a b)"),
                                    stats[:, bass.ds(i, 1), 1:2].rearrange("p a b -> p (a b)"),
                                    ALU.subtract, ALU.mult).then_inc(s["xn"], 1)
                for u in range(U7):
                    v.wait_ge(s["xn"], it * U7 + u + 1)
                    v.scalar_tensor_tensor(SR[:, u, :], XR[:, u, :], 1.0,
                                           acc[:, bass.ds(it * U7 + u, 1), :].rearrange("p a d -> p (a d)"),
                                           ALU.add, ALU.mult).then_inc(s["side"], 1)

            def outputs(it):
                at_least(v, s["op"], it * OPS)
                at_least(v, s["mm"], it * U7 + U7)
                pall = pO[:, :, :, :].rearrange("p a b d -> p (a b) d")[:, 0:U7, :]
                v.tensor_tensor(O[:, :, :], pall, B[:, 0, :].unsqueeze(1).broadcast_to([P, U7, D]), ALU.add).then_inc(s["op"], 1)
                at_least(v, s["op"], it * OPS + 1)
                v.scalar_tensor_tensor(O[:, :, :], O[:, :, :], SLOPE, O[:, :, :], ALU.mult, ALU.max).then_inc(s["op"], 1)
                at_least(v, s["op"], it * OPS + 2)
                v.wait_ge(s["squared"], it + 1)
                v.tensor_reduce(NR[:, :], Q[:, :, :], AX.X, ALU.add).then_inc(s["op"], 1)
                v.wait_ge(s["norm"], it + 1)
                v.tensor_scalar(NR[:, :], NR[:, :], 1e-12, None, ALU.max).then_inc(s["op"], 1)
                v.wait_ge(s["op"], it * OPS + 4)
                v.reciprocal(NR[:, :], NR[:, :]).then_inc(s["op"], 1)
                v.wait_ge(s["op"], it * OPS + 5)
                for u in range(U7):
                    row = sh.X[:, bass.ds(it * U7 + u, 1), :].rearrange("p a d -> p (a d)")
                    v.scalar_tensor_tensor(row, O[:, u, :], NR[:, u:u + 1], row, ALU.mult, ALU.add).then_inc(s["op"], 1)

            inputs(0)

            @every_round(v)
            def _(it):
                if not (isinstance(it, int) and it == NB // U7 - 1):
                    inputs(it + 1)
                outputs(it)

            v.wait_ge(s["op"], OPS * (NB // U7))


def free_edges_pass(sh, tag, ew, src_t, dst_t, table, adst, gmax, keep, gather_done, rounds0, b_gat, gamma, beta, scores):
    nc = sh.nc
    EX = 4
    VC = HEADS * EX + HEADS
    NA = 25
    RND = NGRF // RINGS
    MVR = 4
    HG = GRP // 2
    SEL = 2
    SENT = (2 * GRP - SEL) * 16
    base = rounds0 * 16 * GRP
    picked = slice(GRP - SEL, GRP)
    s = {n: sh.sem(f"{tag}_{n}") for n in ("loaded", "idx", "staged", "slots_free", "lo", "hi",
                                           "turned", "copied", "ad", "sel", "z", "arg", "p", "val", "mv", "packed",
                                           "mm", "self", "par", "fin", "var", "sq")}
    with Scope(nc) as sc:
        SRC = sc.sb(f"{tag}_SRC", [P, NTF], I32)
        DST = sc.sb(f"{tag}_DST", [P, NTF], I32)
        DC = sc.sb(f"{tag}_DC", [P, NTF], I32)
        TI = sc.sb(f"{tag}_TI", [P, NTF], I32)
        LO = sc.sb(f"{tag}_LO", [P, NTF])
        HI = sc.sb(f"{tag}_HI", [P, NTF])
        STG = sc.sb(f"{tag}_STG", [P, RINGS, 2, GRP], I32)
        G = sc.sb(f"{tag}_G", [P, RINGS, GRP, VC])
        A = sc.sb(f"{tag}_A", [P, RINGS, GRP, HEADS])
        OL = sc.sb(f"{tag}_OL", [P, RINGS, GRP, P])
        OH = sc.sb(f"{tag}_OH", [P, RINGS, GRP, NB])
        LT = sc.sb(f"{tag}_LT", [P, SEL, P])
        ADST = sc.sb(f"{tag}_ADST", [P, NB * HEADS])
        MA = sc.sb(f"{tag}_MA", [P, SEL, NB, HEADS])
        Z = sc.sb(f"{tag}_Z", [P, 2, 2, GRP, HEADS])
        ARG = sc.sb(f"{tag}_ARG", [P, 2, GRP, HEADS])
        V = sc.sb(f"{tag}_V", [P, 2, GRP, VC])
        MV = sc.sb(f"{tag}_MV", [P, MVR, NB, VC])
        ZS = sc.sb(f"{tag}_ZS", [P, 2, NB, HEADS])
        PS = sc.sb(f"{tag}_PS", [P, NB, HEADS])
        R = sc.sb(f"{tag}_R", [P, NB, HEADS * EX])
        R2 = sc.sb(f"{tag}_R2", [P, NB, HEADS * EX])
        DN = sc.sb(f"{tag}_DN", [P, NB, HEADS])
        MU = sc.sb(f"{tag}_MU", [P, NB])
        VR = sc.sb(f"{tag}_VR", [P, NB])
        PAR = sc.sb(f"{tag}_PAR", [P, 3, HEADS * EX])
        pS = [sc.ps(f"{tag}_pS{j}", [P, 512]) for j in range(2)]
        pT = sc.ps(f"{tag}_pT", [P, SEL, P])
        pA = sc.ps(f"{tag}_pA", [P, SEL, NB, HEADS])
        block = sc.block()
        parts = [(0, NA), (NA, NB - NA)]

        def over_groups(eng, step):
            for r in range(RINGS):
                step(0, r)
            with eng.Fori(1, RND - 1) as it:
                for r in range(RINGS):
                    step(it, r)
            for r in range(RINGS):
                step(RND - 1, r)

        @block.sync
        def _(sp):
            sp.dma_start(SRC[:, :], src_t).then_inc(s["loaded"], 16)
            sp.dma_start(DST[:, :], dst_t).then_inc(s["loaded"], 16)
            for j, w in enumerate((b_gat, gamma, beta)):
                sp.dma_start(PAR[:, j, :], bcast_rows(w)).then_inc(s["par"], 16)
            ew.fetch(sp)

        @block.gpsimd
        def _(pool):
            pool.wait_ge(s["idx"], 6)

            def stage(rnd, r):
                k = rnd * RINGS + r
                at_least(pool, gather_done[r], base + rnd * SENT)
                at_least(pool, s["val"], 2 * (k - RINGS + 1))
                pool.tensor_copy(STG[:, r, 0, :], SRC[:, bass.ds(k * GRP, GRP)]).then_inc(s["staged"], 1)
                pool.tensor_copy(STG[:, r, 1, :], DC[:, bass.ds(k * GRP, GRP)]).then_inc(s["staged"], 1)

            def gathers(rnd, r):
                k = rnd * RINGS + r
                pool.wait_ge(s["staged"], 2 * k + 2)
                pool.sem_inc(s["slots_free"], 1)
                for u in range(GRP):
                    pool.indirect_dma_start(G[:, r, u, :], None, table, bass.IndirectOffsetOnAxis(
                        ap=STG[:, r, 0, u:u + 1].bitcast(U32), axis=0)).then_inc(gather_done[r], 16)
                    if u < GRP - SEL:
                        pool.indirect_dma_start(A[:, r, u, :], None, adst, bass.IndirectOffsetOnAxis(
                            ap=STG[:, r, 1, u:u + 1].bitcast(U32), axis=0)).then_inc(gather_done[r], 16)

            def step(rnd, r):
                if not (isinstance(rnd, int) and rnd * RINGS + r == NGRF - 1):
                    stage(rnd + (r + 1) // RINGS, (r + 1) % RINGS)
                gathers(rnd, r)

            stage(0, 0)
            over_groups(pool, step)

        @block.vector
        def _(v):
            v.tensor_copy(ADST[:, :].rearrange("p (i h) -> p i h", h=HEADS),
                          keep[:, :, EX * HEADS + HEADS:EX * HEADS + 2 * HEADS]).then_inc(s["packed"], 1)
            v.wait_ge(s["loaded"], 32)
            v.tensor_scalar(SRC[:, :], SRC[:, :], N - 1, None, ALU.min).then_inc(s["idx"], 1)
            v.tensor_scalar(DC[:, :], DST[:, :], N - 1, None, ALU.min).then_inc(s["idx"], 1)
            v.tensor_scalar(TI[:, :], DST[:, :], P - 1, None, ALU.bitwise_and).then_inc(s["idx"], 1)
            v.wait_ge(s["idx"], 3)
            v.tensor_copy(LO[:, :], TI[:, :]).then_inc(s["idx"], 1)
            v.wait_ge(s["idx"], 4)
            v.tensor_scalar(TI[:, :], DST[:, :], 7, None, ALU.logical_shift_right).then_inc(s["idx"], 1)
            v.wait_ge(s["idx"], 5)
            v.tensor_copy(HI[:, :], TI[:, :]).then_inc(s["idx"], 1)
            v.wait_ge(s["idx"], 6)

            def onehots(k, r, us):
                for u in us:
                    v.tensor_scalar(OL[:, r, u, :], sh.iota[:, :], LO[:, bass.ds(k * GRP + u, 1)], None,
                                    ALU.is_equal).then_inc(s["lo"], 1)

            def onehots_hi(k, r):
                v.tensor_tensor(OH[:, r], sh.iota[:, 0:NB].unsqueeze(1).broadcast_to([P, GRP, NB]),
                                HI[:, bass.ds(k * GRP, GRP)].unsqueeze(2).broadcast_to([P, GRP, NB]),
                                ALU.is_equal).then_inc(s["hi"], 1)

            def mask(k, r):
                v.wait_ge(s["ad"], k + 1)
                v.wait_ge(s["hi"], k + 1)
                v.tensor_tensor(MA[:, :, :, :], pA[:, :, :, :], OH[:, r, picked, :].unsqueeze(3).broadcast_to(
                    [P, SEL, NB, HEADS]), ALU.mult).then_inc(s["sel"], 1)

            def pick(k, r):
                v.wait_ge(s["sel"], 2 * k + 1)
                v.tensor_reduce(A[:, r, picked, :], MA[:, :, :, :].rearrange("p u i h -> p u h i"), AX.X,
                                ALU.add).then_inc(s["sel"], 1)

            def step(rnd, r):
                k = rnd * RINGS + r
                par = r % 2
                after = not (isinstance(k, int) and k == NGRF - 1)
                ra = (r + 1) % RINGS
                v.wait_ge(gather_done[r], base + (rnd + 1) * SENT)
                v.wait_ge(s["sel"], 2 * k + 2)
                v.tensor_tensor(Z[:, par, 0], G[:, r, :, EX * HEADS:VC], A[:, r, :, :], ALU.add).then_inc(s["z"], 1)
                v.tensor_tensor(Z[:, par, 1], gmax[:, :].unsqueeze(1).broadcast_to([P, GRP, HEADS]), A[:, r, :, :],
                                ALU.add).then_inc(s["z"], 1)
                if after:
                    at_least(v, s["mm"], (k + 2 - RINGS) * GRP)
                    onehots(k + 1, ra, picked_first[:HG])
                v.wait_ge(s["z"], k * 3 + 2)
                zf = Z[:, par].rearrange("p a u h -> p (a u h)")
                v.scalar_tensor_tensor(zf, zf, SLOPE, zf, ALU.mult, ALU.max).then_inc(s["z"], 1)
                if after:
                    onehots(k + 1, ra, picked_first[HG:])
                v.wait_ge(s["z"], k * 3 + 3)
                v.tensor_tensor(ARG[:, par], Z[:, par, 0], Z[:, par, 1], ALU.subtract).then_inc(s["arg"], 1)
                if after:
                    onehots_hi(k + 1, ra)
                v.wait_ge(s["p"], k + 1)
                v.tensor_tensor(V[:, par, :, 0:EX * HEADS].rearrange("p u (h q) -> p u h q", h=HEADS),
                                G[:, r, :, 0:EX * HEADS].rearrange("p u (h q) -> p u h q", h=HEADS),
                                ARG[:, par].unsqueeze(3).broadcast_to([P, GRP, HEADS, EX]), ALU.mult).then_inc(s["val"], 1)
                v.tensor_copy(V[:, par, :, EX * HEADS:VC], ARG[:, par]).then_inc(s["val"], 1)
                v.wait_ge(s["val"], 2 * k + 2)
                for u in range(GRP):
                    if after and u == GRP - 2:
                        mask(k + 1, ra)
                    if after and u == GRP - 1:
                        pick(k + 1, ra)
                    at_least(v, s["mm"], k * GRP + u - MVR + 1)
                    v.tensor_tensor(MV[:, u % MVR], OH[:, r, u, :].unsqueeze(2).broadcast_to([P, NB, VC]),
                                    V[:, par, u, :].unsqueeze(1).broadcast_to([P, NB, VC]), ALU.mult).then_inc(s["mv"], 1)

            picked_first = list(range(GRP - SEL, GRP)) + list(range(GRP - SEL))
            onehots(0, 0, picked_first)
            onehots_hi(0, 0)
            mask(0, 0)
            pick(0, 0)
            over_groups(v, step)

            self_factor(sh, v, None, s["self"], keep, EX * HEADS, gmax, ZS, PS)[0]()
            v.wait_ge(s["self"], 5)
            v.wait_ge(s["mm"], NTF)
            v.wait_ge(s["par"], 48)

            then = Chain(v, s["fin"])

            def heads(ap):
                return ap.rearrange("p i (h q) -> p i h q", h=HEADS)

            def all16(ap, j):
                return ap[:, j, :].unsqueeze(1).broadcast_to([P, NB, EX * HEADS])

            def per_head(ap, m=NB):
                return ap.unsqueeze(3).broadcast_to([P, m, HEADS, EX])

            then(v.tensor_tensor(heads(R[:, :, :]), heads(keep[:, :, 0:EX * HEADS]), per_head(PS[:, :, :]), ALU.mult))
            for j, (b0, m) in enumerate(parts):
                sums = pS[j][:, 0:m * VC].rearrange("p (i c) -> p i c", c=VC)
                then(v.tensor_tensor(DN[:, b0:b0 + m, :], PS[:, b0:b0 + m, :], sums[:, :, EX * HEADS:VC], ALU.add))
                then(v.tensor_tensor(R[:, b0:b0 + m, :], R[:, b0:b0 + m, :], sums[:, :, 0:EX * HEADS], ALU.add))
            then(v.reciprocal(DN[:, :, :], DN[:, :, :]))
            then(v.tensor_tensor(heads(R[:, :, :]), heads(R[:, :, :]), per_head(DN[:, :, :]), ALU.mult))
            then(v.tensor_tensor(R[:, :, :], R[:, :, :], all16(PAR, 0), ALU.add))
            then(v.tensor_reduce(MU[:, :], R[:, :, :], AX.X, ALU.add))
            then(v.tensor_scalar(MU[:, :], MU[:, :], 1.0 / (EX * HEADS), None, ALU.mult))
            wide = [P, NB, EX * HEADS]
            then(v.tensor_tensor(R[:, :, :], R[:, :, :], MU[:, :].unsqueeze(2).broadcast_to(wide), ALU.subtract))
            then(v.tensor_tensor(R2[:, :, :], R[:, :, :], R[:, :, :], ALU.mult))
            then(v.tensor_reduce(VR[:, :], R2[:, :, :], AX.X, ALU.add))
            then(v.tensor_scalar(VR[:, :], VR[:, :], 1.0 / (EX * HEADS), EPS, ALU.mult, ALU.add), s["var"])
            v.wait_ge(s["sq"], 1)
            then(v.reciprocal(VR[:, :], VR[:, :]))
            then(v.tensor_tensor(R[:, :, :], R[:, :, :], VR[:, :].unsqueeze(2).broadcast_to(wide), ALU.mult))
            then(v.tensor_tensor(R[:, :, :], R[:, :, :], all16(PAR, 1), ALU.mult))
            then(v.tensor_tensor(R[:, :, :], R[:, :, :], all16(PAR, 2), ALU.add))
            then(v.tensor_reduce(scores[:, :, :], R[:, :, :].rearrange("p i (h q) -> p i q h", h=HEADS), AX.X, ALU.add))
            then(v.tensor_scalar(scores[:, :, :], scores[:, :, :], 1.0 / HEADS, None, ALU.mult))

        @block.scalar
        def _(a):
            def copy(k):
                a.wait_ge(s["turned"], k + 1)
                at_least(a, s["ad"], k)
                a.activation(LT[:, :, :], pT[:, :, :], ACT.Copy).then_inc(s["copied"], 1)

            def step(rnd, r):
                k = rnd * RINGS + r
                par = r % 2
                a.wait_ge(s["arg"], k + 1)
                a.activation(ARG[:, par], ARG[:, par], ACT.Exp).then_inc(s["p"], 1)
                if not (isinstance(k, int) and k == NGRF - 1):
                    copy(k + 1)

            copy(0)

            over_groups(a, step)
            self_factor(sh, None, a, s["self"], keep, EX * HEADS, gmax, ZS, PS)[1]()
            a.wait_ge(s["var"], 1)
            a.activation(VR[:, :], VR[:, :], ACT.Sqrt).then_inc(s["sq"], 1)

        @block.tensor
        def _(pe):
            def turn(k, r):
                at_least(pe, s["copied"], k)
                pe.wait_ge(s["lo"], k * GRP + SEL)
                for j in range(SEL):
                    m = pe.transpose(pT[:, j, :], OL[:, r, GRP - SEL + j, :], sh.ident[:, :])
                m.then_inc(s["turned"], 1)

            def spread(k):
                pe.wait_ge(s["copied"], k + 1)
                at_least(pe, s["sel"], 2 * k - 1)
                for j in range(SEL):
                    m = pe.matmul(pA[:, j].rearrange("p i h -> p (i h)"), LT[:, j, :],
                                  ADST[:, :], start=True, stop=True)
                m.then_inc(s["ad"], 1)

            def step(rnd, r):
                k = rnd * RINGS + r
                last = isinstance(k, int) and k == NGRF - 1
                for u in range(GRP):
                    if not last and u == 1:
                        turn(k + 1, (r + 1) % RINGS)
                    if not last and u == 3:
                        spread(k + 1)
                    if u == 0:
                        pe.wait_ge(s["lo"], (k + 1) * GRP)
                    pe.wait_ge(s["mv"], k * GRP + u + 1)
                    for j, (b0, m) in enumerate(parts):
                        mm = pe.matmul(pS[j][:, 0:m * VC], OL[:, r, u, :],
                                       MV[:, u % MVR, b0:b0 + m, :].rearrange("p i c -> p (i c)"),
                                       start=(isinstance(k, int) and k == 0 and u == 0), stop=(last and u == GRP - 1),
                                       skip_group_check=True)
                    mm.then_inc(s["mm"], 1)

            turn(0, 0)
            pe.wait_ge(s["packed"], 1)
            spread(0)
            over_groups(pe, step)


def route(sh, tag, E, logits, weights, pos, pos_get, expert_of):
    nc = sh.nc
    J = TOP * NB
    NT = tiles_of(E)
    s = {n: sh.sem(f"{tag}_{n}") for n in ("iota", "op", "diff", "onehots", "exp", "mm")}
    with Scope(nc) as sc:
        REV = sc.sb(f"{tag}_REV", [P, E])
        DUMP = sc.sb(f"{tag}_DUMP", [P, TOP])
        NV = sc.sb(f"{tag}_NV", [P, 1])
        M = sc.sb(f"{tag}_M", [P, TOP, NB])
        K = sc.sb(f"{tag}_K", [P, NB])
        DD = sc.sb(f"{tag}_DD", [P, NB])
        OH = sc.sb(f"{tag}_OH", [P, TOP, NB, E])
        TOT = sc.sb(f"{tag}_TOT", [P, J, E])
        INC = sc.sb(f"{tag}_INC", [P, J, E])
        L2, Q = TOT[:, 0:NB, :], INC[:, 0:NB, :]
        TI = sc.sb(f"{tag}_TI", [P, E], I32)
        TF = sc.sb(f"{tag}_TF", [P, E])
        CUM = sc.sb(f"{tag}_CUM", [P, E])
        BASE = sc.sb(f"{tag}_BASE", [P, E])
        PF = sc.sb(f"{tag}_PF", [P, J])
        EF = sc.sb(f"{tag}_EF", [1, NT])
        pW = sc.ps(f"{tag}_pW", [P, TOP, 512])
        pC = sc.ps(f"{tag}_pC", [P, TOP, 512])
        block = sc.block()

        @block.gpsimd
        def _(pool):
            pool.iota(DUMP[:, :], [[P, TOP]], base=ROWS, channel_multiplier=1,
                      allow_small_or_imprecise_dtypes=True).then_inc(s["iota"], 1)

        @block.scalar
        def _(a):
            a.wait_ge(s["diff"], 1)
            a.activation(DD[:, :], DD[:, :], ACT.Exp).then_inc(s["exp"], 1)

        @block.tensor
        def _(pe):
            pe.wait_ge(s["onehots"], 1)
            for k in range(TOP):
                rhs = OH[:, k].rearrange("p i e -> p (i e)")
                pe.matmul(pW[:, k, 0:NB * E], sh.tri[:, :], rhs, start=True, stop=True)
                m = pe.matmul(pC[:, k, 0:NB * E], sh.ones[:, :], rhs, start=True, stop=True)
            m.then_inc(s["mm"], 1)

        @block.vector
        def _(v):
            then = Chain(v, s["op"])
            all_e = [P, NB, E]

            def by_e(ap):
                return ap.unsqueeze(1).broadcast_to(all_e)

            def by_i(ap):
                return ap.unsqueeze(2).broadcast_to(all_e)

            then(v.tensor_scalar(REV[:, :], sh.iota[:, 0:E], -1.0, float(E), ALU.mult, ALU.add))
            cur = logits
            for k in range(TOP):
                then(v.tensor_reduce(M[:, k, :], cur[:, :, :], AX.X, ALU.max))
                then(v.tensor_tensor(Q, cur[:, :, :], by_i(M[:, k, :]), ALU.is_equal))
                then(v.tensor_tensor(Q, Q, by_e(REV[:, :]), ALU.mult))
                then(v.tensor_reduce(K[:, :], Q, AX.X, ALU.max))
                then(v.tensor_tensor(OH[:, k], by_e(REV[:, :]), by_i(K[:, :]), ALU.is_equal))
                if k == 0:
                    then(v.scalar_tensor_tensor(L2.rearrange("p i e -> p (i e)"),
                                                OH[:, 0].rearrange("p i e -> p (i e)"), -BIG,
                                                logits[:, :, :].rearrange("p i e -> p (i e)"), ALU.mult, ALU.add))
                    cur = L2
            then(v.tensor_tensor(DD[:, :], M[:, 1, :], M[:, 0, :], ALU.subtract), s["diff"])
            last = OH[:, :, NB - 1, :]
            then(v.tensor_scalar(last, last, sh.valid[:, NB - 1:NB], None, ALU.mult), s["onehots"])
            v.wait_ge(s["exp"], 1)
            then(v.tensor_scalar(weights[:, 0, :], DD[:, :], 1.0, None, ALU.add))
            then(v.reciprocal(weights[:, 0, :], weights[:, 0, :]))
            then(v.tensor_tensor(weights[:, 1, :], weights[:, 0, :], DD[:, :], ALU.mult))
            v.wait_ge(s["mm"], 1)
            counts = TOT[:, :, :].rearrange("p (k i) e -> p k (i e)", k=TOP)
            then(v.tensor_copy(counts, pC[:, :, 0:NB * E]))
            for e in range(E):
                then(v.tensor_tensor_scan(INC[:, :, e], sh.ones[:, 0:J], TOT[:, :, e], 0.0, ALU.mult, ALU.add))
            then(v.tensor_scalar(TI[:, :], INC[:, J - 1, :], float(P - 1), None, ALU.add))
            then(v.tensor_scalar(TI[:, :], TI[:, :], 7, None, ALU.logical_shift_right))
            then(v.tensor_copy(TF[:, :], TI[:, :]))
            then(v.tensor_tensor_scan(CUM[:, :], sh.ones[:, 0:E], TF[:, :], 0.0, ALU.mult, ALU.add))
            then(v.tensor_tensor(BASE[:, :], CUM[:, :], TF[:, :], ALU.subtract))
            then(v.tensor_scalar(BASE[:, :], BASE[:, :], float(P), None, ALU.mult))
            then(v.tensor_tensor(INC[:, :, :], INC[:, :, :], TOT[:, :, :], ALU.subtract))
            inc = INC[:, :, :].rearrange("p (k i) e -> p k (i e)", k=TOP)
            then(v.tensor_tensor(inc, inc, pW[:, :, 0:NB * E], ALU.add))
            then(v.tensor_tensor(INC[:, :, :], INC[:, :, :], BASE[:, :].unsqueeze(1).broadcast_to([P, J, E]), ALU.add))
            then(v.tensor_tensor(INC[:, :, :], INC[:, :, :], OH[:, :, :, :].rearrange("p k i e -> p (k i) e"), ALU.mult))
            then(v.tensor_reduce(PF[:, :], INC[:, :, :], AX.X, ALU.add))
            v.wait_ge(s["iota"], 1)
            then(v.tensor_scalar(NV[:, :], sh.valid[:, NB - 1:NB], -1.0, 1.0, ALU.mult, ALU.add))
            pad = PF[:, NB - 1:J:NB]
            then(v.scalar_tensor_tensor(pad, DUMP[:, :], NV[:, 0:1], pad, ALU.mult, ALU.add))
            then(v.tensor_copy(pos[:, :, :].rearrange("p k i -> p (k i)"), PF[:, :]))
            then(v.tensor_scalar(pos_get[:, :, :].rearrange("p k i -> p (k i)"), PF[:, :], float(NT * P - 1), None, ALU.min))
            then(v.tensor_scalar(EF[:, :], sh.iota[0:1, 0:NT], CUM[0:1, 0:1], None, ALU.is_ge))
            for e in range(1, E - 1):
                then(v.scalar_tensor_tensor(EF[:, :], sh.iota[0:1, 0:NT], CUM[0:1, e:e + 1], EF[:, :], ALU.is_ge, ALU.add))
            then(v.tensor_copy(expert_of[:, 0:NT], EF[:, :]))


def order_rows(sh, tag, E, stats, stats2, pos, node_of, rows, ew):
    nc = sh.nc
    NT = tiles_of(E)
    COLS = U7 * TOP
    XB = 4
    s = {n: sh.sem(f"{tag}_{n}") for n in ("node", "split", "affine", "lo", "mv", "mm", "done", "xn")}
    s_row = [sh.sem(f"{tag}_row{j}") for j in range(XB)]
    with Scope(nc) as sc:
        NODE = sc.sb(f"{tag}_NODE", [P, NB])
        TI = sc.sb(f"{tag}_TI", [P, TOP, NB], I32)
        LO = sc.sb(f"{tag}_LO", [P, TOP, NB])
        HI = sc.sb(f"{tag}_HI", [P, TOP, NB])
        SCALE = sc.sb(f"{tag}_SCALE", [P, NB])
        SHIFT = sc.sb(f"{tag}_SHIFT", [P, NB])
        OL = sc.sb(f"{tag}_OL", [P, U7, P])
        MV = sc.sb(f"{tag}_MV", [P, U7, NT])
        XR = sc.sb(f"{tag}_XR", [P, XB, D])
        pR = sc.ps(f"{tag}_pR", [P, NT])
        ew.psum(sc)
        block = sc.block()

        @block.gpsimd
        def _(pool):
            pool.iota(NODE[:, :], [[P, NB]], base=0, channel_multiplier=1,
                      allow_small_or_imprecise_dtypes=True).then_inc(s["node"], 1)

        @block.sync
        def _(sp):
            for i in range(NB):
                sp.wait_ge(s["xn"], i + 1)
                sp.dma_start(rows[i * P:(i + 1) * P, :], XR[:, i % XB, :]).then_inc(s_row[i % XB], 16)
            for j in range(XB):
                sp.wait_ge(s_row[j], (NB - j + XB - 1) // XB * 16)

        @block.scalar
        def _(a):
            a.wait_ge(s["affine"], 2 if stats2 is None else 5)
            for i in range(NB):
                if i >= XB:
                    a.wait_ge(s_row[i % XB], i // XB * 16)
                a.activation(XR[:, i % XB, :], sh.X[:, i, :], ACT.Identity, bias=SHIFT[:, i:i + 1],
                             scale=SCALE[:, i:i + 1]).then_inc(s["xn"], 1)

        @block.vector
        def _(v):
            mean, rstd = stats[:, :, 0], stats[:, :, 1]
            then = Chain(v, s["affine"])
            if stats2 is None:
                v.tensor_copy(SCALE[:, :], rstd).then_inc(s["affine"], 1)
                v.scalar_tensor_tensor(SHIFT[:, :], mean, -1.0, rstd, ALU.mult, ALU.mult).then_inc(s["affine"], 1)
            else:
                mean2, rstd2 = stats2[:, :, 0], stats2[:, :, 1]
                then(v.tensor_tensor(SCALE[:, :], rstd, rstd2, ALU.mult))
                then(v.tensor_tensor(SHIFT[:, :], mean, SCALE[:, :], ALU.mult))
                then(v.tensor_tensor(mean2, mean2, rstd2, ALU.mult))
                then(v.tensor_tensor(SHIFT[:, :], SHIFT[:, :], mean2, ALU.add))
                then(v.tensor_scalar(SHIFT[:, :], SHIFT[:, :], -1.0, None, ALU.mult))
            ew.on_vector(v)
            split = Chain(v, s["split"])
            split(v.tensor_scalar(TI[:, :, :], pos[:, :, :], P - 1, None, ALU.bitwise_and))
            split(v.tensor_copy(LO[:, :, :], TI[:, :, :]))
            split(v.tensor_scalar(TI[:, :, :], pos[:, :, :], 7, None, ALU.logical_shift_right))
            split(v.tensor_copy(HI[:, :, :], TI[:, :, :]))
            v.wait_ge(s["node"], 1)

            @every_round(v)
            def _(it):
                for k in range(TOP):
                    for u in range(U7):
                        n, i = it * COLS + k * U7 + u, it * U7 + u
                        at_least(v, s["mm"], n - U7 + 1)
                        v.tensor_scalar(OL[:, u, :], sh.iota[:, :], LO[:, k, bass.ds(i, 1)], None,
                                        ALU.is_equal).then_inc(s["lo"], 1)
                        v.tensor_scalar(MV[:, u, :], sh.iota[:, 0:NT], HI[:, k, bass.ds(i, 1)], NODE[:, bass.ds(i, 1)],
                                        ALU.is_equal, ALU.mult).then_inc(s["mv"], 1)

            v.wait_ge(s["mm"], NB * TOP)
            v.tensor_copy(node_of[:, 0:NT], pR[:, :]).then_inc(s["done"], 1)
            v.wait_ge(s["done"], 1)

        @block.tensor
        def _(pe):
            ew.on_tensor(pe)

            @every_round(pe)
            def _(it):
                for n in range(COLS):
                    j = it * COLS + n
                    pe.wait_ge(s["lo"], j + 1)
                    pe.wait_ge(s["mv"], j + 1)
                    pe.matmul(pR[:, :], OL[:, n % U7, :], MV[:, n % U7, :], start=(isinstance(j, int) and j == 0),
                              stop=(isinstance(j, int) and j == NB * TOP - 1), skip_group_check=True).then_inc(s["mm"], 1)


class ExpertWeights:

    def __init__(self, sh, layer, tag, E, H, w1, b1, w2, b2, ln_g=None, ln_b=None):
        self.sh, self.tag, self.E, self.H, self.src = sh, tag, E, H, (w1, w2, b2)
        self.HC = H // P
        self.vecs = [(b1, E * self.HC)] + ([(ln_g, E * KC), (ln_b, E * KC)] if ln_g is not None else [])
        self.gain = ln_g is not None
        self.W1 = layer.sb(f"{tag}_W1", [P, E * KC * H])
        self.W2 = layer.sb(f"{tag}_W2", [P, E * self.HC * D])
        self.B2 = layer.sb(f"{tag}_B2", [P, E, D])
        self.VR = layer.sb(f"{tag}_VR", [P, 3, P])
        self.VT = layer.sb(f"{tag}_VT", [P, 3, E * self.HC])
        self.loaded, self.w1_loaded, self.w2_loaded = (sh.sem(f"{tag}_{n}") for n in ("vectors", "w1", "w2"))
        self.turned, self.copied = (sh.sem(f"{tag}_{n}") for n in ("turned", "copied"))

    def fetch(self, sp):
        w1, w2, b2 = self.src
        n1, n2 = KC * self.H, self.HC * D
        for j, (vec, m) in enumerate(self.vecs):
            sp.dma_start(self.VR[0:m, j, :], vec.rearrange("e (c p) -> (e c) p", p=P)).then_inc(self.loaded, 16)
        for e in range(self.E):
            sp.dma_start(self.W1[:, e * n1:(e + 1) * n1].rearrange("p (c n) -> p c n", c=KC),
                         w1[e].rearrange("(c p) n -> p c n", p=P)).then_inc(self.w1_loaded, 16)
        for e in range(self.E):
            sp.dma_start(self.B2[:, e, :], bcast_rows(b2[e])).then_inc(self.w2_loaded, 16)
            sp.dma_start(self.W2[:, e * n2:(e + 1) * n2].rearrange("p (c n) -> p c n", c=self.HC),
                         w2[e].rearrange("(c p) n -> p c n", p=P)).then_inc(self.w2_loaded, 16)

    def psum(self, sc):
        self.pV = sc.ps(f"{self.tag}_pV", [P, 3, P])

    def on_tensor(self, pe):
        pe.wait_ge(self.loaded, 16 * len(self.vecs))
        for j, (_, m) in enumerate(self.vecs):
            t = pe.transpose(self.pV[:, j, 0:m], self.VR[0:m, j, :], self.sh.ident[0:m, 0:m])
        t.then_inc(self.turned, 1)

    def on_vector(self, v):
        v.wait_ge(self.turned, 1)
        for j, (_, m) in enumerate(self.vecs):
            v.tensor_copy(self.VT[:, j, 0:m], self.pV[:, j, 0:m]).then_inc(self.copied, 1)


def experts(sh, tag, E, H, ew, expert_of, node_of, rows, ys, y_stored):
    nc = sh.nc
    HC = H // P
    NT = tiles_of(E)
    HB = H // 512
    W1, W2, B2, VT = ew.W1, ew.W2, ew.B2, ew.VT
    s = {n: sh.sem(f"{tag}_{n}") for n in ("staged", "slot_free", "tin", "xt", "h", "hc", "tr", "gelu", "y", "yc")}
    s_x = [sh.lasting_sem(f"{tag}_x{j}") for j in range(2)]
    with Scope(nc) as sc:
        STG = sc.sb(f"{tag}_STG", [P, 2], I32)
        XI = sc.sb(f"{tag}_XI", [P, 2, D])
        XT = sc.sb(f"{tag}_XT", [P, 2, KC, P])
        HS = sc.sb(f"{tag}_HS", [P, H])
        GT = sc.sb(f"{tag}_GT", [P, HC, P])
        Y = sc.sb(f"{tag}_Y", [P, 2, D])
        pH = [sc.ps(f"{tag}_pH{j}", [P, H]) for j in range(2)]
        pT = sc.ps(f"{tag}_pT", [P, HC, P])
        pI = sc.ps(f"{tag}_pI", [P, KC, P])
        pY = sc.ps(f"{tag}_pY", [P, D])
        block = sc.block()
        def over_tiles(eng, step):
            step(0, 0)
            step(0, 1)
            with eng.Fori(1, (NT - 3) // 2) as it:
                step(it, 0)
                step(it, 1)
            step((NT - 3) // 2, 0)
            step((NT - 3) // 2, 1)
            step((NT - 1) // 2, 0)

        def expert(eng, regs, t0):
            eng.reg_load(regs, expert_of[0:1, bass.ds(t0, len(regs))])
            return [eng.snap(r, min_val=0, max_val=E - 1) for r in regs]

        @block.sync
        def _(sp):
            def store(rnd, b):
                t = rnd * 2 + b
                sp.wait_ge(s["yc"], t + 1)
                sp.dma_start(ys[bass.ds(t * P, P), :], Y[:, b, :]).then_inc(y_stored[b], 16)

            over_tiles(sp, store)
            sp.wait_ge(y_stored[0], (NT + 1) // 2 * 16)
            sp.wait_ge(y_stored[1], NT // 2 * 16)

        @block.gpsimd
        def _(pool):
            def fetch(rnd, b):
                t = rnd * 2 + b
                at_least(pool, s_x[b], rnd * 16)
                pool.tensor_copy(STG[:, b:b + 1], node_of[:, bass.ds(t, 1)]).then_inc(s["staged"], 1)
                at_least(pool, s["tin"], t - 1)
                pool.wait_ge(s["staged"], t + 1)
                pool.sem_inc(s["slot_free"], 1)
                pool.indirect_dma_start(XI[:, b, :], None, rows, bass.IndirectOffsetOnAxis(
                    ap=STG[:, b:b + 1].bitcast(U32), axis=0)).then_inc(s_x[b], 16)

            over_tiles(pool, fetch)

        @block.scalar
        def _(a):
            regs = [a.alloc_register(f"{tag}_a{j}") for j in range(2)]

            def copy_in(t, b, e):
                a.wait_ge(s["tin"], t + 1)
                at_least(a, s["h"], t - 1)
                if not ew.gain:
                    a.activation(XT[:, b], pI[:, :, :], ACT.Copy).then_inc(s["xt"], 1)
                    return
                for c in range(KC):
                    col = bass.ds(e * KC + c, 1)
                    m = a.activation(XT[:, b, c, :], pI[:, c, :], ACT.Identity, bias=VT[:, 2, col], scale=VT[:, 1, col])
                m.then_inc(s["xt"], 1)

            a.wait_ge(ew.copied, len(ew.vecs))
            copy_in(0, 0, expert(a, regs[0:1], 0)[0])

            def step(rnd, b):
                t = rnd * 2 + b
                if not isinstance(t, int) or t + 1 < NT:
                    e, e_next = expert(a, regs, t)
                    copy_in(t + 1, 1 - b, e_next)
                else:
                    e, = expert(a, regs[0:1], t)
                a.wait_ge(s["tr"], t + 1)
                at_least(a, s["y"], t)
                for c in range(HC):
                    m = a.activation(GT[:, c, :], pT[:, c, :], ACT.Gelu, bias=VT[:, 0, bass.ds(e * HC + c, 1)])
                m.then_inc(s["gelu"], 1)

            over_tiles(a, step)

        @block.vector
        def _(v):
            v.wait_ge(ew.w2_loaded, 32 * E)
            regs = [v.alloc_register(f"{tag}_v")]

            def bias_out(rnd, b):
                t = rnd * 2 + b
                e, = expert(v, regs, t)
                v.wait_ge(s["y"], t + 1)
                at_least(v, y_stored[b], rnd * 16)
                v.tensor_tensor(Y[:, b, :], pY[:, :], B2[:, bass.ds(e, 1), :].rearrange("p a d -> p (a d)"),
                                ALU.add).then_inc(s["yc"], 1)

            def step(rnd, b):
                t = rnd * 2 + b
                v.wait_ge(s["h"], t + 1)
                at_least(v, s["tr"], t)
                v.tensor_copy(HS[:, :], pH[b][:, :]).then_inc(s["hc"], 1)
                if not (isinstance(t, int) and t == 0):
                    bias_out(rnd - (1 - b), 1 - b)

            over_tiles(v, step)
            bias_out((NT - 1) // 2, 0)

        @block.tensor
        def _(pe):
            pe.wait_ge(ew.w1_loaded, 16 * E)
            pe.wait_ge(ew.w2_loaded, 32 * E)
            regs = [pe.alloc_register(f"{tag}_p{j}") for j in range(2)]

            def turn_in(t, b, rnd):
                pe.wait_ge(s_x[b], rnd * 16)
                at_least(pe, s["xt"], t)
                for c in range(KC):
                    m = pe.transpose(pI[:, c, :], XI[:, b, c * P:(c + 1) * P], sh.ident[:, :])
                m.then_inc(s["tin"], 1)

            turn_in(0, 0, 1)

            def by_w1(t, b, e):
                pe.wait_ge(s["xt"], t + 1)
                at_least(pe, s["hc"], t - 1)
                for n in range(HB):
                    for c in range(KC):
                        m = pe.matmul(pH[b][:, n * 512:(n + 1) * 512], XT[:, b, c, :],
                                      W1[:, bass.ds(e * (KC * H) + (c * H + n * 512), 512)],
                                      start=(c == 0), stop=(c == KC - 1))
                m.then_inc(s["h"], 1)

            def by_w2(t, e):
                pe.wait_ge(s["gelu"], t + 1)
                at_least(pe, s["yc"], t)
                for c in range(HC):
                    m = pe.matmul(pY[:, :], GT[:, c, :], W2[:, bass.ds(e * (HC * D) + c * D, D)],
                                  start=(c == 0), stop=(c == HC - 1))
                m.then_inc(s["y"], 1)

            def step(rnd, b):
                t = rnd * 2 + b
                if isinstance(t, int) and t == 0:
                    e, = expert(pe, regs[1:], 0)
                    by_w1(t, b, e)
                else:
                    e_before, e = expert(pe, regs, t - 1)
                    by_w1(t, b, e)
                    by_w2(t - 1, e_before)
                if not isinstance(t, int) or t + 1 < NT:
                    turn_in(t + 1, 1 - b, rnd + b + 1)
                pe.wait_ge(s["hc"], t + 1)
                at_least(pe, s["gelu"], t)
                for c in range(HC):
                    m = pe.transpose(pT[:, c, :], HS[:, c * P:(c + 1) * P], sh.ident[:, :])
                m.then_inc(s["tr"], 1)

            over_tiles(pe, step)
            e, = expert(pe, regs[1:], NT - 1)
            by_w2(NT - 1, e)


def combine(sh, tag, weights, pos_get, ys, y_stored, y_counts, out=None, then=None):
    nc = sh.nc
    s = {n: sh.sem(f"{tag}_{n}") for n in ("staged", "sum", "set_free")}
    s_got = [sh.lasting_sem(f"{tag}_got{j}") for j in range(2)]
    PAIRS = U7 * TOP
    with Scope(nc) as sc:
        R = sc.sb(f"{tag}_R", [P, 2, TOP, U7, D])
        STG = sc.sb(f"{tag}_STG", [P, 2, TOP, U7], I32)
        if then is not None:
            stats, table, sums, zeroed = then
            t = {n: sh.sem(f"{tag}_{n}") for n in ("sum_seen", "st", "st_seen", "ag", "eps", "root", "rstd", "kept", "xn")}
            s_row = [sh.sem(f"{tag}_row{u}") for u in range(U7)]
            ST = sc.sb(f"{tag}_ST", [P, U7, 6])
            AG = sc.sb(f"{tag}_AG", [P, 2, U7, 2])
            XR = sc.sb(f"{tag}_XR", [P, U7, D])
        block = sc.block()

        if then is not None:
            @block.sync
            def _(sp):
                @every_round(sp)
                def _(it):
                    for u in range(U7):
                        sp.wait_ge(t["xn"], it * U7 + u + 1)
                        sp.dma_start(table[bass.ds((it * U7 + u) * P, P), :], XR[:, u, :]).then_inc(s_row[u], 16)

                for u in range(U7):
                    sp.wait_ge(s_row[u], NB // U7 * 16)

            @block.scalar
            def _(a):
                def root(rnd, par):
                    a.wait_ge(t["eps"], rnd * 2 + par + 1)
                    a.activation(AG[:, par, :, 1], AG[:, par, :, 1], ACT.Sqrt).then_inc(t["root"], 1)

                every_pair(a, root)

        if out is not None:
            s_o = sh.sem("out_stored")

            @block.sync
            def _(sp):
                for it in range(NB // U7):
                    sp.wait_ge(s["sum"], (it + 1) * PAIRS)
                    last = it == NB // U7 - 1
                    b0, b1 = it * U7, (it + 1) * U7 - last
                    sp.dma_start(out[b0 * P:b1 * P, :].rearrange("(i p) d -> p i d", p=P), sh.X[:, b0:b1, :]).then_inc(s_o, 16)
                sp.dma_start(out[(NB - 1) * P:N, :], sh.X[0:LAST, NB - 1, :]).then_inc(s_o, 16)
                sp.wait_ge(s_o, (NB // U7 + 1) * 16)

        @block.gpsimd
        def _(pool):
            for sem, count in zip(y_stored, y_counts):
                pool.wait_ge(sem, count)

            def step(rnd, par):
                it = rnd * 2 + par
                at_least(pool, s_got[par], rnd * PAIRS * 16)
                pool.tensor_copy(STG[:, par], pos_get[:, :, bass.ds(it * U7, U7)]).then_inc(s["staged"], 1)
                at_least(pool, s["sum"], (it - 1) * PAIRS)
                pool.wait_ge(s["staged"], it + 1)
                pool.sem_inc(s["set_free"], 1)
                for u in range(U7):
                    for k in range(TOP):
                        pool.indirect_dma_start(R[:, par, k, u, :], None, ys, bass.IndirectOffsetOnAxis(
                            ap=STG[:, par, k, u:u + 1].bitcast(U32), axis=0)).then_inc(s_got[par], 16)

            every_pair(pool, step)

        @block.vector
        def _(v):
            def normalise(it, par):
                at_least(v, t["ag"], it * U7)
                v.wait_ge(s["sum"], (it + 1) * PAIRS)
                v.sem_inc(t["sum_seen"], 1)
                for u in range(U7):
                    i = it * U7 + u
                    v.bn_stats(ST[:, u, :], sh.X[:, bass.ds(i, 1), :].rearrange("p a d -> p (a d)")).then_inc(t["st"], 1)
                v.wait_ge(t["st"], (it + 1) * U7)
                at_least(v, t["xn"], (it - 1) * U7)
                v.sem_inc(t["st_seen"], 1)
                for u in range(U7):
                    v.bn_aggr(AG[:, par, u, :], ST[:, u, :]).then_inc(t["ag"], 1)
                v.wait_ge(t["ag"], (it + 1) * U7)
                v.tensor_scalar(AG[:, par, :, 1], AG[:, par, :, 1], EPS, None, ALU.add).then_inc(t["eps"], 1)
                v.wait_ge(t["root"], it + 1)
                v.reciprocal(AG[:, par, :, 1], AG[:, par, :, 1]).then_inc(t["rstd"], 1)
                v.wait_ge(t["rstd"], it + 1)
                v.tensor_copy(stats[:, bass.ds(it * U7, U7), :], AG[:, par]).then_inc(t["kept"], 1)
                for u in range(U7):
                    i = it * U7 + u
                    at_least(v, s_row[u], it * 16)
                    v.tensor_scalar(XR[:, u, :], sh.X[:, bass.ds(i, 1), :].rearrange("p a d -> p (a d)"),
                                    AG[:, par, u, 0:1], AG[:, par, u, 1:2], ALU.subtract, ALU.mult).then_inc(t["xn"], 1)

            def step(rnd, par):
                it = rnd * 2 + par
                v.wait_ge(s_got[par], (rnd + 1) * PAIRS * 16)
                for k in range(TOP):
                    for u in range(U7):
                        if k > 0:
                            v.wait_ge(s["sum"], it * PAIRS + u + 1)
                        i = it * U7 + u
                        row = sh.X[:, bass.ds(i, 1), :].rearrange("p a d -> p (a d)")
                        v.scalar_tensor_tensor(row, R[:, par, k, u, :], weights[:, k, bass.ds(i, 1)], row,
                                               ALU.mult, ALU.add).then_inc(s["sum"], 1)
                if then is not None:
                    normalise(it, par)

            if then is not None:
                v.memset(sums[:, :, :], 0.0).then_inc(zeroed, 1)
            every_pair(v, step)
            if then is not None:
                v.wait_ge(t["kept"], NB // U7)
            v.wait_ge(s["sum"], NB * TOP)


def add_bias(sh, tag, L, bias, E, ew):
    s_b, s_a = sh.sem(f"{tag}_loaded"), sh.sem(f"{tag}_added")
    with Scope(sh.nc) as sc:
        B = sc.sb(f"{tag}_B", [P, E])
        block = sc.block()

        @block.sync
        def _(sp):
            sp.dma_start(B[:, :], bcast_rows(bias)).then_inc(s_b, 16)
            ew.fetch(sp)

        @block.vector
        def _(v):
            v.wait_ge(s_b, 16)
            v.tensor_tensor(L[:, :, :], L[:, :, :], B[:, :].unsqueeze(1).broadcast_to([P, NB, E]), ALU.add).then_inc(s_a, 1)


def second_stats(sh, tag, stats2):
    s_v, s_q = sh.sem(f"{tag}_var"), sh.sem(f"{tag}_sqrt")
    with Scope(sh.nc) as sc:
        block = sc.block()

        @block.vector
        def _(v):
            v.tensor_scalar(stats2[:, :, 1], stats2[:, :, 1], EPS, None, ALU.add).then_inc(s_v, 1)
            v.wait_ge(s_q, 1)
            v.reciprocal(stats2[:, :, 1], stats2[:, :, 1]).then_inc(s_v, 1)

        @block.scalar
        def _(a):
            a.wait_ge(s_v, 1)
            a.activation(stats2[:, :, 1], stats2[:, :, 1], ACT.Sqrt).then_inc(s_q, 1)


def build(nc, a, out):
    def dram(name, shape):
        return nc.dram_tensor(name, shape, F32, kind="Internal").ap()

    with ExitStack() as ctx:
        sh = Shared(nc, ctx)
        table0 = dram("table0", (NP, D + HEADS))
        table1 = dram("table1", (NP, D))
        table2 = dram("table2", (NP, 16 + HEADS))
        adst2 = dram("adst2", (NP, HEADS))
        rows = [dram(f"rows{j}", (NP, D)) for j in range(2)]
        ys = dram("ys", (ROWS, D))
        planned = [sh.nc.dram_tensor(f"planned{j}", (P, NS), dt, kind="Internal").ap() for j, dt in enumerate((I32, F32, F32))]
        planned_block = nc.dram_tensor("planned_block", (1, NS), I32, kind="Internal").ap()
        gather_done = [sh.lasting_sem(f"gather_done{j}") for j in range(RINGS)]
        acc_zeroed = [sh.lasting_sem(f"acc_zeroed{j}") for j in range(2)]
        y_stored = [sh.lasting_sem(f"y_stored{j}") for j in range(2)]
        stats = sh.sb("stats", [P, NB, 2])
        graph_rounds = SG // RINGS

        setup(sh, a["x"])
        plan_steps(sh, a["first_dst"], (a["src_rows"], a["dst_rows"], a["weight_rows"]), planned, planned_block, stats)

        with Scope(nc) as layer:
            keep = layer.sb("keep0", [P, NB, 2 * HEADS])
            gmax = layer.sb("gmax0", [P, HEADS])
            acc = layer.sb("acc0", [P, NB, D + HEADS])
            project_nodes(sh, "p0", stats, a["L0_gnn_W"], D + 2 * HEADS, att=(a["L0_gnn_att_src"], a["L0_gnn_att_dst"]),
                          table=table0, table_cols=D + HEADS, keep=keep, keep_from=D, zero=(acc, acc_zeroed[0]))
            table_maximum(sh, "m0", keep, 0, gmax)
            graph_pass(sh, "g0", planned, planned_block, table0, D + HEADS, acc, (acc_zeroed[0], NB), gather_done, 0,
                       keep=keep, gmax=gmax)
            finish_attention(sh, "f0", acc, table0, keep, gmax, a["L0_gnn_bias"])
        sh.end_layer()

        layer_norm_stats(sh, "s1", stats)
        with Scope(nc) as layer:
            weights = layer.sb("weights0", [P, TOP, NB])
            pos = layer.sb("pos0", [P, TOP, NB], I32)
            pos_get = layer.sb("pos_get0", [P, TOP, NB], I32)
            expert_of = layer.sb("expert_of0", [1, NT_MAX], I32)
            node_of = layer.sb("node_of0", [P, NT_MAX], I32)
            ew_scope = Scope(nc)
            ew = ExpertWeights(sh, ew_scope.__enter__(), "ew0", 8, 1024, a["L0_ffn_W1"], a["L0_ffn_b1"],
                               a["L0_ffn_W2"], a["L0_ffn_b2"], ln_g=a["L0_ffn_ln_g"], ln_b=a["L0_ffn_ln_b"])
            with Scope(nc) as inner:
                stats2 = inner.sb("stats2", [P, NB, 2])
                with Scope(nc) as router:
                    logits = router.sb("logits0", [P, NB, 8])
                    project_nodes(sh, "p1", stats, a["L0_ffn_Wr"], 8, keep=logits, stats2=stats2)
                    add_bias(sh, "rb", logits, a["L0_ffn_br"], 8, ew)
                    second_stats(sh, "s2", stats2)
                    route(sh, "r0", 8, logits, weights, pos, pos_get, expert_of)
                order_rows(sh, "t0", 8, stats, stats2, pos, node_of, rows[0], ew)
            experts(sh, "e0", 8, 1024, ew, expert_of, node_of, rows[0], ys, y_stored)
            ew_scope.ctx.close()
            acc = layer.sb("acc1", [P, NB, D])
            combine(sh, "c0", weights, pos_get, ys, y_stored, (16 * ((tiles_of(8) + 1) // 2), 16 * (tiles_of(8) // 2)),
                    then=(stats, table1, acc, acc_zeroed[1]))
            sh.end_layer()

            graph_pass(sh, "g1", planned, planned_block, table1, D, acc, (acc_zeroed[1], 1), gather_done, graph_rounds)
            finish_weighted(sh, "f1", acc, stats, a["L1_gnn_W1t"], a["L1_gnn_W2t"], a["L1_gnn_b1"], a["L1_gnn_b2"])
        sh.end_layer()

        layer_norm_stats(sh, "s4", stats)
        with Scope(nc) as layer:
            weights = layer.sb("weights1", [P, TOP, NB])
            pos = layer.sb("pos1", [P, TOP, NB], I32)
            pos_get = layer.sb("pos_get1", [P, TOP, NB], I32)
            expert_of = layer.sb("expert_of1", [1, NT_MAX], I32)
            node_of = layer.sb("node_of1", [P, NT_MAX], I32)
            ew = ExpertWeights(sh, layer, "ew1", 4, 512, a["L1_ffn_W1"], a["L1_ffn_b1"], a["L1_ffn_W2"], a["L1_ffn_b2"])
            with Scope(nc) as inner:
                keep = inner.sb("keep1", [P, NB, 16 + 2 * HEADS])
                gmax = inner.sb("gmax1", [P, HEADS])
                scores = inner.sb("scores", [P, NB, 4])
                project_nodes(sh, "p3", stats, a["L1_ffn_W_gat"], 16 + 2 * HEADS,
                              att=(a["L1_ffn_att_src"], a["L1_ffn_att_dst"]),
                              table=table2, table_cols=16 + HEADS, keep=keep, keep_from=0)
                table_maximum(sh, "m1", keep, 16, gmax)
                store_adst(sh, "d1", keep, 16 + HEADS, adst2)
                free_edges_pass(sh, "q", ew, a["fsrc_t"], a["fdst_t"], table2, adst2, gmax, keep, gather_done, 2 * graph_rounds,
                                a["L1_ffn_b_gat"], a["L1_ffn_ln_gamma"], a["L1_ffn_ln_beta"], scores)
                route(sh, "r1", 4, scores, weights, pos, pos_get, expert_of)
                order_rows(sh, "t1", 4, stats, None, pos, node_of, rows[1], ew)
            y_stored2 = [sh.lasting_sem(f"y1_stored{j}") for j in range(2)]
            experts(sh, "e1", 4, 512, ew, expert_of, node_of, rows[1], ys, y_stored2)
            combine(sh, "c1", weights, pos_get, ys, y_stored2, (16 * ((tiles_of(4) + 1) // 2), 16 * (tiles_of(4) // 2)), out=out)
        sh.layer.close()


def zero_blocks(pool, zero):
    acc, zeroed = zero
    for i in range(NB):
        pool.memset(acc[:, i, :], 0.0).then_inc(zeroed, 1)


def edge_rows(e, fill):
    import numpy as np
    full = np.full(NTE * P, fill, e.dtype)
    full[:e.shape[0]] = e
    return full.reshape(NTE, P)


def edge_columns(e, tiles, fill):
    import numpy as np
    full = np.full(tiles * P, fill, e.dtype)
    full[:e.shape[0]] = e
    return np.ascontiguousarray(full.reshape(tiles, P).T)


NAMES = ["x", "L0_gnn_W", "L0_gnn_att_src", "L0_gnn_att_dst", "L0_gnn_bias", "L0_ffn_Wr", "L0_ffn_br", "L0_ffn_ln_g",
         "L0_ffn_ln_b", "L0_ffn_W1", "L0_ffn_b1", "L0_ffn_W2", "L0_ffn_b2", "L1_gnn_b1", "L1_gnn_b2", "L1_ffn_W_gat",
         "L1_ffn_att_src", "L1_ffn_att_dst", "L1_ffn_b_gat", "L1_ffn_ln_gamma", "L1_ffn_ln_beta", "L1_ffn_W1",
         "L1_ffn_b1", "L1_ffn_W2", "L1_ffn_b2"]


def kernel(**inputs):
    import concourse.bacc as bacc
    import numpy as np
    from concourse.bass_utils import run_bass_kernel_spmd

    arrays = {n: np.ascontiguousarray(inputs[n]) for n in NAMES}
    arrays["L1_gnn_W1t"] = np.ascontiguousarray(np.asarray(inputs["L1_gnn_W1"]).T)
    arrays["L1_gnn_W2t"] = np.ascontiguousarray(np.asarray(inputs["L1_gnn_W2"]).T)
    arrays["src_rows"] = edge_rows(np.asarray(inputs["src"]), 0)
    arrays["dst_rows"] = edge_rows(np.asarray(inputs["dst"]), N)
    arrays["weight_rows"] = edge_rows(np.asarray(inputs["edge_weight"]), 0)
    arrays["first_dst"] = np.ascontiguousarray(arrays["dst_rows"][:, 0]).reshape(1, NTE)
    fe = np.asarray(inputs["L1_ffn_edge_index"])
    arrays["fsrc_t"] = edge_columns(fe[0], NTF, 0)
    arrays["fdst_t"] = edge_columns(fe[1], NTF, 0)

    nc = bacc.Bacc("TRN2", target_bir_lowering=False, num_devices=1)
    args = {n: nc.dram_tensor(f"in_{n}", v.shape, mybir.dt.from_np(v.dtype), kind="ExternalInput").ap()
            for n, v in arrays.items()}
    out = nc.dram_tensor("out_x", (N, D), F32, kind="ExternalOutput").ap()
    build(nc, args, out)
    r = run_bass_kernel_spmd(nc, [{f"in_{n}": v for n, v in arrays.items()}], core_ids=[0])
    return r.results[0]["out_x"]
```
